# Optimizing a Trainium2 kernel written in Bass

```python
import numpy as np
import jax
import jax.numpy as jnp

def _softmax(x, axis=-1):
    return jax.nn.softmax(x, axis=axis)

def _gelu(x):
    return jax.nn.gelu(x, approximate=True)

def _silu(x):
    return jax.nn.silu(x)

def _sigmoid(x):
    return jax.nn.sigmoid(x)

def _layernorm(x, axis=-1, eps=1e-05):
    m = jnp.mean(x, axis=axis, keepdims=True)
    v = jnp.var(x, axis=axis, keepdims=True)
    return (x - m) / jnp.sqrt(v + eps)

def _scatter_add(tgt, idx, src, axis=0):
    return tgt.at[idx].add(src)

def _segment_sum(src, seg, n):
    return jax.ops.segment_sum(src, seg, n)
kernel_name = 'mk_conv_preact_d4_conv_nhwc16_r4_50ad56'

def setup_inputs(seed: int=0):
    np.random.seed(seed)
    _w = jnp.asarray

    def _rec_inputs():
        import jax
        import jax.numpy as jnp
        _gk = jax.random.key(seed)
        x = -0.0003929 + 0.9999 * jax.random.normal(jax.random.fold_in(_gk, 1), (4, 128, 128, 16), jnp.float32)
        return x
    x = _rec_inputs()

    def _L0_conv_setup():
        import jax, jax.numpy as jnp
        import numpy as np
        ORDER = 8
        IN_DIM = 16
        OUT_DIM = 16
        B, L1, L2 = (4, 128, 128)
        key = jax.random.key(seed)
        k1, k2, k3, k4 = jax.random.split(key, 4)
        scale = 1.0 / ORDER
        x = jax.random.normal(k1, (B, L1, L2, IN_DIM), dtype=jnp.float32)
        h0 = jax.random.normal(k2, (IN_DIM, OUT_DIM, 1, 1), dtype=jnp.float32) * scale
        numerators = jax.random.normal(k3, (4, IN_DIM, OUT_DIM, ORDER, ORDER), dtype=jnp.float32) * scale
        denumerator = jax.random.normal(k4, (IN_DIM, OUT_DIM, ORDER, ORDER), dtype=jnp.float32) * scale
        return {'x': x, 'h0': h0, 'numerators': numerators, 'denumerator': denumerator}
    _L0_conv_all = _L0_conv_setup()
    _L0_conv_in = {k: v for k, v in _L0_conv_all.items() if k in ('h0', 'numerators', 'denumerator')}
    del _L0_conv_all

    def _L1_conv_setup():
        import jax, jax.numpy as jnp
        import numpy as np
        P = 8
        DIM = 16
        HEADS = 4
        LN_EPS = 1e-06

        def _conv_patch(x, W, b):
            y = jax.lax.conv_general_dilated(x, W, window_strides=(P, P), padding='VALID', dimension_numbers=('NHWC', 'HWIO', 'NHWC'))
            return y + b

        def _proj_heads(x, W, b):
            y = _conv_patch(x, W, b)
            B, hh, ww, _ = y.shape
            y = y.reshape(B, hh, ww, DIM, P, P, HEADS)
            y = y.transpose(0, 6, 1, 4, 2, 5, 3)
            return y.reshape(B, HEADS, hh * P, ww * P, DIM)

        def _to_patch(t):
            B, hd, H, W, c = t.shape
            t = t.reshape(B, hd, H // P, P, W // P, P, c)
            return t.transpose(0, 1, 6, 2, 4, 3, 5)

        def _from_patch(t):
            B, hd, c, hh, ww, _, _ = t.shape
            t = t.transpose(0, 1, 3, 5, 4, 6, 2)
            return t.reshape(B, hd, hh * P, ww * P, c)
        key = jax.random.key(seed)
        ks = jax.random.split(key, 6)
        B, H, W, Cin = (4, 64, 64, 16)
        feat = DIM * HEADS * P * P
        s_qkv = 0.02
        inp = {'x': jax.random.normal(ks[0], (B, H, W, Cin), jnp.float32), 'Wq': jax.random.normal(ks[1], (P, P, Cin, feat), jnp.float32) * s_qkv, 'bq': jnp.zeros((feat,), jnp.float32), 'Wk': jax.random.normal(ks[2], (P, P, Cin, feat), jnp.float32) * s_qkv, 'bk': jnp.zeros((feat,), jnp.float32), 'Wv': jax.random.normal(ks[3], (P, P, Cin, feat), jnp.float32) * s_qkv, 'bv': jnp.zeros((feat,), jnp.float32), 'ln_scale': jnp.ones((DIM,), jnp.float32), 'ln_bias': jnp.zeros((DIM,), jnp.float32), 'Wout': jax.random.normal(ks[4], (P, P, HEADS * DIM, DIM * P * P), jnp.float32) * 0.02, 'bout': jnp.zeros((DIM * P * P,), jnp.float32)}
        return inp
    _L1_conv_all = _L1_conv_setup()
    _L1_conv_in = {k: v for k, v in _L1_conv_all.items() if k in ('Wq', 'bq', 'Wk', 'bk', 'Wv', 'bv', 'ln_scale', 'ln_bias', 'Wout', 'bout')}
    del _L1_conv_all

    def _L2_conv_setup():
        import jax, jax.numpy as jnp
        import numpy as np
        key = jax.random.key(seed)
        k1, k2, k3 = jax.random.split(key, 3)
        x = jax.random.normal(k1, (16, 128, 128, 16), dtype=jnp.float32)
        filters = jax.random.normal(k2, (3, 3, 16, 16), dtype=jnp.float32) * 0.05
        bias = jax.random.normal(k3, (16,), dtype=jnp.float32) * 0.05
        return {'x': x, 'filters': filters, 'bias': bias}
    _L2_conv_all = _L2_conv_setup()
    _L2_conv_in = {k: v for k, v in _L2_conv_all.items() if k in ('filters', 'bias')}
    del _L2_conv_all

    def _L3_conv_setup():
        import jax, jax.numpy as jnp
        import numpy as np
        ORDER = 8
        IN_DIM = 16
        OUT_DIM = 16
        B, L1, L2 = (4, 128, 128)
        key = jax.random.key(seed)
        k1, k2, k3, k4 = jax.random.split(key, 4)
        scale = 1.0 / ORDER
        x = jax.random.normal(k1, (B, L1, L2, IN_DIM), dtype=jnp.float32)
        h0 = jax.random.normal(k2, (IN_DIM, OUT_DIM, 1, 1), dtype=jnp.float32) * scale
        numerators = jax.random.normal(k3, (4, IN_DIM, OUT_DIM, ORDER, ORDER), dtype=jnp.float32) * scale
        denumerator = jax.random.normal(k4, (IN_DIM, OUT_DIM, ORDER, ORDER), dtype=jnp.float32) * scale
        return {'x': x, 'h0': h0, 'numerators': numerators, 'denumerator': denumerator}
    _L3_conv_all = _L3_conv_setup()
    _L3_conv_in = {k: v for k, v in _L3_conv_all.items() if k in ('h0', 'numerators', 'denumerator')}
    del _L3_conv_all
    return {'x': x, 'L0_conv_h0': _L0_conv_in['h0'], 'L0_conv_numerators': _L0_conv_in['numerators'], 'L0_conv_denumerator': _L0_conv_in['denumerator'], 'L1_conv_Wq': _L1_conv_in['Wq'], 'L1_conv_bq': _L1_conv_in['bq'], 'L1_conv_Wk': _L1_conv_in['Wk'], 'L1_conv_bk': _L1_conv_in['bk'], 'L1_conv_Wv': _L1_conv_in['Wv'], 'L1_conv_bv': _L1_conv_in['bv'], 'L1_conv_ln_scale': _L1_conv_in['ln_scale'], 'L1_conv_ln_bias': _L1_conv_in['ln_bias'], 'L1_conv_Wout': _L1_conv_in['Wout'], 'L1_conv_bout': _L1_conv_in['bout'], 'L2_conv_filters': _L2_conv_in['filters'], 'L2_conv_bias': _L2_conv_in['bias'], 'L3_conv_h0': _L3_conv_in['h0'], 'L3_conv_numerators': _L3_conv_in['numerators'], 'L3_conv_denumerator': _L3_conv_in['denumerator']}

def reference(x, L0_conv_h0, L0_conv_numerators, L0_conv_denumerator, L1_conv_Wq, L1_conv_bq, L1_conv_Wk, L1_conv_bk, L1_conv_Wv, L1_conv_bv, L1_conv_ln_scale, L1_conv_ln_bias, L1_conv_Wout, L1_conv_bout, L2_conv_filters, L2_conv_bias, L3_conv_h0, L3_conv_numerators, L3_conv_denumerator):
    import jax
    import jax.numpy as jnp

    def _L0_conv_ref(x, h0, numerators, denumerator):
        import jax, jax.numpy as jnp
        import numpy as np
        ORDER = 8
        IN_DIM = 16
        OUT_DIM = 16
        B, L1, L2 = (4, 128, 128)
        l1, l2 = (x.shape[-3], x.shape[-2])
        a = jnp.pad(denumerator, ((0, 0), (0, 0), (1, 0), (1, 0)), constant_values=1.0)
        b = jnp.pad(numerators, ((0, 0), (0, 0), (0, 0), (1, 0), (1, 0)), constant_values=0.0)
        H_truncated = jnp.fft.rfft2(b, s=(l1, l2)) / jnp.fft.rfft2(a, s=(l1, l2))
        h_truncated = jnp.fft.irfft2(H_truncated, s=(l1, l2))
        H = jnp.fft.rfft2(h_truncated, s=(2 * l1, 2 * l2))
        H_cc = H[0]
        H_full = h0 + H_cc
        X = jnp.fft.rfft2(x, s=(2 * l1, 2 * l2), axes=(-3, -2))
        Y = jnp.einsum('...hwi,ijhw->...hwj', X, H_full)
        y = jnp.fft.irfft2(Y, s=(2 * l1, 2 * l2), axes=(-3, -2))
        return y[..., :l1, :l2, :]

    def _L1_conv_ref(x, Wq, bq, Wk, bk, Wv, bv, ln_scale, ln_bias, Wout, bout):
        import jax, jax.numpy as jnp
        import numpy as np
        P = 8
        DIM = 16
        HEADS = 4
        LN_EPS = 1e-06

        def _conv_patch(x, W, b):
            y = jax.lax.conv_general_dilated(x, W, window_strides=(P, P), padding='VALID', dimension_numbers=('NHWC', 'HWIO', 'NHWC'))
            return y + b

        def _proj_heads(x, W, b):
            y = _conv_patch(x, W, b)
            B, hh, ww, _ = y.shape
            y = y.reshape(B, hh, ww, DIM, P, P, HEADS)
            y = y.transpose(0, 6, 1, 4, 2, 5, 3)
            return y.reshape(B, HEADS, hh * P, ww * P, DIM)

        def _to_patch(t):
            B, hd, H, W, c = t.shape
            t = t.reshape(B, hd, H // P, P, W // P, P, c)
            return t.transpose(0, 1, 6, 2, 4, 3, 5)

        def _from_patch(t):
            B, hd, c, hh, ww, _, _ = t.shape
            t = t.transpose(0, 1, 3, 5, 4, 6, 2)
            return t.reshape(B, hd, hh * P, ww * P, c)
        q = _proj_heads(x, Wq, bq)
        k = _proj_heads(x, Wk, bk)
        v = _proj_heads(x, Wv, bv)
        qf = jnp.fft.rfft2(_to_patch(q))
        kf = jnp.fft.rfft2(_to_patch(k))
        out = jnp.fft.irfft2(qf * kf, s=(P, P))
        out = _from_patch(out)
        mu = out.mean(-1, keepdims=True)
        var = ((out - mu) ** 2).mean(-1, keepdims=True)
        out = (out - mu) * jax.lax.rsqrt(var + LN_EPS) * ln_scale + ln_bias
        out = v * out
        B, hd, H, W, c = out.shape
        out = out.transpose(0, 2, 3, 1, 4).reshape(B, H, W, hd * c)
        y = _conv_patch(out, Wout, bout)
        Bo, hh, ww, _ = y.shape
        y = y.reshape(Bo, hh, ww, DIM, P, P).transpose(0, 1, 4, 2, 5, 3)
        return y.reshape(Bo, hh * P, ww * P, DIM)

    def _L2_conv_ref(x, filters, bias):
        import jax, jax.numpy as jnp
        import numpy as np
        out = jax.lax.conv_general_dilated(x, filters, window_strides=(1, 1), padding='SAME', dimension_numbers=('NHWC', 'HWIO', 'NHWC'))
        return out + bias

    def _L3_conv_ref(x, h0, numerators, denumerator):
        import jax, jax.numpy as jnp
        import numpy as np
        ORDER = 8
        IN_DIM = 16
        OUT_DIM = 16
        B, L1, L2 = (4, 128, 128)
        l1, l2 = (x.shape[-3], x.shape[-2])
        a = jnp.pad(denumerator, ((0, 0), (0, 0), (1, 0), (1, 0)), constant_values=1.0)
        b = jnp.pad(numerators, ((0, 0), (0, 0), (0, 0), (1, 0), (1, 0)), constant_values=0.0)
        H_truncated = jnp.fft.rfft2(b, s=(l1, l2)) / jnp.fft.rfft2(a, s=(l1, l2))
        h_truncated = jnp.fft.irfft2(H_truncated, s=(l1, l2))
        H = jnp.fft.rfft2(h_truncated, s=(2 * l1, 2 * l2))
        H_cc = H[0]
        H_full = h0 + H_cc
        X = jnp.fft.rfft2(x, s=(2 * l1, 2 * l2), axes=(-3, -2))
        Y = jnp.einsum('...hwi,ijhw->...hwj', X, H_full)
        y = jnp.fft.irfft2(Y, s=(2 * l1, 2 * l2), axes=(-3, -2))
        return y[..., :l1, :l2, :]

    def _gn(v, G=8, eps=1e-05):
        B_, H_, W_, C_ = v.shape
        g = v.reshape(B_, H_, W_, G, C_ // G)
        m = jnp.mean(g, axis=(1, 2, 4), keepdims=True)
        s = jnp.var(g, axis=(1, 2, 4), keepdims=True)
        return ((g - m) / jnp.sqrt(s + eps)).reshape(v.shape)

    def _ln_c(v, eps=1e-06):
        m = jnp.mean(v, axis=-1, keepdims=True)
        s = jnp.var(v, axis=-1, keepdims=True)
        return (v - m) / jnp.sqrt(s + eps)

    def _ln_t(v, eps=1e-05):
        m = jnp.mean(v, axis=-1, keepdims=True)
        s = jnp.var(v, axis=-1, keepdims=True)
        return (v - m) / jnp.sqrt(s + eps)

    def _to_tokens(v):
        B_, H_, W_, C_ = v.shape
        return v.reshape(B_, H_ * W_, C_)

    def _from_tokens(t, like):
        return t.reshape(like.shape)
    x = x + _L0_conv_ref(_gn(x), L0_conv_h0, L0_conv_numerators, L0_conv_denumerator)
    x = x + _L1_conv_ref(_gn(x), L1_conv_Wq, L1_conv_bq, L1_conv_Wk, L1_conv_bk, L1_conv_Wv, L1_conv_bv, L1_conv_ln_scale, L1_conv_ln_bias, L1_conv_Wout, L1_conv_bout)
    x = x + _L2_conv_ref(_gn(x), L2_conv_filters, L2_conv_bias)
    x = x + _L3_conv_ref(_gn(x), L3_conv_h0, L3_conv_numerators, L3_conv_denumerator)
    return x

_drawn_inputs = setup_inputs


def setup_inputs(seed=0):
    import zlib

    import numpy as np

    out = dict(_drawn_inputs(seed))
    spreads = {'L1_conv_bq': (0.0, 0.309),
     'L1_conv_bk': (0.0, 0.295),
     'L1_conv_bv': (0.0, 0.305),
     'L1_conv_ln_scale': (1.0, 0.6),
     'L1_conv_ln_bias': (0.0, 0.405),
     'L1_conv_bout': (0.0, 0.354)}
    factors = {'L2_conv_bias': 8.0}
    for name, (base, spread) in spreads.items():
        noise = np.random.default_rng([zlib.crc32(name.encode()), seed]).standard_normal(out[name].shape)
        drawn = base * np.exp(spread * noise) if base else spread * noise
        out[name] = jnp.asarray(drawn.astype(out[name].dtype))
    for name, factor in factors.items():
        out[name] = (out[name] * factor).astype(out[name].dtype)
    return out
```

```python
from contextlib import ExitStack
import numpy as np
import concourse.bass as bass
from concourse import mybir
ALU = mybir.AluOpType
ACT = mybir.ActivationFunctionType
AX = mybir.AxisListType
F32 = mybir.dt.float32

def allocators(nc, ctx, prefix):
    sems = []

    def clear():
        nc.clear_and_free_semaphores(sems)
        nc.all_engine_barrier()

    ctx.callback(clear)

    def sb(name, shape, dt=F32):
        return ctx.enter_context(nc.sbuf_tensor(prefix + name, shape, dt))

    def ps(name, shape):
        return ctx.enter_context(nc.psum_tensor(prefix + name, shape, F32))

    def sem(name):
        sems.append(nc.alloc_semaphore(name=prefix + name))
        return sems[-1]

    return sb, ps, sem

L, FW, B, C = 128, 64, 4, 16


def dft_tables():
    f64 = np.float64
    n = np.arange(L, dtype=f64)
    tau = 2 * np.pi
    p = np.repeat(np.arange(1, 9), 8).astype(f64)
    q = np.tile(np.arange(1, 9), 8).astype(f64)
    edge = [(a, b) for a in range(9) for b in range(9) if a == 0 or b == 0]
    taps = np.zeros((65, FW + 1, 2, L))
    for fw in range(FW + 1):
        ang = tau * (np.outer(p, n) + (q * fw)[:, None]) / L
        taps[:64, fw, 0], taps[:64, fw, 1] = np.cos(ang), -np.sin(ang)
        e = sum(np.exp(-1j * tau * (n * a + fw * b) / L) for a, b in edge)
        taps[64, fw, 0], taps[64, fw, 1] = e.real, e.imag
    ang = tau * np.outer(n, n) / L
    inv_h = np.stack([np.cos(ang), np.sin(ang), -np.sin(ang)], 1) / L
    s = np.arange(FW, dtype=f64)
    fwd = np.zeros((2, L, 2, FW))
    fwd[0, :, 0], fwd[0, :, 1] = np.cos(tau * np.outer(n, s) / L), -np.sin(tau * np.outer(n, s) / L)
    fwd[0, :, 1, 0] = (-1.0) ** n
    odd = tau * np.outer(n, 2 * s + 1) / (2 * L)
    fwd[1, :, 0], fwd[1, :, 1] = np.cos(odd), -np.sin(odd)
    back = np.zeros((2, FW, L))
    back[0], back[1] = 2 * np.cos(tau * np.outer(s, n) / L) / L, -2 * np.sin(tau * np.outer(s, n) / L) / L
    back[0, 0], back[1, 0] = 1.0 / L, (-1.0) ** n / L
    back = back.reshape(L, L)
    respread = np.zeros((L, 2, FW, 2))
    for c in range(2):
        for k in range(FW):
            respread[c * FW + k, 0, k, c] = 1.0
    respread[:, 1] = (back @ fwd[1].reshape(L, 2 * FW)).reshape(L, 2, FW).transpose(0, 2, 1)
    inv = np.zeros((2, FW, 2, 2, L))
    for par in range(2):
        a = tau * np.outer(2 * s + par, n) / (2 * L)
        co, si = np.cos(a) / L, np.sin(a) / L
        inv[0, :, par, 0], inv[1, :, par, 0] = co, -si
        inv[0, :, par, 1], inv[1, :, par, 1] = -si, -co
    inv[:, 0, 0] = 0.0
    inv[0, 0, 0, 0] = 0.5 / L
    inv[1, 0, 0, 1] = 0.5 * (-1.0) ** n / L
    return {
        "taps": taps.reshape(65, -1), "inv_h": inv_h.reshape(L, -1),
        "fwd_w": fwd.reshape(2, L, L).transpose(1, 0, 2).reshape(L, -1),
        "respread": respread.reshape(L, -1), "inv_w": inv.reshape(L, -1),
    }


def patch_tables():
    f64 = np.float64
    u, v = np.repeat(np.arange(8), 8), np.tile(np.arange(8), 8)
    real = [(a, b) for a in (0, 4) for b in (0, 4)]
    pairs = [(a, b) for a in range(8) for b in range(8) if (a, b) not in real and (a, b) < ((-a) % 8, (-b) % 8)]
    ang = lambda fs: 2 * np.pi * np.array([[(a * x + b * y) / 8 for a, b in fs] for x, y in zip(u, v)], dtype=f64)
    cx, rl = ang(pairs), ang(real)
    re, im = np.cos(cx), -np.sin(cx)
    q = np.concatenate([re, im, re, im, np.cos(rl), np.zeros((64, 4))], 1)
    k = np.concatenate([re, im, im, re, np.cos(rl), np.zeros((64, 4))], 1)
    co, si = 2 * np.cos(cx).T / 64, -2 * np.sin(cx).T / 64
    back = np.concatenate([co, -co, si, si, np.cos(rl).T / 64, np.zeros((4, 64))])
    two = np.zeros((2, 2, 128, 2, 128))
    for n, m in enumerate((q, k)):
        for d in range(2):
            two[n, 0, 64 * d:64 * d + 64, d] = m
    pix, grp = np.arange(128) % 64, np.arange(128) % 16 // 2
    return {
        "patch_q": two[0, 0].reshape(128, 256), "patch_k": two[1, 0].reshape(128, 256), "patch_back": back,
        "over_dims": (pix[:, None] == pix) / 16.0, "average_groups": (grp[:, None] == grp) / 256.0,
        "average": np.full((128, 128), 1 / 256), "ident": np.eye(128),
        "mask": (np.arange(128) <= 64).astype(f64)[:, None],
    }


def build_filters(nc, io, scratch, const):
    QUARTERS, PAIRS = 8, 64
    BLOCKS = [list(range(4 * n, 4 * n + 4)) for n in range(15)] + [[60, 61], [62, 63], [FW]]
    NB = len(BLOCKS)
    KB = L // 8
    with ExitStack() as ctx:
        sb, ps, sem = allocators(nc, ctx, "f_")
        raw = sb("raw", [128, 8, 64])
        ident = sb("ident", [128, 128])
        taps_ab = sb("taps_ab", [65, QUARTERS, 2, PAIRS])
        table = sb("table", [65, 2, 4, 2, L])
        inv_h = sb("inv_h", [L, 3, L])
        respread = sb("respread", [L, 2, 128])
        h0s = sb("h0s", [128, 2, C, C])
        h0m = sb("h0m", [128, 2, C, C])
        mask = sb("mask", [128, 1])
        den = sb("den", [128, 2, 4, 2, PAIRS])
        sq = sb("sq", [128, 2, 4, 2, PAIRS])
        mag = sb("mag", [128, 2, 4, PAIRS])
        rec = sb("rec", [128, 2, 4, PAIRS])
        straight = sb("straight", [128, 2, 4, 2, PAIRS])
        crossed = sb("crossed", [128, 2, 4, 2, PAIRS])
        ratio = sb("ratio", [128, 2, 4, 2, PAIRS])
        nyq = sb("nyq", [128, 2, PAIRS])
        spec = sb("spec", [L, 2, PAIRS, FW])
        lags = sb("lags", [128, 4, L, C])
        stage = sb("stage", [128, 2, FW, 4, 2, KB])
        ab = [ps(f"ab{k}", [128, 4, 2, 2, PAIRS]) for k in range(2)]
        mid = [ps(f"mid{k}", [128, 4, 128]) for k in range(2)]
        far = [ps(f"far{k}", [128, 4, 128]) for k in range(2)]

        raw_in, consts_in, h0_in = sem("raw_in"), sem("consts_in"), sem("h0_in")
        table_in = [sem(f"table_in{k}") for k in range(2)]
        turned, turned_out, edges_set, h0_ready = sem("turned"), sem("turned_out"), sem("edges_set"), sem("h0_ready")
        ab_ready, den_ready, mag_ready, rec_ready = sem("ab_ready"), sem("den_ready"), sem("mag_ready"), sem("rec_ready")
        prod_ready, num_ready, ratio_ready, quot_ready = sem("prod_ready"), sem("num_ready"), sem("ratio_ready"), sem("quot_ready")
        spec_ready, mid_ready, mid_out, lags_ready = sem("spec_ready"), sem("mid_ready"), sem("mid_out"), sem("lags_ready")
        far_ready, far_out = sem("far_ready"), [sem(f"far_out{k}") for k in range(2)]
        stored = [sem(f"stored{k}") for k in range(2)]

        block = ctx.enter_context(nc.Block())

        def table_load(eng, blk):
            fws = BLOCKS[blk]
            eng.dma_start(table[:, blk % 2, 0:len(fws)],
                          const["taps"][:, fws[0] * 2 * L:(fws[-1] + 1) * 2 * L]).then_inc(table_in[blk % 2], 16)

        @block.sync
        def _(sp):
            for layer in range(2):
                for ab_ in range(2):
                    src = io[("den", "num")[ab_] + str(layer)].rearrange("(t a) b p q -> t (a b) (p q)", t=2)
                    for t in range(2):
                        sp.dma_start(raw[:, layer * 4 + ab_ * 2 + t, :], src[t]).then_inc(raw_in, 16)
            sp.dma_start(ident[:], const["ident"]).then_inc(raw_in, 16)
            sp.dma_start(inv_h[:], const["inv_h"]).then_inc(consts_in, 16)
            sp.dma_start(respread[:], const["respread"]).then_inc(consts_in, 16)
            sp.dma_start(mask[:], const["mask"]).then_inc(h0_in, 16)
            for layer in range(2):
                h0 = io[f"h0{layer}"].rearrange("i j a b -> (a b) (i j)")
                sp.dma_start(h0s[:, layer], h0.broadcast_to([128, 256])).then_inc(h0_in, 16)
            table_load(sp, 0)
            table_load(sp, 1)
            for blk in range(2, NB):
                sp.wait_ge(ab_ready, blk - 1)
                table_load(sp, blk)
            with sp.Fori(1, QUARTERS) as q:
                for blk in range(NB):
                    sp.wait_ge(ab_ready, q * NB + blk - 1)
                    table_load(sp, blk)

        def transform_taps(q, blk):
            n = q * NB + blk
            nc.tensor.wait_ge(table_in[blk % 2], 16 * (q * (NB // 2) + blk // 2 + 1))
            if not (isinstance(q, int) and n < 2):
                nc.tensor.wait_ge(prod_ready, n - 1)
            for k in range(len(BLOCKS[blk])):
                for part in range(2):
                    mm = nc.tensor.matmul(ab[blk % 2][:, k, part], table[:, blk % 2, k, part],
                                          taps_ab[:, q], start=True, stop=True)
            mm.then_inc(ab_ready, 1)

        def to_lags(q, g):
            n = q * 16 + g
            if not (isinstance(q, int) and n < 2):
                nc.tensor.wait_ge(mid_out, n - 1)
            for k in range(4):
                pair = 4 * g + k
                re, im = spec[:, 0, pair, :], spec[:, 1, pair, :]
                lo, hi = mid[g % 2][0:FW, k], mid[g % 2][FW:128, k]
                nc.tensor.matmul(lo, re, inv_h[:, 0], start=True, stop=False)
                nc.tensor.matmul(hi, im, inv_h[:, 0], start=True, stop=False)
                nc.tensor.matmul(lo, im, inv_h[:, 2], start=False, stop=True)
                mm = nc.tensor.matmul(hi, re, inv_h[:, 1], start=False, stop=True)
            mm.then_inc(mid_ready, 1)

        def to_slots(q, u):
            par, kb = u // KB, u % KB
            nc.tensor.wait_ge(far_out[u % 2], q * KB + u // 2 + 1)
            for j in range(4):
                mm = nc.tensor.matmul(far[u % 2][:, j], lags[:, j, 8 * kb:8 * kb + 8, :], respread[:, par], start=True, stop=True)
            mm.then_inc(far_ready, 1)

        @block.tensor
        def _(pe):
            pe.wait_ge(raw_in, 16 * 9)
            for t in range(8):
                if t >= 2:
                    pe.wait_ge(turned_out, t - 1)
                nc.tensor.transpose(mid[t % 2][0:64, 0, :], raw[:, t, :], ident[:]).then_inc(turned, 1)
            pe.wait_ge(turned_out, 8)
            pe.wait_ge(edges_set, 1)

            def lags_of(q):
                pe.wait_ge(spec_ready, q + 1)
                if not isinstance(q, int):
                    pe.wait_ge(far_ready, q * 2 * KB)
                for g in range(16):
                    to_lags(q, g)

            for blk in range(NB):
                transform_taps(0, blk)
            pe.wait_ge(consts_in, 32)
            lags_of(0)
            with pe.Fori(1, QUARTERS) as q:
                for blk in range(NB):
                    transform_taps(q, blk)
                    if blk == 0:
                        pe.wait_ge(lags_ready, q)
                    if blk < 16:
                        to_slots(q - 1, 2 * blk)
                        to_slots(q - 1, 2 * blk + 1)
                lags_of(q)
            pe.wait_ge(lags_ready, QUARTERS)
            for u in range(2 * KB):
                to_slots(QUARTERS - 1, u)

        @block.scalar
        def _(act):
            def split_den(q, blk):
                n, f, s = q * NB + blk, len(BLOCKS[blk]), blk % 2
                act.wait_ge(ab_ready, n + 1)
                if not (isinstance(q, int) and n < 2):
                    act.wait_ge(prod_ready, n - 1)
                    act.wait_ge(mag_ready, n - 1)
                nc.scalar.activation(den[:, s, 0:f], ab[s][:, 0:f, :, 0], ACT.Copy)
                nc.scalar.activation(sq[:, s, 0:f], ab[s][:, 0:f, :, 0], ACT.Square).then_inc(den_ready, 1)

            def lags_out(q):
                if not (isinstance(q, int) and q == 0):
                    act.wait_ge(far_ready, q * 2 * KB)
                for g in range(16):
                    act.wait_ge(mid_ready, q * 16 + g + 1)
                    nc.scalar.activation(lags[:, g // 4, :, 4 * (g % 4):4 * (g % 4) + 4].rearrange("p k i -> p i k"),
                                         mid[g % 2][:], ACT.Copy).then_inc(mid_out, 1)

            def slots_out(q, u):
                par, kb = u // KB, u % KB
                act.wait_ge(far_ready, q * 2 * KB + u + 1)
                if kb == 0:
                    act.wait_ge(stored[par], 16 * (q + 1))
                nc.scalar.activation(stage[:, par, :, :, :, kb].rearrange("p s j c -> p j s c"),
                                     far[u % 2][:].rearrange("p j (s c) -> p j s c", c=2), ACT.Copy).then_inc(far_out[u % 2], 1)
                if kb == KB - 1:
                    for k in range(2):
                        act.wait_ge(far_out[k], q * KB + u // 2 + 2)
                    act.dma_start(scratch["filters"][q, par * FW:(par + 1) * FW].rearrange("s p n -> p s n"),
                                  stage[:, par].rearrange("p s j c k -> p s (j c k)")).then_inc(stored[par], 16)

            for k in range(2):
                act.sem_inc(far_out[k], 1)
                act.sem_inc(stored[k], 16)
            for blk in range(NB):
                split_den(0, blk)
            lags_out(0)
            with act.Fori(1, QUARTERS) as q:
                for blk in range(NB):
                    split_den(q, blk)
                    if blk < 16:
                        slots_out(q - 1, 2 * blk)
                        slots_out(q - 1, 2 * blk + 1)
                lags_out(q)
            for u in range(2 * KB):
                slots_out(QUARTERS - 1, u)
            for par in range(2):
                act.wait_ge(stored[par], 16 * (QUARTERS + 1))

        @block.vector
        def _(dve):
            for t in range(8):
                dve.wait_ge(turned, t + 1)
                layer, ab_, half = t // 4, t // 2 % 2, t % 2
                for jq in range(4):
                    op = nc.vector.tensor_copy(
                        taps_ab[0:64, 4 * layer + jq, ab_].rearrange("r (j i) -> r i j", i=C)[:, 8 * half:8 * half + 8, :],
                        mid[t % 2][0:64, 0, :].rearrange("r (i q j) -> r q i j", q=4, j=4)[:, jq])
                op.then_inc(turned_out, 1)
            dve.memset(taps_ab[64:65, :, 1, :], 0.0)
            dve.memset(taps_ab[64:65, :, 0, :], 1.0).then_inc(edges_set, 1)
            dve.wait_ge(h0_in, 48)
            nc.vector.tensor_scalar(h0m[:], h0s[:], mask[:, 0:1], None, ALU.mult).then_inc(h0_ready, 1)

            def quotients(q):
                for blk in range(NB):
                    n, f, s = q * NB + blk, len(BLOCKS[blk]), blk % 2
                    dve.wait_ge(den_ready, n + 1)
                    if not (isinstance(q, int) and n < 2):
                        dve.wait_ge(quot_ready, n - 1)
                    nc.vector.tensor_tensor(straight[:, s, 0:f], ab[s][:, 0:f, :, 1], den[:, s, 0:f], ALU.mult)
                    nc.vector.tensor_tensor(crossed[:, s, 0:f, 0], ab[s][:, 0:f, 1, 1], den[:, s, 0:f, 0], ALU.mult)
                    nc.vector.tensor_tensor(crossed[:, s, 0:f, 1], ab[s][:, 0:f, 0, 1], den[:, s, 0:f, 1],
                                            ALU.mult).then_inc(prod_ready, 1)
                    dve.wait_ge(mag_ready, n + 1)
                    nc.vector.reciprocal(rec[:, s, 0:f], mag[:, s, 0:f]).then_inc(rec_ready, 1)

            def add_h0(q, layer, jq):
                dve.wait_ge(mid_out, 16 * (q + 1))
                if isinstance(q, int) and q == 0:
                    dve.wait_ge(h0_ready, 1)
                at0 = lags[:, :, 0, :]
                nc.vector.tensor_tensor(at0, at0, h0m[:, layer, :, bass.ds(4 * jq, 4)].rearrange("p i j -> p j i"),
                                        ALU.add).then_inc(lags_ready, 1)

            quotients(0)
            add_h0(0, 0, 0)
            with dve.Fori(1, 4) as q:
                quotients(q)
                add_h0(q, 0, q)
            with dve.Fori(4, QUARTERS) as q:
                quotients(q)
                add_h0(q, 1, q - 4)

        @block.gpsimd
        def _(pool):
            def combine(q):
                for blk in range(NB):
                    n, f, s = q * NB + blk, len(BLOCKS[blk]), blk % 2
                    pool.wait_ge(den_ready, n + 1)
                    if not (isinstance(q, int) and n < 2):
                        pool.wait_ge(rec_ready, n - 1)
                    nc.gpsimd.tensor_tensor(mag[:, s, 0:f], sq[:, s, 0:f, 0], sq[:, s, 0:f, 1], ALU.add).then_inc(mag_ready, 1)
                    pool.wait_ge(prod_ready, n + 1)
                    if not (isinstance(q, int) and n < 2):
                        pool.wait_ge(quot_ready, n - 1)
                    nc.gpsimd.tensor_tensor(ratio[:, s, 0:f, 0], straight[:, s, 0:f, 0], straight[:, s, 0:f, 1], ALU.add)
                    nc.gpsimd.tensor_tensor(ratio[:, s, 0:f, 1], crossed[:, s, 0:f, 0], crossed[:, s, 0:f, 1],
                                            ALU.subtract).then_inc(num_ready, 1)
                    pool.wait_ge(num_ready, n + 1)
                    pool.wait_ge(rec_ready, n + 1)
                    if blk == 0 and not (isinstance(q, int) and q == 0):
                        pool.wait_ge(mid_ready, 16 * q)
                    for part in range(2):
                        out = nyq[:, part:part + 1] if blk == NB - 1 else \
                            spec[:, part, :, BLOCKS[blk][0]:BLOCKS[blk][-1] + 1].rearrange("p n f -> p f n")
                        op = nc.gpsimd.tensor_tensor(out, ratio[:, s, 0:f, part], rec[:, s, 0:f], ALU.mult)
                    op.then_inc(quot_ready, 1)
                pool.wait_ge(quot_ready, (q + 1) * NB)
                nc.gpsimd.tensor_tensor(spec[:, 0, :, 0], spec[:, 0, :, 0], nyq[:, 1], ALU.subtract)
                nc.gpsimd.tensor_tensor(spec[:, 1, :, 0], spec[:, 1, :, 0], nyq[:, 0], ALU.add).then_inc(spec_ready, 1)

            combine(0)
            with pool.Fori(1, QUARTERS) as q:
                combine(q)


GROUPS = L // 4
ROW = L + 8


def spectrum(nc, image, source, scratch, const, tag):
    with ExitStack() as ctx:
        sb, ps, sem = allocators(nc, ctx, tag)
        ident = sb("ident", [128, 128])
        average = sb("average", [128, 128])
        fwd_w = sb("fwd_w", [L, 2, 128])
        eps = sb("eps", [128, 1])
        stats = sb("stats", [128, 32, 6])
        dev = sb("dev", [128, 32, 2])
        spread = sb("spread", [128, 32, 2])
        mean = sb("mean", [128, 32])
        var = sb("var", [128, 32])
        std = sb("std", [128, 32])
        rstd = sb("rstd", [128, 32])
        cols = sb("cols", [L, C, B, L])
        rows = sb("rows", [128, 4, B, ROW])
        turn = [ps(f"turn{k}", [128, 4, L]) for k in range(4)]
        freq = [ps(f"freq{k}", [128, B, L]) for k in range(2)]
        tot = ps("tot", [128, 64])

        image_in, consts_in, stats_ready, zeroed = sem("image_in"), sem("consts_in"), sem("stats_ready"), sem("zeroed")
        sum_ready, mean_ready, dev_ready, sq_ready = sem("sum_ready"), sem("mean_ready"), sem("dev_ready"), sem("sq_ready")
        spread_ready, var_ready, std_ready, rstd_ready = sem("spread_ready"), sem("var_ready"), sem("std_ready"), sem("rstd_ready")
        turn_ready, cols_ready, freq_ready, rows_ready = sem("turn_ready"), sem("cols_ready"), sem("freq_ready"), sem("rows_ready")
        stored = [sem(f"stored{k}") for k in range(4)]
        block = ctx.enter_context(nc.Block())

        @block.sync
        def _(sp):
            if source is not None:
                for b in range(B):
                    sp.dma_start(image[:, b], source[b]).then_inc(image_in, 16)
            sp.dma_start(ident[:], const["ident"]).then_inc(consts_in, 16)
            sp.dma_start(average[:], const["average"]).then_inc(consts_in, 16)
            sp.dma_start(fwd_w[:], const["fwd_w"]).then_inc(consts_in, 16)
            for u in range(2 * C):
                i, par = u // 2, u % 2
                sp.wait_ge(rows_ready, u + 1)
                for part in range(2):
                    sp.dma_start(scratch["spectrum"][i, par * FW:(par + 1) * FW, part],
                                 rows[part * FW:(part + 1) * FW, u % 4].rearrange("p b h -> p (b h)")).then_inc(stored[u % 4], 16)
            for k in range(4):
                sp.wait_ge(stored[k], 16 * 2 * (2 * C // 4))

        @block.vector
        def _(dve):
            dve.memset(eps[:], 1e-5)
            dve.memset(rows[:, :, :, 0:8], 0.0).then_inc(zeroed, 1)
            if source is not None:
                dve.wait_ge(image_in, 16 * B)
            for n in range(32):
                b, g = n // 8, n % 8
                op = nc.vector.bn_stats(stats[:, n], image[:, b, :, 2 * g:2 * g + 2])
            op.then_inc(stats_ready, 1)
            sample = stats[:].rearrange("p n (s k) -> p n s k", k=3)
            dve.wait_ge(sum_ready, 1)
            nc.vector.tensor_reduce(mean[:], tot[:].rearrange("p (n s) -> p n s", s=2), AX.X, ALU.add).then_inc(mean_ready, 1)
            dve.wait_ge(mean_ready, 1)
            nc.vector.tensor_tensor(dev[:], sample[:, :, :, 1], mean[:].unsqueeze(2).broadcast_to([128, 32, 2]),
                                    ALU.subtract).then_inc(dev_ready, 1)
            dve.wait_ge(dev_ready, 1)
            nc.vector.tensor_tensor(dev[:], dev[:], dev[:], ALU.mult).then_inc(sq_ready, 1)
            dve.wait_ge(sq_ready, 1)
            nc.vector.scalar_tensor_tensor(out=spread[:], in0=sample[:, :, :, 2], scalar=1.0 / 128, in1=dev[:],
                                           op0=ALU.mult, op1=ALU.add).then_inc(spread_ready, 1)
            dve.wait_ge(sum_ready, 2)
            nc.vector.tensor_reduce(var[:], tot[:].rearrange("p (n s) -> p n s", s=2), AX.X, ALU.add).then_inc(var_ready, 1)
            dve.wait_ge(std_ready, 1)
            nc.vector.reciprocal(rstd[:], std[:]).then_inc(rstd_ready, 1)
            dve.wait_ge(rstd_ready, 1)
            for i in range(C):
                dve.wait_ge(turn_ready, i + 1)
                for b in range(B):
                    n = 8 * b + i // 2
                    op = nc.vector.tensor_scalar(cols[:, i, b], turn[i % 4][:, b], mean[:, n:n + 1], rstd[:, n:n + 1],
                                                 ALU.subtract, ALU.mult)
                op.then_inc(cols_ready, 1)

        @block.scalar
        def _(act):
            act.wait_ge(var_ready, 1)
            act.wait_ge(zeroed, 1)
            nc.scalar.activation(std[:], var[:], ACT.Sqrt, bias=eps[:, 0:1]).then_inc(std_ready, 1)
            for u in range(2 * C):
                act.wait_ge(freq_ready, u + 1)
                if u >= 4:
                    act.wait_ge(stored[u % 4], 32 * (u // 4))
                nc.scalar.activation(rows[:, u % 4, :, 8:ROW], freq[u % 2][:], ACT.Copy).then_inc(rows_ready, 1)

        @block.tensor
        def _(pe):
            pe.wait_ge(consts_in, 48)
            pe.wait_ge(stats_ready, 1)
            nc.tensor.matmul(tot[:].rearrange("p (n s) -> p n s", s=2), average[:],
                             stats[:].rearrange("p n (s k) -> p n s k", k=3)[:, :, :, 1], start=True, stop=True).then_inc(sum_ready, 1)
            pe.wait_ge(mean_ready, 1)
            pe.wait_ge(spread_ready, 1)
            nc.tensor.matmul(tot[:], average[:], spread[:].rearrange("p n s -> p (n s)"), start=True, stop=True).then_inc(sum_ready, 1)

            def turn_channel(i):
                if i >= 4:
                    pe.wait_ge(cols_ready, i - 3)
                for b in range(B):
                    mm = nc.tensor.matmul(turn[i % 4][:, b], image[:, b, :, i], ident[:], start=True, stop=True)
                mm.then_inc(turn_ready, 1)

            for i in range(3):
                turn_channel(i)
            for i in range(C):
                pe.wait_ge(cols_ready, i + 1)
                for par in range(2):
                    u = 2 * i + par
                    if u >= 2:
                        pe.wait_ge(rows_ready, u - 1)
                    nc.tensor.matmul(freq[par][:], fwd_w[:, par], cols[:, i], start=True, stop=True).then_inc(freq_ready, 1)
                if i + 3 < C:
                    turn_channel(i + 3)


def convolve(nc, layer, scratch, tag):
    KB, RING = L // 8, 2
    with ExitStack() as ctx:
        sb, ps, sem = allocators(nc, ctx, tag)
        filt = sb("filt", [128, RING, 4, 4, 128])
        shifted = sb("shifted", [128, RING, 4, 2, B, L])
        out = sb("out", [128, RING, 2, B * L])
        acc = [[ps(f"acc{k}{cx}", [128, B, L]) for cx in range(2)] for k in range(RING)]
        filt_in = [sem(f"filt_in{k}") for k in range(RING)]
        rows_in = [sem(f"rows_in{k}") for k in range(RING)]
        group_done, acc_out = sem("group_done"), [[sem(f"acc_out{k}{cx}") for cx in range(2)] for k in range(RING)]
        stored = [sem(f"stored{k}") for k in range(RING)]
        block = ctx.enter_context(nc.Block())

        def load(eng, g, k):
            for s in range(4):
                eng.dma_start(filt[:, k, s], scratch["filters"][4 * layer:4 * layer + 4, 4 * g + s].rearrange("q p n -> p q n")
                              ).then_inc(filt_in[k], 16)
            for lag in range(8):
                eng.dma_start(shifted[C * lag:C * (lag + 1), k].rearrange("p s c b h -> p (s c b) h"),
                              scratch["spectrum"][:, bass.ds(4 * g, 4)].rearrange("i s c (b h) -> i (s c b) h", b=B)
                              [:, :, 8 - lag:8 - lag + L]).then_inc(rows_in[k], 16)

        @block.sync
        def _(sp):
            for k in range(RING):
                load(sp, k, k)
            with sp.Fori(1, GROUPS // RING) as n:
                for k in range(RING):
                    sp.wait_ge(group_done, RING * (n - 1) + k + 1)
                    load(sp, RING * n + k, k)

        @block.tensor
        def _(pe):
            with pe.Fori(0, GROUPS // RING) as n:
                for k in range(RING):
                    pe.wait_ge(filt_in[k], 16 * 4 * (n + 1))
                    pe.wait_ge(rows_in[k], 16 * 8 * (n + 1))
                    for cx in range(2):
                        pe.wait_ge(acc_out[k][cx], n + 1)
                        for kb in range(KB):
                            for s in range(4):
                                mm = nc.tensor.matmul(
                                    acc[k][cx][32 * s:32 * s + 32, :, 8 * kb:L],
                                    filt[:, k, s].rearrange("p q (m k) -> p (q m) k", k=KB)[:, :, kb],
                                    shifted[:, k, s, cx, :, 0:L - 8 * kb], start=kb == 0, stop=kb == KB - 1)
                    mm.then_inc(group_done, 1)

        def evacuate(eng, copy, cx, store):
            for k in range(RING):
                eng.sem_inc(acc_out[k][cx], 1)
            with eng.Fori(0, GROUPS // RING) as n:
                for k in range(RING):
                    eng.wait_ge(group_done, RING * n + k + 1)
                    eng.wait_ge(stored[k], 16 * (n + 1))
                    copy(out[:, k, cx], acc[k][cx][:].rearrange("p b h -> p (b h)")).then_inc(acc_out[k][cx], 1)
                    store(n, k)

        @block.vector
        def _(dve):
            evacuate(dve, nc.vector.tensor_copy, 0, lambda n, k: None)

        @block.scalar
        def _(act):
            def store(n, k):
                for cx in range(2):
                    act.wait_ge(acc_out[k][cx], n + 2)
                act.dma_start(scratch["products"][bass.ds(4 * (RING * n + k), 4)].rearrange("s j c n -> (s j c) n"),
                              out[:, k].rearrange("p x n -> p (x n)")).then_inc(stored[k], 16)

            for k in range(RING):
                act.sem_inc(stored[k], 16)
            evacuate(act, nc.scalar.copy, 1, store)
            for k in range(RING):
                act.wait_ge(stored[k], 16 * (GROUPS // RING + 1))


def back_to_image(nc, image, out_dram, scratch, const, tag):
    with ExitStack() as ctx:
        sb, ps, sem = allocators(nc, ctx, tag)
        inv_w = sb("inv_w", [128, 2, 2, L])
        prod = sb("prod", [128, 2, 2, 4, 2, B, L])
        img = [ps(f"img{k}", [128, B, L]) for k in range(4)]
        consts_in, done, added, out_stored = sem("consts_in"), sem("done"), sem("added"), sem("out_stored")
        prod_in = [sem(f"prod_in{k}") for k in range(2)]
        block = ctx.enter_context(nc.Block())

        @block.sync
        def _(sp):
            sp.dma_start(inv_w[:], const["inv_w"]).then_inc(consts_in, 16)
            for ch in range(4):
                if ch >= 2:
                    sp.wait_ge(done, 4 * (ch - 1))
                for par in range(2):
                    for c in range(2):
                        sp.dma_start(prod[FW * c:FW * (c + 1), ch % 2, par].rearrange("p j x b h -> p j (x b h)"),
                                     scratch["products"][FW * par:FW * (par + 1), 4 * ch:4 * ch + 4, c]).then_inc(prod_in[ch % 2], 16)
            if out_dram is not None:
                sp.wait_ge(added, C)
                for b in range(B):
                    sp.dma_start(out_dram[b], image[:, b]).then_inc(out_stored, 16)
                sp.wait_ge(out_stored, 16 * B)

        @block.tensor
        def _(pe):
            pe.wait_ge(consts_in, 16)
            for j in range(C):
                if j % 4 == 0:
                    pe.wait_ge(prod_in[j // 4 % 2], 16 * 4 * (j // 8 + 1))
                if j >= 4:
                    pe.wait_ge(added, j - 3)
                for b in range(B):
                    for t in range(4):
                        par, cx = t // 2, t % 2
                        mm = nc.tensor.matmul(img[j % 4][:, b], prod[:, j // 4 % 2, par, j % 4, cx, b], inv_w[:, par, cx],
                                              start=t == 0, stop=t == 3)
                mm.then_inc(done, 1)

        @block.vector
        def _(dve):
            for j in range(C):
                dve.wait_ge(done, j + 1)
                nc.vector.tensor_tensor(image[:, :, :, j], image[:, :, :, j], img[j % 4][:], ALU.add).then_inc(added, 1)


PATCHES = 1024
N = 512
R32 = mybir.dt.float32r


def split_high(eng, out, src):
    return eng.activation(out, src, ACT.Copy)


def split_low(eng, out, src, high):
    return eng.tensor_tensor(out, src, high.bitcast(F32), ALU.subtract)


def split_product(pe, out, w, x, first, last):
    pe.matmul(out, w[0], x[0], start=first, stop=False)
    pe.matmul(out, w[0], x[1], start=False, stop=False)
    return pe.matmul(out, w[1], x[0], start=False, stop=last)


def moments_tensors(sb, ps):
    return (sb("average", [128, 128]), sb("eps", [128, 1]), sb("stats", [128, B, 8, 6]), sb("dev", [128, B, 16]),
            sb("spread", [128, B, 16]), sb("var", [128, B]), sb("std", [128, B]), ps("tot", [128, B, 16]))


def to_patches(nc, image, mean, rstd, scratch, const, tag):
    with ExitStack() as ctx:
        sb, ps, sem = allocators(nc, ctx, tag)
        ident = sb("ident", [128, 128])
        xt = sb("xt", [128, 8, PATCHES])
        average, eps, stats, dev, spread, var, std, tot = moments_tensors(sb, ps)
        turn = [ps(f"turn{k}", [128, 4, L]) for k in range(4)]
        ident_in, average_in, turned, moved, stored = (sem(n) for n in ("ident_in", "average_in", "turned", "moved", "stored"))
        stats_ready, step, sum_ready, std_ready = sem("stats_ready"), sem("step"), sem("sum_ready"), sem("std_ready")
        sample = stats[:].rearrange("p b r (s k) -> p b (r s) k", k=3)
        block = ctx.enter_context(nc.Block())

        @block.sync
        def _(sp):
            sp.dma_start(ident[:], const["ident"]).then_inc(ident_in, 16)
            sp.dma_start(average[:], const["average_groups"]).then_inc(average_in, 16)
            for half in range(2):
                sp.wait_ge(moved, 8 * half + 8)
                sp.dma_start(scratch["patches"][half], xt[:, :, N * half:N * half + N]).then_inc(stored, 16)
            sp.wait_ge(stored, 32)

        @block.tensor
        def _(pe):
            pe.wait_ge(ident_in, 16)
            for t in range(16):
                if t >= 4:
                    pe.wait_ge(moved, t - 3)
                for k in range(4):
                    b, ww = (4 * t + k) // 16, (4 * t + k) % 16
                    mm = nc.tensor.matmul(turn[t % 4][:, k], image[:, b, 8 * ww:8 * ww + 8, :].rearrange("h s c -> h (s c)"),
                                          ident[:], start=True, stop=True)
                mm.then_inc(turned, 1)
            pe.wait_ge(average_in, 16)
            pe.wait_ge(stats_ready, 8 * B)
            nc.tensor.matmul(tot[:], average[:], sample[:, :, :, 1], start=True, stop=True).then_inc(sum_ready, 1)
            pe.wait_ge(step, 5)
            nc.tensor.matmul(tot[:], average[:], spread[:], start=True, stop=True).then_inc(sum_ready, 1)

        @block.scalar
        def _(act):
            for t in range(16):
                act.wait_ge(turned, t + 1)
                nc.scalar.activation(xt[:, :, 64 * t:64 * t + 64], turn[t % 4][:].rearrange("p k (h r) -> p r (k h)", r=8),
                                     ACT.Copy).then_inc(moved, 1)
            act.wait_ge(step, 6)
            nc.scalar.activation(std[:], var[:], ACT.Sqrt, bias=eps[:, 0:1]).then_inc(std_ready, 1)

        @block.vector
        def _(dve):
            dve.memset(eps[:], 1e-5).then_inc(step, 1)
            for b in range(B):
                dve.wait_ge(moved, 4 * b + 4)
                for r in range(8):
                    nc.vector.bn_stats(stats[:, b, r], xt[:, r, 256 * b:256 * b + 256]).then_inc(stats_ready, 1)
            dve.wait_ge(sum_ready, 1)
            nc.vector.tensor_reduce(mean[:], tot[:], AX.X, ALU.add).then_inc(step, 1)
            dve.wait_ge(step, 2)
            nc.vector.tensor_tensor(dev[:], sample[:, :, :, 1], mean[:].unsqueeze(2).broadcast_to([128, B, 16]),
                                    ALU.subtract).then_inc(step, 1)
            dve.wait_ge(step, 3)
            nc.vector.tensor_tensor(dev[:], dev[:], dev[:], ALU.mult).then_inc(step, 1)
            dve.wait_ge(step, 4)
            nc.vector.scalar_tensor_tensor(out=spread[:], in0=sample[:, :, :, 2], scalar=1.0 / 128, in1=dev[:],
                                           op0=ALU.mult, op1=ALU.add).then_inc(step, 1)
            dve.wait_ge(sum_ready, 2)
            nc.vector.tensor_reduce(var[:], tot[:], AX.X, ALU.add).then_inc(step, 1)
            dve.wait_ge(std_ready, 1)
            nc.vector.reciprocal(rstd[:], std[:]).then_inc(step, 1)
            dve.wait_ge(step, 7)


def normalise_padded(nc, xt, padded, scratch, const, tag):
    with ExitStack() as ctx:
        sb, ps, sem = allocators(nc, ctx, tag)
        average, eps, stats, dev, spread, var, std, tot = moments_tensors(sb, ps)
        mean, rstd = sb("mean", [128, B]), sb("rstd", [128, B])
        xt_in, average_in, stats_ready, step = sem("xt_in"), sem("average_in"), sem("stats_ready"), sem("step")
        sum_ready, std_ready, done, border = sem("sum_ready"), sem("std_ready"), sem("done"), sem("border")
        sample = stats[:].rearrange("p b r (s k) -> p b (r s) k", k=3)
        block = ctx.enter_context(nc.Block())

        @block.sync
        def _(sp):
            sp.dma_start(average[:], const["average_groups"]).then_inc(average_in, 16)
            for b in range(B):
                sp.dma_start(xt[:, :, 256 * b:256 * b + 256], scratch["patches"][b // 2][:, :, 256 * (b % 2):256 * (b % 2) + 256]
                             ).then_inc(xt_in, 16)
                sp.wait_ge(xt_in, 16 * b + 16)

        @block.gpsimd
        def _(pool):
            pool.memset(padded[:, :, 0:18:17, :], 0.0).then_inc(border, 1)
            pool.wait_ge(border, 1)
            pool.memset(padded[:, :, :, 0:L + 2:L + 1], 0.0).then_inc(border, 1)

        @block.tensor
        def _(pe):
            pe.wait_ge(average_in, 16)
            pe.wait_ge(stats_ready, 8 * B)
            nc.tensor.matmul(tot[:], average[:], sample[:, :, :, 1], start=True, stop=True).then_inc(sum_ready, 1)
            pe.wait_ge(step, 5)
            nc.tensor.matmul(tot[:], average[:], spread[:], start=True, stop=True).then_inc(sum_ready, 1)

        @block.scalar
        def _(act):
            act.wait_ge(step, 6)
            nc.scalar.activation(std[:], var[:], ACT.Sqrt, bias=eps[:, 0:1]).then_inc(std_ready, 1)

        @block.vector
        def _(dve):
            dve.memset(eps[:], 1e-5).then_inc(step, 1)
            for b in range(B):
                dve.wait_ge(xt_in, 16 * b + 16)
                for r in range(8):
                    nc.vector.bn_stats(stats[:, b, r], xt[:, r, 256 * b:256 * b + 256]).then_inc(stats_ready, 1)
            dve.wait_ge(sum_ready, 1)
            nc.vector.tensor_reduce(mean[:], tot[:], AX.X, ALU.add).then_inc(step, 1)
            dve.wait_ge(step, 2)
            nc.vector.tensor_tensor(dev[:], sample[:, :, :, 1], mean[:].unsqueeze(2).broadcast_to([128, B, 16]),
                                    ALU.subtract).then_inc(step, 1)
            dve.wait_ge(step, 3)
            nc.vector.tensor_tensor(dev[:], dev[:], dev[:], ALU.mult).then_inc(step, 1)
            dve.wait_ge(step, 4)
            nc.vector.scalar_tensor_tensor(out=spread[:], in0=sample[:, :, :, 2], scalar=1.0 / 128, in1=dev[:],
                                           op0=ALU.mult, op1=ALU.add).then_inc(step, 1)
            dve.wait_ge(sum_ready, 2)
            nc.vector.tensor_reduce(var[:], tot[:], AX.X, ALU.add).then_inc(step, 1)
            dve.wait_ge(std_ready, 1)
            nc.vector.reciprocal(rstd[:], std[:]).then_inc(step, 1)
            dve.wait_ge(step, 7)
            for b in range(B):
                nc.vector.tensor_scalar(padded[:, b, 1:17, 1:L + 1].rearrange("p w (h r) -> p r w h", r=8),
                                        xt[:, :, 256 * b:256 * b + 256].rearrange("p r (w h) -> p r w h", h=16),
                                        mean[:, b:b + 1], rstd[:, b:b + 1], ALU.subtract, ALU.mult).then_inc(done, 1)


def patch_correlate(nc, io, half, x, mean, rstd, store, sums, scratch, const, tag):
    with ExitStack() as ctx:
        sb, ps, sem = allocators(nc, ctx, tag)
        raw = [sb(f"raw_{n}", [128, 8, 512]) for n in "qk"]
        w = [sb(f"w_{n}", [128, 2, 8, 2, 128], R32) for n in "qk"]
        bias = [sb(f"bias_{n}", [128, 8, 4]) for n in "qk"]
        to_freq = [sb(f"to_freq_{n}", [128, 2, 128]) for n in "qk"]
        gather = sb("gather", [128, 64])
        src = [sb(f"src_{n}", [128, 2, N]) for n in "qk"]
        qf = sb("qf", [128, 2, 2, N])
        pf = sb("pf", [128, 2, 2, N])
        acc = [ps(f"acc_{n}", [128, N]) for n in "qk"]
        freq = [[ps(f"freq_{n}{d}", [128, N]) for d in range(2)] for n in "qk"]
        o_ps = ps("o_ps", [128, N])
        consts_in, bias_in, x_in, scaled, x_high, x_low = (sem(n) for n in (
            "consts_in", "bias_in", "x_in", "scaled", "x_high", "x_low"))
        raw_in, high, low, done, out = ([sem(f"{n}_{m}") for m in "qk"] for n in ("raw_in", "high", "low", "done", "out"))
        qf_done, qf_out, kf_done, pf_ready = sem("qf_done"), sem("qf_out"), sem("kf_done"), sem("pf_ready")
        o_done, o_out, sums_zero, summed = sem("o_done"), sem("o_out"), sem("sums_zero"), sem("summed")
        block = ctx.enter_context(nc.Block())
        w_dram = [io[n].rearrange("r s c (d n) -> d (s c) r n", d=8) for n in ("Wq", "Wk")]
        xs = raw[1]
        STEPS = 16

        @block.sync
        def _(sp):
            sp.dma_start(raw[1][:], scratch["patches"][half]).then_inc(x_in, 16)
            sp.dma_start(raw[0][:], w_dram[0][0]).then_inc(raw_in[0], 16)
            for n, name in enumerate(("bq", "bk")):
                for e in range(2):
                    sp.dma_start(bias[n][64 * e:64 * e + 64], io[name].rearrange("(d a p h) -> a p d h", d=8, a=2, h=4)[e]
                                 ).then_inc(bias_in, 16)
            sp.dma_start(to_freq[0][:], const["patch_q"]).then_inc(consts_in, 16)
            sp.dma_start(to_freq[1][:], const["patch_k"]).then_inc(consts_in, 16)
            sp.dma_start(gather[:], const["patch_back"]).then_inc(consts_in, 16)
            sp.wait_ge(x_low, 2)
            sp.dma_start(raw[1][:], w_dram[1][0]).then_inc(raw_in[1], 16)
            with sp.Fori(1, 8) as d:
                for n in range(2):
                    sp.wait_ge(low[n], 2 * d)
                    sp.dma_start(raw[n][:], w_dram[n][d]).then_inc(raw_in[n], 16)

        def slab(n, g):
            return raw[n][:].rearrange("p r (e h) -> p r h e", h=4)[:, :, 2 * g:2 * g + 2, :]

        @block.tensor
        def _(pe):
            def project(n, t, k):
                pe.wait_ge(out[n], 2 * t + k)
                if k == 0:
                    pe.wait_ge(low[n], t + 1)
                for r in range(8):
                    mm = split_product(pe, acc[n][:], [w[n][:, m, r, k] for m in range(2)], [x[:, m, r] for m in range(2)],
                                       r == 0, r == 7)
                mm.then_inc(done[n], 1)

            def transform(n, t, k):
                pe.wait_ge(out[n], 2 * t + k + 1)
                pe.wait_ge(pf_ready if n else qf_out, 2 * t + k)
                for d in range(2):
                    mm = pe.matmul(freq[n][d][:], to_freq[n][:, d], src[n][:, k], start=True, stop=True)
                mm.then_inc(kf_done if n else qf_done, 1)

            def back(t, k):
                pe.wait_ge(pf_ready, 2 * t + k + 1)
                pe.wait_ge(o_out, 2 * t + k)
                for d in range(2):
                    mm = pe.matmul(o_ps[64 * d:64 * d + 64], gather[:], pf[:, k, d], start=True, stop=True)
                mm.then_inc(o_done, 1)

            def step(t, first):
                project(0, t, 0)
                if not first:
                    transform(1, t - 1, 1)
                project(0, t, 1)
                if not first:
                    back(t - 1, 0)
                transform(0, t, 0)
                if not first:
                    back(t - 1, 1)
                project(1, t, 0)
                transform(0, t, 1)
                project(1, t, 1)
                transform(1, t, 0)

            pe.wait_ge(consts_in, 48)
            pe.wait_ge(x_low, 2)
            step(0, True)
            step(1, False)
            with pe.Fori(1, 8) as d:
                step(2 * d, False)
                step(2 * d + 1, False)
            transform(1, STEPS - 1, 1)
            back(STEPS - 1, 0)
            back(STEPS - 1, 1)

        @block.scalar
        def _(act):
            def split(n, t, g):
                act.wait_ge(raw_in[n], 16 * (t // 2 + 1))
                if t:
                    act.wait_ge(done[n], 2 * t)
                split_high(nc.scalar, w[n][:, 0], slab(n, g)).then_inc(high[n], 1)

            def evacuate(n, t, k):
                act.wait_ge(done[n], 2 * t + k + 1)
                if t:
                    if n:
                        act.wait_ge(kf_done, 2 * t + k - 1)
                    else:
                        act.wait_ge(qf_done, 2 * t + k - 1)
                at = 2 * (t % 2) + k
                nc.scalar.activation(src[n][:, k], acc[n][:], ACT.Identity, bias=bias[n][:, t // 2, at:at + 1]).then_inc(out[n], 1)

            def spectrum_out(t, k):
                act.wait_ge(qf_done, 2 * t + k + 1)
                if t:
                    act.wait_ge(pf_ready, 2 * t + k - 1)
                for d in range(2):
                    op = nc.scalar.activation(qf[:, k, d], freq[0][d][:], ACT.Copy)
                op.then_inc(qf_out, 1)

            split(0, 0, 0)
            for b in range(2):
                act.wait_ge(scaled, b + 1)
                split_high(nc.scalar, x[:, 0, :, 256 * b:256 * b + 256], xs[:, :, 256 * b:256 * b + 256]).then_inc(x_high, 1)
            act.wait_ge(bias_in, 64)
            split(1, 0, 0)
            for t in range(STEPS):
                evacuate(0, t, 0)
                evacuate(0, t, 1)
                spectrum_out(t, 0)
                if t + 1 < STEPS:
                    split(0, t + 1, (t + 1) % 2)
                evacuate(1, t, 0)
                spectrum_out(t, 1)
                evacuate(1, t, 1)
                if t + 1 < STEPS:
                    split(1, t + 1, (t + 1) % 2)

        @block.vector
        def _(dve):
            def split(n, t, g):
                dve.wait_ge(high[n], t + 1)
                split_low(nc.vector, w[n][:, 1], slab(n, g), w[n][:, 0]).then_inc(low[n], 1)

            def product(t, k):
                dve.wait_ge(kf_done, 2 * t + k + 1)
                dve.wait_ge(qf_out, 2 * t + k + 1)
                for d in range(2):
                    op = nc.vector.tensor_tensor(pf[:, k, d], freq[1][d][:], qf[:, k, d], ALU.mult)
                op.then_inc(pf_ready, 1)

            def pixels_out(t, k, d, g):
                dve.wait_ge(o_done, 2 * t + k + 1)
                flat = store[:].rearrange("p h d n -> p (h d n)")
                at = dve.snap(d * N + (2 * g + k) * 8 * N)
                nc.vector.tensor_copy(flat[:, bass.ds(at, N)], o_ps[:]).then_inc(o_out, 1)

            def step(t, d, g, first, last):
                if not first:
                    product(t - 1, 1)
                    pixels_out(t - 1, 0, d - 1 if g == 0 else d, 1 - g)
                    pixels_out(t - 1, 1, d - 1 if g == 0 else d, 1 - g)
                if not last:
                    split(0, t + 1, 1 - g)
                product(t, 0)
                if not last:
                    split(1, t + 1, 1 - g)

            dve.memset(sums[:], 0.0).then_inc(sums_zero, 1)
            dve.wait_ge(x_in, 16)
            for b in range(2):
                at = slice(256 * b, 256 * b + 256)
                n = 2 * half + b
                nc.vector.tensor_scalar(xs[:, :, at], xs[:, :, at], mean[:, n:n + 1], rstd[:, n:n + 1],
                                        ALU.subtract, ALU.mult).then_inc(scaled, 1)
            for b in range(2):
                at = slice(256 * b, 256 * b + 256)
                dve.wait_ge(x_high, b + 1)
                split_low(nc.vector, x[:, 1, :, at], xs[:, :, at], x[:, 0, :, at]).then_inc(x_low, 1)
            split(0, 0, 0)
            split(1, 0, 0)
            step(0, 0, 0, True, False)
            step(1, 0, 1, False, False)
            with dve.Fori(1, 7) as d:
                step(2 * d, d, 0, False, False)
                step(2 * d + 1, d, 1, False, False)
            step(14, 7, 0, False, False)
            step(15, 7, 1, False, True)
            product(15, 1)
            pixels_out(15, 0, 7, 1)
            pixels_out(15, 1, 7, 1)

        @block.gpsimd
        def _(pool):
            pool.wait_ge(sums_zero, 1)
            pool.sem_inc(summed, 1)
            with pool.Fori(0, 8) as d:
                for head in range(4):
                    t = 4 * d + head
                    pool.wait_ge(o_out, t + 1)
                    pool.wait_ge(summed, t + 1)
                    flat = store[:].rearrange("p h d n -> p (h d n)")
                    at = pool.snap(d * N + head * 8 * N)
                    nc.gpsimd.tensor_tensor(sums[:, head], sums[:, head], flat[:, bass.ds(at, N)], ALU.add).then_inc(summed, 1)


def patch_norm(nc, store, sums, rstd, const, tag):
    with ExitStack() as ctx:
        sb, ps, sem = allocators(nc, ctx, tag)
        over_dims = sb("over_dims", [128, 128])
        eps = sb("eps", [128, 1])
        square = sb("square", [128, 2, 2, N])
        std = sb("std", [128, 4, N])
        mean_ps = [ps(f"mean_ps{h}", [128, N]) for h in range(4)]
        var_ps = [ps(f"var_ps{h}", [128, N]) for h in range(4)]
        const_in, eps_set, mean_ready, centred = sem("const_in"), sem("eps_set"), sem("mean_ready"), sem("centred")
        squared, summed, std_ready, done = sem("squared"), sem("summed"), sem("std_ready"), sem("done")
        block = ctx.enter_context(nc.Block())
        TILES = [(h, d) for h in range(4) for d in range(0, 8, 2)]

        @block.sync
        def _(sp):
            sp.dma_start(over_dims[:], const["over_dims"]).then_inc(const_in, 16)

        @block.tensor
        def _(pe):
            pe.wait_ge(const_in, 16)
            for h in range(4):
                pe.matmul(mean_ps[h][:], over_dims[:], sums[:, h], start=True, stop=True).then_inc(mean_ready, 1)
            for t, (h, d) in enumerate(TILES):
                pe.wait_ge(squared, t + 1)
                for e in range(2):
                    mm = pe.matmul(var_ps[h][:], over_dims[:], square[:, t % 2, e], start=d + e == 0, stop=d + e == 7)
                mm.then_inc(summed, 1)

        @block.vector
        def _(dve):
            dve.memset(eps[:], 1e-6).then_inc(eps_set, 1)

            def inverse(h):
                dve.wait_ge(std_ready, h + 1)
                nc.vector.reciprocal(rstd[:, h], std[:, h]).then_inc(done, 1)

            for t, (h, d) in enumerate(TILES):
                dve.wait_ge(mean_ready, h + 1)
                nc.vector.tensor_tensor(store[:, h, d:d + 2], store[:, h, d:d + 2],
                                        mean_ps[h][:].unsqueeze(1).broadcast_to([128, 2, N]), ALU.subtract).then_inc(centred, 1)
                if d == 4 and h:
                    inverse(h - 1)
            inverse(3)

        @block.scalar
        def _(act):
            act.wait_ge(eps_set, 1)

            def root(h):
                act.wait_ge(summed, 4 * h + 4)
                nc.scalar.activation(std[:, h], var_ps[h][:], ACT.Sqrt, bias=eps[:, 0:1]).then_inc(std_ready, 1)

            for t, (h, d) in enumerate(TILES):
                act.wait_ge(centred, t + 1)
                if t >= 2:
                    act.wait_ge(summed, t - 1)
                nc.scalar.activation(square[:, t % 2], store[:, h, d:d + 2], ACT.Square).then_inc(squared, 1)
                if d == 2 and h:
                    root(h - 1)
            root(3)


def patch_values(nc, io, x, store, rstd, const, tag):
    with ExitStack() as ctx:
        sb, ps, sem = allocators(nc, ctx, tag)
        raw = sb("raw", [128, 2, 8, 512])
        w = sb("w", [128, 2, 2, 8, 2, 128], R32)
        bv = sb("bv", [128, 8, 4])
        scale_shift = sb("scale_shift", [128, 8, 2])
        normed = sb("normed", [128, 2, N])
        affine = sb("affine", [128, 2, N])
        v_ps = [ps(f"v_ps{k}", [128, N]) for k in range(4)]
        vec_in, v_done, normed_ready, affine_ready, used = (sem(n) for n in (
            "vec_in", "v_done", "normed_ready", "affine_ready", "used"))
        raw_in, high, low = [sem(f"raw_in{k}") for k in range(2)], sem("high"), sem("low")
        block = ctx.enter_context(nc.Block())
        w_dram = io["Wv"].rearrange("r s c (d n) -> d (s c) r n", d=8)
        STEPS = 16

        @block.sync
        def _(sp):
            for k in range(2):
                sp.dma_start(raw[:, k], w_dram[k]).then_inc(raw_in[k], 16)
            for e in range(2):
                at = slice(64 * e, 64 * e + 64)
                sp.dma_start(bv[at], io["bv"].rearrange("(d a p h) -> a p d h", d=8, a=2, h=4)[e]).then_inc(vec_in, 16)
                for k, name in enumerate(("ln_scale", "ln_bias")):
                    with nc.allow_non_contiguous_dma(reason="16 values"):
                        sp.dma_start(scale_shift[at, :, k], io[name].rearrange("(o d a) -> a o d", o=1, a=2)[e].broadcast_to([64, 8])
                                     ).then_inc(vec_in, 16)
            with sp.Fori(1, 4) as n:
                for k in range(2):
                    sp.wait_ge(low, 4 * n + 2 * k - 2)
                    sp.dma_start(raw[:, k], w_dram[2 * n + k]).then_inc(raw_in[k], 16)

        def slab(t):
            return raw[:, t // 2 % 2].rearrange("p r (e h) -> p r h e", h=4)[:, :, 2 * (t % 2):2 * (t % 2) + 2, :]

        @block.tensor
        def _(pe):
            with pe.Fori(0, 8) as d:
                for g in range(2):
                    pe.wait_ge(low, 2 * d + g + 1)
                    for k in range(2):
                        pe.wait_ge(used, 4 * d + 2 * g + k + 1)
                        for r in range(8):
                            mm = split_product(pe, v_ps[2 * g + k][:], [w[:, g, m, r, k] for m in range(2)],
                                               [x[:, m, r] for m in range(2)], r == 0, r == 7)
                        mm.then_inc(v_done, 1)

        @block.gpsimd
        def _(pool):
            for t in range(4 * 8):
                d, head = t // 4, t % 4
                if t >= 2:
                    pool.wait_ge(affine_ready, t - 1)
                nc.gpsimd.tensor_tensor(normed[:, t % 2], store[:, head, d], rstd[:, head], ALU.mult).then_inc(normed_ready, 1)

        @block.scalar
        def _(act):
            def split(t):
                act.wait_ge(raw_in[t // 2 % 2], 16 * (t // 4 + 1))
                if t >= 2:
                    act.wait_ge(v_done, 2 * t - 2)
                split_high(nc.scalar, w[:, t % 2, 0], slab(t)).then_inc(high, 1)

            split(0)
            split(1)
            act.wait_ge(vec_in, 16 * 6)
            for t in range(32):
                d = t // 4
                act.wait_ge(normed_ready, t + 1)
                if t >= 2:
                    act.wait_ge(used, t - 1 + 4)
                nc.scalar.activation(affine[:, t % 2], normed[:, t % 2], ACT.Identity, scale=scale_shift[:, d, 0:1],
                                     bias=scale_shift[:, d, 1:2]).then_inc(affine_ready, 1)
                if t % 2 and t // 2 + 2 < STEPS:
                    split(t // 2 + 2)

        @block.vector
        def _(dve):
            def split(t):
                dve.wait_ge(high, t + 1)
                split_low(nc.vector, w[:, t % 2, 1], slab(t), w[:, t % 2, 0]).then_inc(low, 1)

            dve.sem_inc(used, 4)
            split(0)
            split(1)
            dve.wait_ge(vec_in, 16 * 6)
            for t in range(32):
                d, head = t // 4, t % 4
                dve.wait_ge(v_done, t + 1)
                dve.wait_ge(affine_ready, t + 1)
                nc.vector.scalar_tensor_tensor(out=store[:, head, d], in0=v_ps[head][:], scalar=bv[:, d, head:head + 1],
                                               in1=affine[:, t % 2], op0=ALU.add, op1=ALU.mult).then_inc(used, 1)
                if t % 2 and t // 2 + 2 < STEPS:
                    split(t // 2 + 2)


def patch_project(nc, io, half, store, scratch, const, tag):
    with ExitStack() as ctx:
        sb, ps, sem = allocators(nc, ctx, tag)
        raw = sb("raw", [128, 2, 8 * 128])
        w = sb("w", [128, 2, 2, 8, 8, C], R32)
        u = sb("u", [128, 2, 2, N], R32)
        xt = sb("xt", [128, 8, N])
        bout = sb("bout", [128, 8])
        acc = [ps(f"acc{r}", [128, N]) for r in range(8)]
        bias_in, xt_in, low, done, acc_done, summed, stored = (sem(n) for n in (
            "bias_in", "xt_in", "low", "done", "acc_done", "summed", "stored"))
        raw_in = [sem(f"raw_in{k}") for k in range(2)]
        high = sem("high")
        block = ctx.enter_context(nc.Block())
        w_dram = io["Wout"].rearrange("a b (h d e) n -> h d e (a b) n", h=4, e=2)
        TILES = [(d, h) for d in range(8) for h in range(4)]

        @block.sync
        def _(sp):
            def load(d, h):
                for e in range(2):
                    sp.dma_start(raw[64 * e:64 * e + 64, h % 2], w_dram[h, d, e]).then_inc(raw_in[h % 2], 16)

            load(0, 0)
            load(0, 1)
            for h in range(2, 4):
                sp.wait_ge(low, h - 1)
                load(0, h)
            sp.dma_start(xt[:], scratch["patches"][half]).then_inc(xt_in, 16)
            with nc.allow_non_contiguous_dma(reason="the bias, once"):
                for s in range(8):
                    sp.dma_start(bout[C * s:C * s + C], io["bout"].rearrange("(c r s) -> s c r", r=8, s=8)[s]).then_inc(bias_in, 16)
            with sp.Fori(1, 8) as d:
                for h in range(4):
                    sp.wait_ge(low, 4 * d + h - 1)
                    load(d, h)
            for r in range(8):
                sp.wait_ge(summed, r + 1)
                sp.dma_start(scratch["patches"][half][:, r], xt[:, r]).then_inc(stored, 16)
            sp.wait_ge(stored, 16 * 8)

        @block.scalar
        def _(act):
            for t, (d, h) in enumerate(TILES):
                k = t % 2
                act.wait_ge(raw_in[k], 32 * (t // 2 + 1))
                if t >= 2:
                    act.wait_ge(done, t - 1)
                split_high(nc.scalar, w[:, k, 0], raw[:, k].rearrange("p (c r s) -> p r s c", r=8, s=8))
                split_high(nc.scalar, u[:, k, 0], store[:, h, d]).then_inc(high, 1)

        @block.vector
        def _(dve):
            for t, (d, h) in enumerate(TILES):
                k = t % 2
                dve.wait_ge(high, t + 1)
                split_low(nc.vector, w[:, k, 1], raw[:, k].rearrange("p (c r s) -> p r s c", r=8, s=8), w[:, k, 0])
                split_low(nc.vector, u[:, k, 1], store[:, h, d], u[:, k, 0]).then_inc(low, 1)
            dve.wait_ge(bias_in, 16 * 8)
            dve.wait_ge(xt_in, 16)
            for r in range(8):
                dve.wait_ge(acc_done, r + 1)
                nc.vector.scalar_tensor_tensor(out=xt[:, r], in0=acc[r][:], scalar=bout[:, r:r + 1], in1=xt[:, r],
                                               op0=ALU.add, op1=ALU.add).then_inc(summed, 1)

        @block.tensor
        def _(pe):
            def tile(t, k, first, last):
                pe.wait_ge(low, t + 1)
                for r in range(8):
                    mm = split_product(pe, acc[r][:], [w[:, k, m, r].rearrange("p s c -> p (s c)") for m in range(2)],
                                       [u[:, k, m] for m in range(2)], first, last)
                    if last:
                        mm.then_inc(acc_done, 1)
                if not last:
                    mm.then_inc(done, 1)

            tile(0, 0, True, False)
            tile(1, 1, False, False)
            with pe.Fori(1, 15) as n:
                for k in range(2):
                    tile(2 * n + k, k, False, False)
            tile(30, 0, False, False)
            tile(31, 1, False, True)


def local_conv(nc, io, xt, padded, image, const, tag):
    with ExitStack() as ctx:
        sb, ps, sem = allocators(nc, ctx, tag)
        ident = sb("ident", [128, 128])
        band = sb("band", [128, 3, 128])
        cross = sb("cross", [96, 128])
        bias = sb("bias", [128, 1])
        edge = sb("edge", [96, B, 16, L])
        res = sb("res", [128, 3, 4, L])
        acc = [ps(f"acc{k}", [128, 4, L]) for k in range(3)]
        turn = [ps(f"turn{k}", [128, 4, 128]) for k in range(3)]
        zeroed, w_in, edge_in, ident_in, bias_in = sem("zeroed"), sem("w_in"), sem("edge_in"), sem("ident_in"), sem("bias_in")
        acc_done, res_ready, turned, moved = sem("acc_done"), sem("res_ready"), sem("turned"), sem("moved")
        block = ctx.enter_context(nc.Block())

        @block.sync
        def _(sp):
            for dy in range(3):
                for side in range(2):
                    rows = padded[16 * 7:128] if side == 0 else padded[0:16]
                    for b in range(B):
                        sp.dma_start(edge[32 * dy + 16 * side:32 * dy + 16 * side + 16, b],
                                     rows[:, b, 2 * side:2 * side + 16, dy:dy + L]).then_inc(edge_in, 16)

        @block.scalar
        def _(act):
            act.wait_ge(zeroed, 1)
            for s in range(8):
                for dx in range(3):
                    at = s + dx - 1
                    if 0 <= at < 8:
                        act.dma_start(band[C * at:C * at + C, :, C * s:C * s + C],
                                      io["filters3"][:, dx].rearrange("y i j -> i y j")).then_inc(w_in, 16)
            for dy in range(3):
                act.dma_start(cross[32 * dy:32 * dy + 16, 0:C], io["filters3"][dy, 0]).then_inc(w_in, 16)
                act.dma_start(cross[32 * dy + 16:32 * dy + 32, 7 * C:8 * C], io["filters3"][dy, 2]).then_inc(w_in, 16)
            act.dma_start(ident[:], const["ident"]).then_inc(ident_in, 16)
            for s in range(8):
                act.dma_start(bias[C * s:C * s + C, :], io["bias3"].rearrange("(c o) -> c o", o=1)).then_inc(bias_in, 16)
            for t in range(16):
                b, w4 = t // 4, t % 4
                act.wait_ge(turned, t + 1)
                nc.scalar.activation(image[:, b, 32 * w4:32 * w4 + 32, :].rearrange("h w c -> h (w c)"),
                                     turn[t % 3][:].rearrange("h a n -> h (a n)"), ACT.Copy).then_inc(moved, 1)

        @block.tensor
        def _(pe):
            pe.wait_ge(w_in, 16 * 28)
            pe.wait_ge(ident_in, 16)

            def turn_tile(t):
                pe.wait_ge(res_ready, t + 1)
                if t >= 3:
                    pe.wait_ge(moved, t - 2)
                for k in range(4):
                    mm = nc.tensor.matmul(turn[t % 3][:, k], res[:, t % 3, k], ident[:], start=True, stop=True)
                mm.then_inc(turned, 1)

            for t in range(16):
                b, w4 = t // 4, t % 4
                if t >= 3:
                    pe.wait_ge(res_ready, t - 2)
                for dy in range(3):
                    nc.tensor.matmul(acc[t % 3][:], band[:, dy], padded[:, b, 4 * w4 + 1:4 * w4 + 5, dy:dy + L],
                                     start=dy == 0, stop=False)
                if t == 0:
                    pe.wait_ge(edge_in, 16 * 6 * B)
                nc.tensor.matmul(acc[t % 3][:], cross[:], edge[:, b, 4 * w4:4 * w4 + 4], start=False, stop=True).then_inc(acc_done, 1)
                if t >= 1:
                    turn_tile(t - 1)
            turn_tile(15)

        @block.vector
        def _(dve):
            dve.memset(band[:], 0.0)
            dve.memset(cross[:], 0.0).then_inc(zeroed, 1)
            dve.wait_ge(bias_in, 16 * 8)
            for t in range(16):
                dve.wait_ge(acc_done, t + 1)
                if t >= 3:
                    dve.wait_ge(turned, t - 2)
                nc.vector.scalar_tensor_tensor(
                    out=res[:, t % 3].rearrange("p w (h r) -> p (w h) r", r=8), in0=acc[t % 3][:].rearrange("p w (h r) -> p (w h) r", r=8),
                    scalar=bias[:, 0:1], in1=xt[:, :, 64 * t:64 * t + 64].rearrange("p r n -> p n r"),
                    op0=ALU.add, op1=ALU.add).then_inc(res_ready, 1)


def build(nc, io, const, out):
    scratch = {
        "filters": nc.dram_tensor("filters_dram", (8, L, 128, 128), F32, kind="Internal").ap(),
        "spectrum": nc.dram_tensor("spectrum_dram", (C, L, 2, B * ROW), F32, kind="Internal").ap(),
        "products": nc.dram_tensor("products_dram", (L, C, 2, 2 * B * L), F32, kind="Internal").ap(),
        "patches": nc.dram_tensor("patches_dram", (2, 128, 8, N), F32, kind="Internal").ap(),
    }
    build_filters(nc, io, scratch, const)
    with nc.sbuf_tensor("mean1", [128, B], F32) as mean, nc.sbuf_tensor("rstd1", [128, B], F32) as rstd:
        with nc.sbuf_tensor("image0", [128, B, L, C], F32) as image:
            spectrum(nc, image, io["x"], scratch, const, "s0_")
            convolve(nc, 0, scratch, "c0_")
            back_to_image(nc, image, None, scratch, const, "b0_")
            to_patches(nc, image, mean, rstd, scratch, const, "tp_")
        for half in range(2):
            patch_mixer(nc, io, half, mean, rstd, scratch, const)
    with nc.sbuf_tensor("image1", [128, B, L, C], F32) as image:
        with nc.sbuf_tensor("xt", [128, 8, PATCHES], F32) as xt, nc.sbuf_tensor("padded", [128, B, 18, L + 2], F32) as padded:
            normalise_padded(nc, xt, padded, scratch, const, "n2_")
            local_conv(nc, io, xt, padded, image, const, "l_")
        spectrum(nc, image, None, scratch, const, "s3_")
        convolve(nc, 1, scratch, "c3_")
        back_to_image(nc, image, out, scratch, const, "b3_")


def patch_mixer(nc, io, half, mean, rstd, scratch, const):
    with nc.sbuf_tensor(f"xn{half}", [128, 2, 8, N], R32) as x, nc.sbuf_tensor(f"store{half}", [128, 4, 8, N], F32) as store:
        with nc.sbuf_tensor(f"sums{half}", [128, 4, N], F32) as sums:
            patch_correlate(nc, io, half, x, mean, rstd, store, sums, scratch, const, f"q{half}_")
            with nc.sbuf_tensor(f"rstds{half}", [128, 4, N], F32) as rstds:
                patch_norm(nc, store, sums, rstds, const, f"ln{half}_")
                patch_values(nc, io, x, store, rstds, const, f"v{half}_")
        patch_project(nc, io, half, store, scratch, const, f"o{half}_")


INPUTS = {
    "x": "x", "L0_conv_h0": "h00", "L0_conv_numerators": "num0", "L0_conv_denumerator": "den0",
    "L1_conv_Wq": "Wq", "L1_conv_bq": "bq", "L1_conv_Wk": "Wk", "L1_conv_bk": "bk", "L1_conv_Wv": "Wv", "L1_conv_bv": "bv",
    "L1_conv_ln_scale": "ln_scale", "L1_conv_ln_bias": "ln_bias", "L1_conv_Wout": "Wout", "L1_conv_bout": "bout",
    "L2_conv_filters": "filters3", "L2_conv_bias": "bias3",
    "L3_conv_h0": "h01", "L3_conv_numerators": "num1", "L3_conv_denumerator": "den1",
}


def kernel(**inputs):
    import numpy as _np
    import concourse.bacc as _bacc
    from concourse import mybir as _mybir
    from concourse.bass_utils import run_bass_kernel_spmd as _run

    nc = _bacc.Bacc("TRN2", target_bir_lowering=False, num_devices=1)
    arrays, io, const = {}, {}, {}
    for name, short in INPUTS.items():
        a = _np.ascontiguousarray(inputs[name])
        arrays[f"in_{name}"] = a
        io[short] = nc.dram_tensor(f"in_{name}", a.shape, _mybir.dt.from_np(a.dtype), kind="ExternalInput").ap()
    for layer in range(2):
        io[f"num{layer}"] = io[f"num{layer}"][0]
    for name, table in {**dft_tables(), **patch_tables()}.items():
        a = _np.ascontiguousarray(table.astype(_np.float32))
        arrays[f"const_{name}"] = a
        const[name] = nc.dram_tensor(f"const_{name}", a.shape, _mybir.dt.float32, kind="ExternalInput").ap()
    out = nc.dram_tensor("out_dram", (4, 128, 128, 16), _mybir.dt.float32, kind="ExternalOutput").ap()
    build(nc, io, const, out)
    r = _run(nc, [arrays], core_ids=[0])
    return r.results[0]["out_dram"]
```

```python
from contextlib import ExitStack
import numpy as np
import concourse.bass as bass
from concourse import mybir
ALU = mybir.AluOpType
ACT = mybir.ActivationFunctionType
AX = mybir.AxisListType
F32 = mybir.dt.float32

def allocators(nc, ctx, prefix):
    sems = []

    def clear():
        nc.clear_and_free_semaphores(sems)
        nc.all_engine_barrier()

    ctx.callback(clear)

    def sb(name, shape, dt=F32):
        return ctx.enter_context(nc.sbuf_tensor(prefix + name, shape, dt))

    def ps(name, shape):
        return ctx.enter_context(nc.psum_tensor(prefix + name, shape, F32))

    def sem(name):
        sems.append(nc.alloc_semaphore(name=prefix + name))
        return sems[-1]

    return sb, ps, sem

L, FW, B, C = 128, 64, 4, 16


def dft_tables():
    f64 = np.float64
    n = np.arange(L, dtype=f64)
    tau = 2 * np.pi
    p = np.repeat(np.arange(1, 9), 8).astype(f64)
    q = np.tile(np.arange(1, 9), 8).astype(f64)
    edge = [(a, b) for a in range(9) for b in range(9) if a == 0 or b == 0]
    taps = np.zeros((65, FW + 1, 2, L))
    for fw in range(FW + 1):
        ang = tau * (np.outer(p, n) + (q * fw)[:, None]) / L
        taps[:64, fw, 0], taps[:64, fw, 1] = np.cos(ang), -np.sin(ang)
        e = sum(np.exp(-1j * tau * (n * a + fw * b) / L) for a, b in edge)
        taps[64, fw, 0], taps[64, fw, 1] = e.real, e.imag
    ang = tau * np.outer(n, n) / L
    inv_h = np.stack([np.cos(ang), np.sin(ang), -np.sin(ang)], 1) / L
    s = np.arange(FW, dtype=f64)
    fwd = np.zeros((2, L, 2, FW))
    fwd[0, :, 0], fwd[0, :, 1] = np.cos(tau * np.outer(n, s) / L), -np.sin(tau * np.outer(n, s) / L)
    fwd[0, :, 1, 0] = (-1.0) ** n
    odd = tau * np.outer(n, 2 * s + 1) / (2 * L)
    fwd[1, :, 0], fwd[1, :, 1] = np.cos(odd), -np.sin(odd)
    back = np.zeros((2, FW, L))
    back[0], back[1] = 2 * np.cos(tau * np.outer(s, n) / L) / L, -2 * np.sin(tau * np.outer(s, n) / L) / L
    back[0, 0], back[1, 0] = 1.0 / L, (-1.0) ** n / L
    back = back.reshape(L, L)
    respread = np.zeros((L, 2, FW, 2))
    for c in range(2):
        for k in range(FW):
            respread[c * FW + k, 0, k, c] = 1.0
    respread[:, 1] = (back @ fwd[1].reshape(L, 2 * FW)).reshape(L, 2, FW).transpose(0, 2, 1)
    respread = respread.reshape(L, L // 4, 4, 2).transpose(0, 1, 3, 2)
    inv = np.zeros((2, FW, 2, 2, L))
    for par in range(2):
        a = tau * np.outer(2 * s + par, n) / (2 * L)
        co, si = np.cos(a) / L, np.sin(a) / L
        inv[0, :, par, 0], inv[1, :, par, 0] = co, -si
        inv[0, :, par, 1], inv[1, :, par, 1] = -si, -co
    inv[:, 0, 0] = 0.0
    inv[0, 0, 0, 0] = 0.5 / L
    inv[1, 0, 0, 1] = 0.5 * (-1.0) ** n / L
    return {
        "taps": taps.reshape(65, -1), "inv_h": inv_h.reshape(L, -1),
        "fwd_w": fwd.reshape(2, L, L).transpose(1, 0, 2).reshape(L, -1),
        "respread": respread.reshape(L, -1), "inv_w": inv.reshape(L, -1),
    }


def patch_tables():
    f64 = np.float64
    u, v = np.repeat(np.arange(8), 8), np.tile(np.arange(8), 8)
    real = [(a, b) for a in (0, 4) for b in (0, 4)]
    pairs = [(a, b) for a in range(8) for b in range(8) if (a, b) not in real and (a, b) < ((-a) % 8, (-b) % 8)]
    ang = lambda fs: 2 * np.pi * np.array([[(a * x + b * y) / 8 for a, b in fs] for x, y in zip(u, v)], dtype=f64)
    cx, rl = ang(pairs), ang(real)
    re, im = np.cos(cx), -np.sin(cx)
    q = np.concatenate([re, im, re, im, np.cos(rl), np.zeros((64, 4))], 1)
    k = np.concatenate([re, im, im, re, np.cos(rl), np.zeros((64, 4))], 1)
    co, si = 2 * np.cos(cx).T / 64, -2 * np.sin(cx).T / 64
    back = np.concatenate([co, -co, si, si, np.cos(rl).T / 64, np.zeros((4, 64))])
    two = np.zeros((2, 2, 128, 2, 128))
    for n, m in enumerate((q, k)):
        for d in range(2):
            two[n, 0, 64 * d:64 * d + 64, d] = m
    pix, grp = np.arange(128) % 64, np.arange(128) % 16 // 2
    return {
        "patch_q": two[0, 0].reshape(128, 256), "patch_k": two[1, 0].reshape(128, 256), "patch_back": back,
        "over_dims": (pix[:, None] == pix) / 16.0, "average_groups": (grp[:, None] == grp) / 256.0,
        "average": np.full((128, 128), 1 / 256), "ident": np.eye(128),
    }


R32 = mybir.dt.float32r
GROUPS = L // 4


def split_high(eng, out, src):
    return eng.activation(out, src, ACT.Copy)


def split_low(eng, out, src, high):
    return eng.tensor_tensor(out, src, high.bitcast(F32), ALU.subtract)


def split_product(pe, out, w, x, first, last):
    pe.matmul(out, w[0], x[0], start=first, stop=False)
    pe.matmul(out, w[0], x[1], start=False, stop=False)
    return pe.matmul(out, w[1], x[0], start=False, stop=last)


def build_filters(nc, io, scratch, const):
    QUARTERS, PAIRS = 8, 64
    BLOCKS = [list(range(4 * n, 4 * n + 4)) for n in range(15)] + [[60, 61], [62, 63], [FW]]
    NB = len(BLOCKS)
    KB, PIECES = L // 8, 8
    with ExitStack() as ctx:
        sb, ps, sem = allocators(nc, ctx, "f_")
        raw = sb("raw", [128, 8, 64])
        ident = sb("ident", [128, 128])
        taps_ab = sb("taps_ab", [65, QUARTERS, 2, PAIRS])
        table = sb("table", [65, 2, 4, 2, L])
        inv_h = sb("inv_h", [L, 3, L])
        respread_raw = sb("respread_raw", [L, 2 * 128])
        respread = sb("respread", [L, 2, 2 * 128], R32)
        h0s = sb("h0s", [65, 2, C, C])
        h0_taps = sb("h0_taps", [65, QUARTERS, PAIRS])
        den = sb("den", [128, 2, 4, 2, PAIRS])
        sq = sb("sq", [128, 2, 4, 2, PAIRS])
        mag = sb("mag", [128, 2, 4, PAIRS])
        rec = sb("rec", [128, 2, 4, PAIRS])
        straight = sb("straight", [128, 2, 4, 2, PAIRS])
        crossed = sb("crossed", [128, 2, 4, 2, PAIRS])
        ratio = sb("ratio", [128, 2, 4, 2, PAIRS])
        nyq = sb("nyq", [128, 2, PAIRS])
        spec = sb("spec", [L, 2, 2, PAIRS, FW])
        lags = sb("lags", [128, 2, 2, L, C], R32)
        stage = sb("stage", [128, 2, GROUPS, 4, 4, KB])
        ab = [ps(f"ab{k}", [128, 4, 2, 2, PAIRS]) for k in range(2)]
        mid = [ps(f"mid{k}", [128, 4, 128]) for k in range(2)]
        far = [ps(f"far{k}", [128, GROUPS, 2, 8]) for k in range(2)]

        raw_in, consts_in, h0_in = sem("raw_in"), sem("consts_in"), sem("h0_in")
        table_in = [sem(f"table_in{k}") for k in range(2)]
        turned, turned_out, edges_set, taps_ready = sem("turned"), sem("turned_out"), sem("edges_set"), sem("taps_ready")
        respread_split = sem("respread_split")
        ab_ready, den_ready, mag_ready, rec_ready = sem("ab_ready"), sem("den_ready"), sem("mag_ready"), sem("rec_ready")
        prod_ready, num_ready, ratio_ready, quot_ready = sem("prod_ready"), sem("num_ready"), sem("ratio_ready"), sem("quot_ready")
        spec_ready, mid_ready, lags_high, lags_low = sem("spec_ready"), sem("mid_ready"), sem("lags_high"), sem("lags_low")
        far_ready, far_out = sem("far_ready"), [sem(f"far_out{k}") for k in range(2)]
        stored = [sem(f"stored{k}") for k in range(2)]

        block = ctx.enter_context(nc.Block())

        def table_load(eng, q, blk):
            fws = BLOCKS[blk]
            eng.dma_start(table[:, blk % 2, 0:len(fws)],
                          const["taps"][:, fws[0] * 2 * L:(fws[-1] + 1) * 2 * L]).then_inc(table_in[blk % 2], 16)

        @block.sync
        def _(sp):
            for layer in range(2):
                for ab_ in range(2):
                    src = io[("den", "num")[ab_] + str(layer)].rearrange("(t a) b p q -> t (a b) (p q)", t=2)
                    for t in range(2):
                        sp.dma_start(raw[:, layer * 4 + ab_ * 2 + t, :], src[t]).then_inc(raw_in, 16)
            sp.dma_start(ident[:], const["ident"]).then_inc(raw_in, 16)
            sp.dma_start(inv_h[:], const["inv_h"]).then_inc(consts_in, 16)
            sp.dma_start(respread_raw[:], const["respread"]).then_inc(consts_in, 16)
            for layer in range(2):
                h0 = io[f"h0{layer}"].rearrange("i j a b -> (a b) (i j)")
                sp.dma_start(h0s[:, layer], h0.broadcast_to([65, 256])).then_inc(h0_in, 16)
            table_load(sp, 0, 0)
            table_load(sp, 0, 1)
            for blk in range(2, NB):
                sp.wait_ge(ab_ready, blk - 1)
                table_load(sp, 0, blk)

            def store(q, jp, piece):
                if piece == 0:
                    for k in range(2):
                        sp.wait_ge(far_out[k], q * KB + 9 + 8 * jp)
                at = slice(GROUPS // PIECES * piece, GROUPS // PIECES * (piece + 1))
                sp.dma_start(scratch["filters"][q, jp, :, at], stage[:, jp, at].rearrange("p g m s k -> p g (m s k)")
                             ).then_inc(stored[jp], 16)

            def step(q):
                for blk in range(NB):
                    sp.wait_ge(ab_ready, q * NB + blk - 1)
                    table_load(sp, q, blk)
                    if 2 <= blk < 10 and not (isinstance(q, int) and q == 1):
                        store(q - 2, 1, blk - 2)
                    if blk >= 10:
                        store(q - 1, 0, blk - 10)

            step(1)
            with sp.Fori(2, QUARTERS) as q:
                step(q)
            for q, jp in ((QUARTERS - 2, 1), (QUARTERS - 1, 0), (QUARTERS - 1, 1)):
                for piece in range(PIECES):
                    store(q, jp, piece)
            for jp in range(2):
                sp.wait_ge(stored[jp], 16 * PIECES * QUARTERS)

        def transform_taps(q, blk):
            n = q * NB + blk
            nc.tensor.wait_ge(table_in[blk % 2], 16 * (q * (NB // 2) + blk // 2 + 1))
            if not (isinstance(q, int) and n < 2):
                nc.tensor.wait_ge(prod_ready, n - 1)
            for k in range(len(BLOCKS[blk])):
                for part in range(2):
                    mm = nc.tensor.matmul(ab[blk % 2][:, k, part], table[:, blk % 2, k, part],
                                          taps_ab[:, q], start=True, stop=True)
            mm.then_inc(ab_ready, 1)

        LAG_GROUPS, SLOT_UNITS = [range(0)] * NB, [range(0)] * NB
        for n in range(4):
            LAG_GROUPS[1 + n], LAG_GROUPS[8 + n] = range(2 * n, 2 * n + 2), range(8 + 2 * n, 10 + 2 * n)
        for n, at in enumerate((0, 5, 10)):
            SLOT_UNITS[5 + n] = range(at, (5, 10, 16)[n])
        for n in range(5):
            SLOT_UNITS[12 + n] = range(16 + 3 * n, 19 + 3 * n if n < 4 else 32)

        def lag_tile(half, g):
            return lags[:, half, g // 4 % 2, :, 4 * (g % 4):4 * (g % 4) + 4].rearrange("p k i -> p i k")

        def to_lags(q, k, g):
            n = q * 16 + g
            if not (isinstance(q, int) and n < 2):
                nc.tensor.wait_ge(lags_low, n - 1)
            for m in range(4):
                pair = 4 * g + m
                re, im = spec[:, k, 0, pair, :], spec[:, k, 1, pair, :]
                lo, hi = mid[g % 2][0:FW, m], mid[g % 2][FW:128, m]
                nc.tensor.matmul(lo, re, inv_h[:, 0], start=True, stop=False)
                nc.tensor.matmul(hi, im, inv_h[:, 0], start=True, stop=False)
                nc.tensor.matmul(lo, im, inv_h[:, 2], start=False, stop=True)
                mm = nc.tensor.matmul(hi, re, inv_h[:, 1], start=False, stop=True)
            mm.then_inc(mid_ready, 1)

        def to_slots(q, u):
            kb = u % KB
            if kb == 0:
                nc.tensor.wait_ge(lags_low, q * 16 + u // 2 + 8)
            nc.tensor.wait_ge(far_out[u % 2], q * KB + u // 2 + 1)
            for j in range(2):
                mm = split_product(nc.tensor, far[u % 2][:, :, j], [lags[:, m, j, 8 * kb:8 * kb + 8, :] for m in range(2)],
                                   [respread[:, m] for m in range(2)], True, True)
            mm.then_inc(far_ready, 1)

        @block.tensor
        def _(pe):
            pe.wait_ge(raw_in, 16 * 9)
            for t in range(8):
                if t >= 2:
                    pe.wait_ge(turned_out, t - 1)
                nc.tensor.transpose(mid[t % 2][0:64, 0, :], raw[:, t, :], ident[:]).then_inc(turned, 1)
            pe.wait_ge(turned_out, 8)
            pe.wait_ge(taps_ready, 2)

            def turn_back(q, k, blk):
                if blk == 1:
                    pe.wait_ge(spec_ready, q + 1)
                for g in LAG_GROUPS[blk]:
                    to_lags(q, k, g)
                for u in SLOT_UNITS[blk]:
                    to_slots(q, u)

            def step(q, k):
                for blk in range(NB):
                    transform_taps(q + 1, blk)
                    turn_back(q, k, blk)

            for blk in range(NB):
                transform_taps(0, blk)
            pe.wait_ge(consts_in, 32)
            pe.wait_ge(respread_split, 2)
            step(0, 0)
            with pe.Fori(1, QUARTERS // 2) as p:
                step(2 * p - 1, 1)
                step(2 * p, 0)
            for blk in range(NB):
                turn_back(QUARTERS - 1, 1, blk)

        @block.scalar
        def _(act):
            def split_den(q, blk):
                n, f, s = q * NB + blk, len(BLOCKS[blk]), blk % 2
                act.wait_ge(ab_ready, n + 1)
                if not (isinstance(q, int) and n < 2):
                    act.wait_ge(prod_ready, n - 1)
                    act.wait_ge(mag_ready, n - 1)
                nc.scalar.activation(den[:, s, 0:f], ab[s][:, 0:f, :, 0], ACT.Copy)
                nc.scalar.activation(sq[:, s, 0:f], ab[s][:, 0:f, :, 0], ACT.Square).then_inc(den_ready, 1)

            def lags_out(q, g):
                if g % 8 == 0 and not (isinstance(q, int) and q == 0 and g == 0):
                    act.wait_ge(far_ready, q * 2 * KB + 2 * g)
                act.wait_ge(mid_ready, q * 16 + g + 1)
                split_high(nc.scalar, lag_tile(0, g), mid[g % 2][:]).then_inc(lags_high, 1)

            def slots_out(q, u):
                jp, kb = u // KB, u % KB
                act.wait_ge(far_ready, q * 2 * KB + u + 1)
                if kb == 0 and not (isinstance(q, int) and q == 0):
                    act.wait_ge(stored[jp], 16 * PIECES * q)
                nc.scalar.activation(stage[:, jp, :, :, :, kb], far[u % 2][:].rearrange("p g j (c s) -> p g (j c) s", c=2),
                                     ACT.Copy).then_inc(far_out[u % 2], 1)
            for k in range(2):
                act.sem_inc(far_out[k], 1)
            def step(q):
                for blk in range(NB):
                    split_den(q + 1, blk)
                    for g in LAG_GROUPS[blk]:
                        lags_out(q, g)
                    for u in SLOT_UNITS[blk]:
                        slots_out(q, u)

            act.wait_ge(consts_in, 32)
            split_high(nc.scalar, respread[:, 0], respread_raw[:]).then_inc(respread_split, 1)
            for blk in range(NB):
                split_den(0, blk)
            step(0)
            with act.Fori(1, QUARTERS - 1) as q:
                step(q)
            for blk in range(NB):
                for g in LAG_GROUPS[blk]:
                    lags_out(QUARTERS - 1, g)
                for u in SLOT_UNITS[blk]:
                    slots_out(QUARTERS - 1, u)

        @block.vector
        def _(dve):
            for t in range(8):
                dve.wait_ge(turned, t + 1)
                layer, ab_, half = t // 4, t // 2 % 2, t % 2
                for jq in range(4):
                    op = nc.vector.tensor_copy(
                        taps_ab[0:64, 4 * layer + jq, ab_].rearrange("r (j i) -> r i j", i=C)[:, 8 * half:8 * half + 8, :],
                        mid[t % 2][0:64, 0, :].rearrange("r (i q j) -> r q i j", q=4, j=4)[:, jq])
                op.then_inc(turned_out, 1)
            dve.memset(taps_ab[64:65, :, 1, :], 0.0)
            dve.memset(taps_ab[64:65, :, 0, :], 1.0).then_inc(edges_set, 1)
            dve.wait_ge(h0_in, 32)
            dve.wait_ge(turned_out, 8)
            dve.wait_ge(edges_set, 1)
            for layer in range(2):
                at = slice(4 * layer, 4 * layer + 4)
                nc.vector.tensor_tensor(h0_taps[:, at].rearrange("p q (j i) -> p q j i", i=C),
                                        taps_ab[:, at, 0].rearrange("p q (j i) -> p q j i", i=C),
                                        h0s[:, layer].rearrange("p i (q j) -> p q j i", j=4), ALU.mult).then_inc(edges_set, 1)
            dve.wait_ge(edges_set, 3)
            for layer in range(2):
                at = slice(4 * layer, 4 * layer + 4)
                nc.vector.tensor_tensor(taps_ab[:, at, 1], taps_ab[:, at, 1], h0_taps[:, at], ALU.add).then_inc(taps_ready, 1)
            dve.wait_ge(respread_split, 1)
            split_low(nc.vector, respread[:, 1], respread_raw[:], respread[:, 0]).then_inc(respread_split, 1)

            def quotient(q, blk):
                n, f, s = q * NB + blk, len(BLOCKS[blk]), blk % 2
                dve.wait_ge(den_ready, n + 1)
                if not (isinstance(q, int) and n < 2):
                    dve.wait_ge(quot_ready, n - 1)
                nc.vector.tensor_tensor(straight[:, s, 0:f], ab[s][:, 0:f, :, 1], den[:, s, 0:f], ALU.mult)
                nc.vector.tensor_tensor(crossed[:, s, 0:f, 0], ab[s][:, 0:f, 1, 1], den[:, s, 0:f, 0], ALU.mult)
                nc.vector.tensor_tensor(crossed[:, s, 0:f, 1], ab[s][:, 0:f, 0, 1], den[:, s, 0:f, 1],
                                        ALU.mult).then_inc(prod_ready, 1)
                dve.wait_ge(mag_ready, n + 1)
                nc.vector.reciprocal(rec[:, s, 0:f], mag[:, s, 0:f]).then_inc(rec_ready, 1)

            def lags_rest(q, g):
                dve.wait_ge(lags_high, q * 16 + g + 1)
                split_low(nc.vector, lag_tile(1, g), mid[g % 2][:], lag_tile(0, g)).then_inc(lags_low, 1)

            def step(q):
                for blk in range(NB):
                    quotient(q + 1, blk)
                    for g in LAG_GROUPS[blk]:
                        lags_rest(q, g)

            for blk in range(NB):
                quotient(0, blk)
            step(0)
            with dve.Fori(1, QUARTERS - 1) as q:
                step(q)
            for g in range(16):
                lags_rest(QUARTERS - 1, g)

        @block.gpsimd
        def _(pool):
            def magnitude(q, blk):
                n, f, s = q * NB + blk, len(BLOCKS[blk]), blk % 2
                pool.wait_ge(den_ready, n + 1)
                if not (isinstance(q, int) and n < 2):
                    pool.wait_ge(rec_ready, n - 1)
                nc.gpsimd.tensor_tensor(mag[:, s, 0:f], sq[:, s, 0:f, 0], sq[:, s, 0:f, 1], ALU.add).then_inc(mag_ready, 1)

            def combine(q, k):
                magnitude(q, 0)
                for blk in range(NB):
                    n, f, s = q * NB + blk, len(BLOCKS[blk]), blk % 2
                    pool.wait_ge(prod_ready, n + 1)
                    if not (isinstance(q, int) and n < 2):
                        pool.wait_ge(quot_ready, n - 1)
                    nc.gpsimd.tensor_tensor(ratio[:, s, 0:f, 0], straight[:, s, 0:f, 0], straight[:, s, 0:f, 1], ALU.add)
                    nc.gpsimd.tensor_tensor(ratio[:, s, 0:f, 1], crossed[:, s, 0:f, 0], crossed[:, s, 0:f, 1],
                                            ALU.subtract).then_inc(num_ready, 1)
                    if blk + 1 < NB:
                        magnitude(q, blk + 1)
                    pool.wait_ge(num_ready, n + 1)
                    pool.wait_ge(rec_ready, n + 1)
                    if blk == 0 and not (isinstance(q, int) and q < 2):
                        pool.wait_ge(mid_ready, 16 * (q - 1))
                    for part in range(2):
                        out = nyq[:, part:part + 1] if blk == NB - 1 else \
                            spec[:, k, part, :, BLOCKS[blk][0]:BLOCKS[blk][-1] + 1].rearrange("p n f -> p f n")
                        op = nc.gpsimd.tensor_tensor(out, ratio[:, s, 0:f, part], rec[:, s, 0:f], ALU.mult)
                    op.then_inc(quot_ready, 1)
                pool.wait_ge(quot_ready, (q + 1) * NB)
                nc.gpsimd.tensor_tensor(spec[:, k, 0, :, 0], spec[:, k, 0, :, 0], nyq[:, 1], ALU.subtract)
                nc.gpsimd.tensor_tensor(spec[:, k, 1, :, 0], spec[:, k, 1, :, 0], nyq[:, 0], ALU.add).then_inc(spec_ready, 1)

            combine(0, 0)
            combine(1, 1)
            with pool.Fori(1, QUARTERS // 2) as p:
                combine(2 * p, 0)
                combine(2 * p + 1, 1)


ROW = L + 8


def spectrum(nc, image, source, scratch, const, tag):
    with ExitStack() as ctx:
        sb, ps, sem = allocators(nc, ctx, tag)
        ident = sb("ident", [128, 128])
        average = sb("average", [128, 128])
        fwd_w = sb("fwd_w", [L, 2, 128])
        eps = sb("eps", [128, 1])
        stats = sb("stats", [128, 32, 6])
        dev = sb("dev", [128, 32, 2])
        spread = sb("spread", [128, 32, 2])
        mean = sb("mean", [128, 32])
        var = sb("var", [128, 32])
        std = sb("std", [128, 32])
        rstd = sb("rstd", [128, 32])
        cols = sb("cols", [L, C, B, L])
        rows = sb("rows", [128, 4, B, ROW])
        turn = [ps(f"turn{k}", [128, 4, L]) for k in range(4)]
        freq = [ps(f"freq{k}", [128, B, L]) for k in range(2)]
        tot = ps("tot", [128, 64])

        image_in, consts_in, stats_ready, zeroed = sem("image_in"), sem("consts_in"), sem("stats_ready"), sem("zeroed")
        sum_ready, mean_ready, dev_ready, sq_ready = sem("sum_ready"), sem("mean_ready"), sem("dev_ready"), sem("sq_ready")
        spread_ready, var_ready, std_ready, rstd_ready = sem("spread_ready"), sem("var_ready"), sem("std_ready"), sem("rstd_ready")
        turn_ready, cols_ready, freq_ready, rows_ready = sem("turn_ready"), sem("cols_ready"), sem("freq_ready"), sem("rows_ready")
        stored = [sem(f"stored{k}") for k in range(4)]
        block = ctx.enter_context(nc.Block())

        @block.sync
        def _(sp):
            if source is not None:
                for b in range(B):
                    sp.dma_start(image[:, b], source[b]).then_inc(image_in, 16)
            sp.dma_start(ident[:], const["ident"]).then_inc(consts_in, 16)
            sp.dma_start(average[:], const["average"]).then_inc(consts_in, 16)
            sp.dma_start(fwd_w[:], const["fwd_w"]).then_inc(consts_in, 16)
            for u in range(2 * C):
                i, par = u // 2, u % 2
                sp.wait_ge(rows_ready, u + 1)
                for part in range(2):
                    sp.dma_start(scratch["spectrum"][i, par * FW:(par + 1) * FW, part],
                                 rows[part * FW:(part + 1) * FW, u % 4].rearrange("p b h -> p (b h)")).then_inc(stored[u % 4], 16)
            for k in range(4):
                sp.wait_ge(stored[k], 16 * 2 * (2 * C // 4))

        @block.vector
        def _(dve):
            dve.memset(eps[:], 1e-5)
            dve.memset(rows[:, :, :, 0:8], 0.0).then_inc(zeroed, 1)
            if source is not None:
                dve.wait_ge(image_in, 16 * B)
            for n in range(32):
                b, g = n // 8, n % 8
                op = nc.vector.bn_stats(stats[:, n], image[:, b, :, 2 * g:2 * g + 2])
            op.then_inc(stats_ready, 1)
            sample = stats[:].rearrange("p n (s k) -> p n s k", k=3)
            dve.wait_ge(sum_ready, 1)
            nc.vector.tensor_reduce(mean[:], tot[:].rearrange("p (n s) -> p n s", s=2), AX.X, ALU.add).then_inc(mean_ready, 1)
            dve.wait_ge(mean_ready, 1)
            nc.vector.tensor_tensor(dev[:], sample[:, :, :, 1], mean[:].unsqueeze(2).broadcast_to([128, 32, 2]),
                                    ALU.subtract).then_inc(dev_ready, 1)
            dve.wait_ge(dev_ready, 1)
            nc.vector.tensor_tensor(dev[:], dev[:], dev[:], ALU.mult).then_inc(sq_ready, 1)
            dve.wait_ge(sq_ready, 1)
            nc.vector.scalar_tensor_tensor(out=spread[:], in0=sample[:, :, :, 2], scalar=1.0 / 128, in1=dev[:],
                                           op0=ALU.mult, op1=ALU.add).then_inc(spread_ready, 1)
            dve.wait_ge(sum_ready, 2)
            nc.vector.tensor_reduce(var[:], tot[:].rearrange("p (n s) -> p n s", s=2), AX.X, ALU.add).then_inc(var_ready, 1)
            dve.wait_ge(std_ready, 1)
            nc.vector.reciprocal(rstd[:], std[:]).then_inc(rstd_ready, 1)
            dve.wait_ge(rstd_ready, 1)
            for i in range(C):
                dve.wait_ge(turn_ready, i + 1)
                for b in range(B):
                    n = 8 * b + i // 2
                    op = nc.vector.tensor_scalar(cols[:, i, b], turn[i % 4][:, b], mean[:, n:n + 1], rstd[:, n:n + 1],
                                                 ALU.subtract, ALU.mult)
                op.then_inc(cols_ready, 1)

        @block.scalar
        def _(act):
            act.wait_ge(var_ready, 1)
            act.wait_ge(zeroed, 1)
            nc.scalar.activation(std[:], var[:], ACT.Sqrt, bias=eps[:, 0:1]).then_inc(std_ready, 1)
            for u in range(2 * C):
                act.wait_ge(freq_ready, u + 1)
                if u >= 4:
                    act.wait_ge(stored[u % 4], 32 * (u // 4))
                nc.scalar.activation(rows[:, u % 4, :, 8:ROW], freq[u % 2][:], ACT.Copy).then_inc(rows_ready, 1)

        @block.tensor
        def _(pe):
            pe.wait_ge(consts_in, 48)
            pe.wait_ge(stats_ready, 1)
            nc.tensor.matmul(tot[:].rearrange("p (n s) -> p n s", s=2), average[:],
                             stats[:].rearrange("p n (s k) -> p n s k", k=3)[:, :, :, 1], start=True, stop=True).then_inc(sum_ready, 1)
            pe.wait_ge(mean_ready, 1)
            pe.wait_ge(spread_ready, 1)
            nc.tensor.matmul(tot[:], average[:], spread[:].rearrange("p n s -> p (n s)"), start=True, stop=True).then_inc(sum_ready, 1)

            def turn_channel(i):
                if i >= 4:
                    pe.wait_ge(cols_ready, i - 3)
                for b in range(B):
                    mm = nc.tensor.matmul(turn[i % 4][:, b], image[:, b, :, i], ident[:], start=True, stop=True)
                mm.then_inc(turn_ready, 1)

            for i in range(3):
                turn_channel(i)
            for i in range(C):
                pe.wait_ge(cols_ready, i + 1)
                for par in range(2):
                    u = 2 * i + par
                    if u >= 2:
                        pe.wait_ge(rows_ready, u - 1)
                    nc.tensor.matmul(freq[par][:], fwd_w[:, par], cols[:, i], start=True, stop=True).then_inc(freq_ready, 1)
                if i + 3 < C:
                    turn_channel(i + 3)


def convolve(nc, layer, scratch, tag):
    KB, RING = L // 8, 2
    with ExitStack() as ctx:
        sb, ps, sem = allocators(nc, ctx, tag)
        filt = sb("filt", [128, RING, 32, 4, KB])
        shifted = sb("shifted", [128, RING, 4, 2, B, L])
        out = sb("out", [128, RING, 2, B * L])
        acc = [[ps(f"acc{k}{cx}", [128, B, L]) for cx in range(2)] for k in range(RING)]
        filt_in = [sem(f"filt_in{k}") for k in range(RING)]
        rows_in = [sem(f"rows_in{k}") for k in range(RING)]
        group_done, acc_out = sem("group_done"), [[sem(f"acc_out{k}{cx}") for cx in range(2)] for k in range(RING)]
        stored = [sem(f"stored{k}") for k in range(RING)]
        block = ctx.enter_context(nc.Block())

        def load(eng, g, k):
            for jq in range(4):
                eng.dma_start(filt[:, k, 8 * jq:8 * jq + 8].rearrange("p (j m) s k -> p j (m s k)", j=2),
                              scratch["filters"][4 * layer + jq, :, :, g].rearrange("j p n -> p j n")).then_inc(filt_in[k], 16)
            for lag in range(8):
                eng.dma_start(shifted[C * lag:C * (lag + 1), k].rearrange("p s c b h -> p (s c b) h"),
                              scratch["spectrum"][:, bass.ds(4 * g, 4)].rearrange("i s c (b h) -> i (s c b) h", b=B)
                              [:, :, 8 - lag:8 - lag + L]).then_inc(rows_in[k], 16)

        @block.sync
        def _(sp):
            for k in range(RING):
                load(sp, k, k)
            with sp.Fori(1, GROUPS // RING) as n:
                for k in range(RING):
                    sp.wait_ge(group_done, RING * (n - 1) + k + 1)
                    load(sp, RING * n + k, k)

        @block.tensor
        def _(pe):
            with pe.Fori(0, GROUPS // RING) as n:
                for k in range(RING):
                    pe.wait_ge(filt_in[k], 16 * 4 * (n + 1))
                    pe.wait_ge(rows_in[k], 16 * 8 * (n + 1))
                    for cx in range(2):
                        pe.wait_ge(acc_out[k][cx], n + 1)
                        for kb in range(KB):
                            for s in range(4):
                                mm = nc.tensor.matmul(
                                    acc[k][cx][32 * s:32 * s + 32, :, 8 * kb:L],
                                    filt[:, k, :, s, kb],
                                    shifted[:, k, s, cx, :, 0:L - 8 * kb], start=kb == 0, stop=kb == KB - 1)
                    mm.then_inc(group_done, 1)

        def evacuate(eng, copy, cx, store):
            for k in range(RING):
                eng.sem_inc(acc_out[k][cx], 1)
            with eng.Fori(0, GROUPS // RING) as n:
                for k in range(RING):
                    eng.wait_ge(group_done, RING * n + k + 1)
                    eng.wait_ge(stored[k], 16 * (n + 1))
                    copy(out[:, k, cx], acc[k][cx][:].rearrange("p b h -> p (b h)")).then_inc(acc_out[k][cx], 1)
                    store(n, k)

        @block.vector
        def _(dve):
            evacuate(dve, nc.vector.tensor_copy, 0, lambda n, k: None)

        @block.scalar
        def _(act):
            def store(n, k):
                for cx in range(2):
                    act.wait_ge(acc_out[k][cx], n + 2)
                act.dma_start(scratch["products"][bass.ds(4 * (RING * n + k), 4)].rearrange("s j c n -> (s j c) n"),
                              out[:, k].rearrange("p x n -> p (x n)")).then_inc(stored[k], 16)

            for k in range(RING):
                act.sem_inc(stored[k], 16)
            evacuate(act, nc.scalar.copy, 1, store)
            for k in range(RING):
                act.wait_ge(stored[k], 16 * (GROUPS // RING + 1))


def back_to_image(nc, image, out_dram, scratch, const, tag):
    with ExitStack() as ctx:
        sb, ps, sem = allocators(nc, ctx, tag)
        inv_w = sb("inv_w", [128, 2, 2, L])
        prod = sb("prod", [128, 2, 2, 4, 2, B, L])
        img = [ps(f"img{k}", [128, B, L]) for k in range(4)]
        consts_in, done, added, out_stored = sem("consts_in"), sem("done"), sem("added"), sem("out_stored")
        prod_in = [sem(f"prod_in{k}") for k in range(2)]
        block = ctx.enter_context(nc.Block())

        @block.sync
        def _(sp):
            sp.dma_start(inv_w[:], const["inv_w"]).then_inc(consts_in, 16)
            for ch in range(4):
                if ch >= 2:
                    sp.wait_ge(done, 4 * (ch - 1))
                for par in range(2):
                    for c in range(2):
                        sp.dma_start(prod[FW * c:FW * (c + 1), ch % 2, par].rearrange("p j x b h -> p j (x b h)"),
                                     scratch["products"][FW * par:FW * (par + 1), 4 * ch:4 * ch + 4, c]).then_inc(prod_in[ch % 2], 16)
            if out_dram is not None:
                sp.wait_ge(added, C)
                for b in range(B):
                    sp.dma_start(out_dram[b], image[:, b]).then_inc(out_stored, 16)
                sp.wait_ge(out_stored, 16 * B)

        @block.tensor
        def _(pe):
            pe.wait_ge(consts_in, 16)
            for j in range(C):
                if j % 4 == 0:
                    pe.wait_ge(prod_in[j // 4 % 2], 16 * 4 * (j // 8 + 1))
                if j >= 4:
                    pe.wait_ge(added, j - 3)
                for b in range(B):
                    for t in range(4):
                        par, cx = t // 2, t % 2
                        mm = nc.tensor.matmul(img[j % 4][:, b], prod[:, j // 4 % 2, par, j % 4, cx, b], inv_w[:, par, cx],
                                              start=t == 0, stop=t == 3)
                mm.then_inc(done, 1)

        @block.vector
        def _(dve):
            for j in range(C):
                dve.wait_ge(done, j + 1)
                nc.vector.tensor_tensor(image[:, :, :, j], image[:, :, :, j], img[j % 4][:], ALU.add).then_inc(added, 1)


PATCHES = 1024
N = 512


def moments_tensors(sb, ps):
    return (sb("average", [128, 128]), sb("eps", [128, 1]), sb("stats", [128, B, 8, 6]), sb("dev", [128, B, 16]),
            sb("spread", [128, B, 16]), sb("var", [128, B]), sb("std", [128, B]), ps("tot", [128, B, 16]))


def to_patches(nc, image, mean, rstd, scratch, const, tag):
    with ExitStack() as ctx:
        sb, ps, sem = allocators(nc, ctx, tag)
        ident = sb("ident", [128, 128])
        xt = sb("xt", [128, 8, PATCHES])
        average, eps, stats, dev, spread, var, std, tot = moments_tensors(sb, ps)
        turn = [ps(f"turn{k}", [128, 4, L]) for k in range(4)]
        ident_in, average_in, turned, moved, stored = (sem(n) for n in ("ident_in", "average_in", "turned", "moved", "stored"))
        stats_ready, step, sum_ready, std_ready = sem("stats_ready"), sem("step"), sem("sum_ready"), sem("std_ready")
        sample = stats[:].rearrange("p b r (s k) -> p b (r s) k", k=3)
        block = ctx.enter_context(nc.Block())

        @block.sync
        def _(sp):
            sp.dma_start(ident[:], const["ident"]).then_inc(ident_in, 16)
            sp.dma_start(average[:], const["average_groups"]).then_inc(average_in, 16)
            for half in range(2):
                sp.wait_ge(moved, 8 * half + 8)
                sp.dma_start(scratch["patches"][half], xt[:, :, N * half:N * half + N]).then_inc(stored, 16)
            sp.wait_ge(stored, 32)

        @block.tensor
        def _(pe):
            pe.wait_ge(ident_in, 16)
            for t in range(16):
                if t >= 4:
                    pe.wait_ge(moved, t - 3)
                for k in range(4):
                    b, ww = (4 * t + k) // 16, (4 * t + k) % 16
                    mm = nc.tensor.matmul(turn[t % 4][:, k], image[:, b, 8 * ww:8 * ww + 8, :].rearrange("h s c -> h (s c)"),
                                          ident[:], start=True, stop=True)
                mm.then_inc(turned, 1)
            pe.wait_ge(average_in, 16)
            pe.wait_ge(stats_ready, 8 * B)
            nc.tensor.matmul(tot[:], average[:], sample[:, :, :, 1], start=True, stop=True).then_inc(sum_ready, 1)
            pe.wait_ge(step, 5)
            nc.tensor.matmul(tot[:], average[:], spread[:], start=True, stop=True).then_inc(sum_ready, 1)

        @block.scalar
        def _(act):
            for t in range(16):
                act.wait_ge(turned, t + 1)
                nc.scalar.activation(xt[:, :, 64 * t:64 * t + 64], turn[t % 4][:].rearrange("p k (h r) -> p r (k h)", r=8),
                                     ACT.Copy).then_inc(moved, 1)
            act.wait_ge(step, 6)
            nc.scalar.activation(std[:], var[:], ACT.Sqrt, bias=eps[:, 0:1]).then_inc(std_ready, 1)

        @block.vector
        def _(dve):
            dve.memset(eps[:], 1e-5).then_inc(step, 1)
            for b in range(B):
                dve.wait_ge(moved, 4 * b + 4)
                for r in range(8):
                    nc.vector.bn_stats(stats[:, b, r], xt[:, r, 256 * b:256 * b + 256]).then_inc(stats_ready, 1)
            dve.wait_ge(sum_ready, 1)
            nc.vector.tensor_reduce(mean[:], tot[:], AX.X, ALU.add).then_inc(step, 1)
            dve.wait_ge(step, 2)
            nc.vector.tensor_tensor(dev[:], sample[:, :, :, 1], mean[:].unsqueeze(2).broadcast_to([128, B, 16]),
                                    ALU.subtract).then_inc(step, 1)
            dve.wait_ge(step, 3)
            nc.vector.tensor_tensor(dev[:], dev[:], dev[:], ALU.mult).then_inc(step, 1)
            dve.wait_ge(step, 4)
            nc.vector.scalar_tensor_tensor(out=spread[:], in0=sample[:, :, :, 2], scalar=1.0 / 128, in1=dev[:],
                                           op0=ALU.mult, op1=ALU.add).then_inc(step, 1)
            dve.wait_ge(sum_ready, 2)
            nc.vector.tensor_reduce(var[:], tot[:], AX.X, ALU.add).then_inc(step, 1)
            dve.wait_ge(std_ready, 1)
            nc.vector.reciprocal(rstd[:], std[:]).then_inc(step, 1)
            dve.wait_ge(step, 7)


def normalise_padded(nc, xt, padded, scratch, const, tag):
    with ExitStack() as ctx:
        sb, ps, sem = allocators(nc, ctx, tag)
        average, eps, stats, dev, spread, var, std, tot = moments_tensors(sb, ps)
        mean, rstd = sb("mean", [128, B]), sb("rstd", [128, B])
        xt_in, average_in, stats_ready, step = sem("xt_in"), sem("average_in"), sem("stats_ready"), sem("step")
        sum_ready, std_ready, done, border = sem("sum_ready"), sem("std_ready"), sem("done"), sem("border")
        sample = stats[:].rearrange("p b r (s k) -> p b (r s) k", k=3)
        block = ctx.enter_context(nc.Block())

        @block.sync
        def _(sp):
            sp.dma_start(average[:], const["average_groups"]).then_inc(average_in, 16)
            for b in range(B):
                sp.dma_start(xt[:, :, 256 * b:256 * b + 256], scratch["patches"][b // 2][:, :, 256 * (b % 2):256 * (b % 2) + 256]
                             ).then_inc(xt_in, 16)
                sp.wait_ge(xt_in, 16 * b + 16)

        @block.gpsimd
        def _(pool):
            pool.memset(padded[:, :, 0:18:17, :], 0.0).then_inc(border, 1)
            pool.wait_ge(border, 1)
            pool.memset(padded[:, :, :, 0:L + 2:L + 1], 0.0).then_inc(border, 1)

        @block.tensor
        def _(pe):
            pe.wait_ge(average_in, 16)
            pe.wait_ge(stats_ready, 8 * B)
            nc.tensor.matmul(tot[:], average[:], sample[:, :, :, 1], start=True, stop=True).then_inc(sum_ready, 1)
            pe.wait_ge(step, 5)
            nc.tensor.matmul(tot[:], average[:], spread[:], start=True, stop=True).then_inc(sum_ready, 1)

        @block.scalar
        def _(act):
            act.wait_ge(step, 6)
            nc.scalar.activation(std[:], var[:], ACT.Sqrt, bias=eps[:, 0:1]).then_inc(std_ready, 1)

        @block.vector
        def _(dve):
            dve.memset(eps[:], 1e-5).then_inc(step, 1)
            for b in range(B):
                dve.wait_ge(xt_in, 16 * b + 16)
                for r in range(8):
                    nc.vector.bn_stats(stats[:, b, r], xt[:, r, 256 * b:256 * b + 256]).then_inc(stats_ready, 1)
            dve.wait_ge(sum_ready, 1)
            nc.vector.tensor_reduce(mean[:], tot[:], AX.X, ALU.add).then_inc(step, 1)
            dve.wait_ge(step, 2)
            nc.vector.tensor_tensor(dev[:], sample[:, :, :, 1], mean[:].unsqueeze(2).broadcast_to([128, B, 16]),
                                    ALU.subtract).then_inc(step, 1)
            dve.wait_ge(step, 3)
            nc.vector.tensor_tensor(dev[:], dev[:], dev[:], ALU.mult).then_inc(step, 1)
            dve.wait_ge(step, 4)
            nc.vector.scalar_tensor_tensor(out=spread[:], in0=sample[:, :, :, 2], scalar=1.0 / 128, in1=dev[:],
                                           op0=ALU.mult, op1=ALU.add).then_inc(step, 1)
            dve.wait_ge(sum_ready, 2)
            nc.vector.tensor_reduce(var[:], tot[:], AX.X, ALU.add).then_inc(step, 1)
            dve.wait_ge(std_ready, 1)
            nc.vector.reciprocal(rstd[:], std[:]).then_inc(step, 1)
            dve.wait_ge(step, 7)
            for b in range(B):
                nc.vector.tensor_scalar(padded[:, b, 1:17, 1:L + 1].rearrange("p w (h r) -> p r w h", r=8),
                                        xt[:, :, 256 * b:256 * b + 256].rearrange("p r (w h) -> p r w h", h=16),
                                        mean[:, b:b + 1], rstd[:, b:b + 1], ALU.subtract, ALU.mult).then_inc(done, 1)


def patch_correlate(nc, io, half, x, mean, rstd, store, sums, scratch, const, tag):
    with ExitStack() as ctx:
        sb, ps, sem = allocators(nc, ctx, tag)
        raw = [sb(f"raw_{n}", [128, 8, 512]) for n in "qk"]
        w = [sb(f"w_{n}", [128, 2, 8, 2, 128], R32) for n in "qk"]
        bias = [sb(f"bias_{n}", [128, 8, 4]) for n in "qk"]
        to_freq = [sb(f"to_freq_{n}", [128, 2, 128]) for n in "qk"]
        gather = sb("gather", [128, 64])
        src = [sb(f"src_{n}", [128, 2, N]) for n in "qk"]
        qf = sb("qf", [128, 2, 2, N])
        pf = sb("pf", [128, 2, 2, N])
        acc = [ps(f"acc_{n}", [128, N]) for n in "qk"]
        freq = [[ps(f"freq_{n}{d}", [128, N]) for d in range(2)] for n in "qk"]
        o_ps = ps("o_ps", [128, N])
        consts_in, bias_in, x_in, scaled, x_high, x_low = (sem(n) for n in (
            "consts_in", "bias_in", "x_in", "scaled", "x_high", "x_low"))
        raw_in, high, low, done, out = ([sem(f"{n}_{m}") for m in "qk"] for n in ("raw_in", "high", "low", "done", "out"))
        qf_done, qf_out, kf_done, pf_ready = sem("qf_done"), sem("qf_out"), sem("kf_done"), sem("pf_ready")
        o_done, o_out, sums_zero, summed = sem("o_done"), sem("o_out"), sem("sums_zero"), sem("summed")
        block = ctx.enter_context(nc.Block())
        w_dram = [io[n].rearrange("r s c (d n) -> d (s c) r n", d=8) for n in ("Wq", "Wk")]
        xs = raw[1]
        STEPS = 16

        @block.sync
        def _(sp):
            sp.dma_start(raw[1][:], scratch["patches"][half]).then_inc(x_in, 16)
            sp.dma_start(raw[0][:], w_dram[0][0]).then_inc(raw_in[0], 16)
            for n, name in enumerate(("bq", "bk")):
                for e in range(2):
                    sp.dma_start(bias[n][64 * e:64 * e + 64], io[name].rearrange("(d a p h) -> a p d h", d=8, a=2, h=4)[e]
                                 ).then_inc(bias_in, 16)
            sp.dma_start(to_freq[0][:], const["patch_q"]).then_inc(consts_in, 16)
            sp.dma_start(to_freq[1][:], const["patch_k"]).then_inc(consts_in, 16)
            sp.dma_start(gather[:], const["patch_back"]).then_inc(consts_in, 16)
            sp.wait_ge(x_low, 2)
            sp.dma_start(raw[1][:], w_dram[1][0]).then_inc(raw_in[1], 16)
            with sp.Fori(1, 8) as d:
                for n in range(2):
                    sp.wait_ge(low[n], 2 * d)
                    sp.dma_start(raw[n][:], w_dram[n][d]).then_inc(raw_in[n], 16)

        def slab(n, g):
            return raw[n][:].rearrange("p r (e h) -> p r h e", h=4)[:, :, 2 * g:2 * g + 2, :]

        @block.tensor
        def _(pe):
            def project(n, t, k):
                pe.wait_ge(out[n], 2 * t + k)
                if k == 0:
                    pe.wait_ge(low[n], t + 1)
                for r in range(8):
                    mm = split_product(pe, acc[n][:], [w[n][:, m, r, k] for m in range(2)], [x[:, m, r] for m in range(2)],
                                       r == 0, r == 7)
                mm.then_inc(done[n], 1)

            def transform(n, t, k):
                pe.wait_ge(out[n], 2 * t + k + 1)
                pe.wait_ge(pf_ready if n else qf_out, 2 * t + k)
                for d in range(2):
                    mm = pe.matmul(freq[n][d][:], to_freq[n][:, d], src[n][:, k], start=True, stop=True)
                mm.then_inc(kf_done if n else qf_done, 1)

            def back(t, k):
                pe.wait_ge(pf_ready, 2 * t + k + 1)
                pe.wait_ge(o_out, 2 * t + k)
                for d in range(2):
                    mm = pe.matmul(o_ps[64 * d:64 * d + 64], gather[:], pf[:, k, d], start=True, stop=True)
                mm.then_inc(o_done, 1)

            def step(t, first):
                project(0, t, 0)
                if not first:
                    transform(1, t - 1, 1)
                project(0, t, 1)
                if not first:
                    back(t - 1, 0)
                transform(0, t, 0)
                if not first:
                    back(t - 1, 1)
                project(1, t, 0)
                transform(0, t, 1)
                project(1, t, 1)
                transform(1, t, 0)

            pe.wait_ge(consts_in, 48)
            pe.wait_ge(x_low, 2)
            step(0, True)
            step(1, False)
            with pe.Fori(1, 8) as d:
                step(2 * d, False)
                step(2 * d + 1, False)
            transform(1, STEPS - 1, 1)
            back(STEPS - 1, 0)
            back(STEPS - 1, 1)

        @block.scalar
        def _(act):
            def split(n, t, g):
                act.wait_ge(raw_in[n], 16 * (t // 2 + 1))
                if t:
                    act.wait_ge(done[n], 2 * t)
                split_high(nc.scalar, w[n][:, 0], slab(n, g)).then_inc(high[n], 1)

            def evacuate(n, t, k):
                act.wait_ge(done[n], 2 * t + k + 1)
                if t:
                    if n:
                        act.wait_ge(kf_done, 2 * t + k - 1)
                    else:
                        act.wait_ge(qf_done, 2 * t + k - 1)
                at = 2 * (t % 2) + k
                nc.scalar.activation(src[n][:, k], acc[n][:], ACT.Identity, bias=bias[n][:, t // 2, at:at + 1]).then_inc(out[n], 1)

            def spectrum_out(t, k):
                act.wait_ge(qf_done, 2 * t + k + 1)
                if t:
                    act.wait_ge(pf_ready, 2 * t + k - 1)
                for d in range(2):
                    op = nc.scalar.activation(qf[:, k, d], freq[0][d][:], ACT.Copy)
                op.then_inc(qf_out, 1)

            split(0, 0, 0)
            for b in range(2):
                act.wait_ge(scaled, b + 1)
                split_high(nc.scalar, x[:, 0, :, 256 * b:256 * b + 256], xs[:, :, 256 * b:256 * b + 256]).then_inc(x_high, 1)
            act.wait_ge(bias_in, 64)
            split(1, 0, 0)
            for t in range(STEPS):
                evacuate(0, t, 0)
                evacuate(0, t, 1)
                spectrum_out(t, 0)
                if t + 1 < STEPS:
                    split(0, t + 1, (t + 1) % 2)
                evacuate(1, t, 0)
                spectrum_out(t, 1)
                evacuate(1, t, 1)
                if t + 1 < STEPS:
                    split(1, t + 1, (t + 1) % 2)

        @block.vector
        def _(dve):
            def split(n, t, g):
                dve.wait_ge(high[n], t + 1)
                split_low(nc.vector, w[n][:, 1], slab(n, g), w[n][:, 0]).then_inc(low[n], 1)

            def product(t, k):
                dve.wait_ge(kf_done, 2 * t + k + 1)
                dve.wait_ge(qf_out, 2 * t + k + 1)
                for d in range(2):
                    op = nc.vector.tensor_tensor(pf[:, k, d], freq[1][d][:], qf[:, k, d], ALU.mult)
                op.then_inc(pf_ready, 1)

            def pixels_out(t, k, d, g):
                dve.wait_ge(o_done, 2 * t + k + 1)
                flat = store[:].rearrange("p h d n -> p (h d n)")
                at = dve.snap(d * N + (2 * g + k) * 8 * N)
                nc.vector.tensor_copy(flat[:, bass.ds(at, N)], o_ps[:]).then_inc(o_out, 1)

            def step(t, d, g, first, last):
                if not first:
                    product(t - 1, 1)
                    pixels_out(t - 1, 0, d - 1 if g == 0 else d, 1 - g)
                    pixels_out(t - 1, 1, d - 1 if g == 0 else d, 1 - g)
                if not last:
                    split(0, t + 1, 1 - g)
                product(t, 0)
                if not last:
                    split(1, t + 1, 1 - g)

            dve.memset(sums[:], 0.0).then_inc(sums_zero, 1)
            dve.wait_ge(x_in, 16)
            for b in range(2):
                at = slice(256 * b, 256 * b + 256)
                n = 2 * half + b
                nc.vector.tensor_scalar(xs[:, :, at], xs[:, :, at], mean[:, n:n + 1], rstd[:, n:n + 1],
                                        ALU.subtract, ALU.mult).then_inc(scaled, 1)
            for b in range(2):
                at = slice(256 * b, 256 * b + 256)
                dve.wait_ge(x_high, b + 1)
                split_low(nc.vector, x[:, 1, :, at], xs[:, :, at], x[:, 0, :, at]).then_inc(x_low, 1)
            split(0, 0, 0)
            split(1, 0, 0)
            step(0, 0, 0, True, False)
            step(1, 0, 1, False, False)
            with dve.Fori(1, 7) as d:
                step(2 * d, d, 0, False, False)
                step(2 * d + 1, d, 1, False, False)
            step(14, 7, 0, False, False)
            step(15, 7, 1, False, True)
            product(15, 1)
            pixels_out(15, 0, 7, 1)
            pixels_out(15, 1, 7, 1)

        @block.gpsimd
        def _(pool):
            pool.wait_ge(sums_zero, 1)
            pool.sem_inc(summed, 1)
            with pool.Fori(0, 8) as d:
                for head in range(4):
                    t = 4 * d + head
                    pool.wait_ge(o_out, t + 1)
                    pool.wait_ge(summed, t + 1)
                    flat = store[:].rearrange("p h d n -> p (h d n)")
                    at = pool.snap(d * N + head * 8 * N)
                    nc.gpsimd.tensor_tensor(sums[:, head], sums[:, head], flat[:, bass.ds(at, N)], ALU.add).then_inc(summed, 1)


def patch_norm(nc, store, sums, rstd, const, tag):
    with ExitStack() as ctx:
        sb, ps, sem = allocators(nc, ctx, tag)
        over_dims = sb("over_dims", [128, 128])
        eps = sb("eps", [128, 1])
        square = sb("square", [128, 2, 2, N])
        std = sb("std", [128, 4, N])
        mean_ps = [ps(f"mean_ps{h}", [128, N]) for h in range(4)]
        var_ps = [ps(f"var_ps{h}", [128, N]) for h in range(4)]
        const_in, eps_set, mean_ready, centred = sem("const_in"), sem("eps_set"), sem("mean_ready"), sem("centred")
        squared, summed, std_ready, done = sem("squared"), sem("summed"), sem("std_ready"), sem("done")
        block = ctx.enter_context(nc.Block())
        TILES = [(h, d) for h in range(4) for d in range(0, 8, 2)]

        @block.sync
        def _(sp):
            sp.dma_start(over_dims[:], const["over_dims"]).then_inc(const_in, 16)

        @block.tensor
        def _(pe):
            pe.wait_ge(const_in, 16)
            for h in range(4):
                pe.matmul(mean_ps[h][:], over_dims[:], sums[:, h], start=True, stop=True).then_inc(mean_ready, 1)
            for t, (h, d) in enumerate(TILES):
                pe.wait_ge(squared, t + 1)
                for e in range(2):
                    mm = pe.matmul(var_ps[h][:], over_dims[:], square[:, t % 2, e], start=d + e == 0, stop=d + e == 7)
                mm.then_inc(summed, 1)

        @block.vector
        def _(dve):
            dve.memset(eps[:], 1e-6).then_inc(eps_set, 1)

            def inverse(h):
                dve.wait_ge(std_ready, h + 1)
                nc.vector.reciprocal(rstd[:, h], std[:, h]).then_inc(done, 1)

            for t, (h, d) in enumerate(TILES):
                dve.wait_ge(mean_ready, h + 1)
                nc.vector.tensor_tensor(store[:, h, d:d + 2], store[:, h, d:d + 2],
                                        mean_ps[h][:].unsqueeze(1).broadcast_to([128, 2, N]), ALU.subtract).then_inc(centred, 1)
                if d == 4 and h:
                    inverse(h - 1)
            inverse(3)

        @block.scalar
        def _(act):
            act.wait_ge(eps_set, 1)

            def root(h):
                act.wait_ge(summed, 4 * h + 4)
                nc.scalar.activation(std[:, h], var_ps[h][:], ACT.Sqrt, bias=eps[:, 0:1]).then_inc(std_ready, 1)

            for t, (h, d) in enumerate(TILES):
                act.wait_ge(centred, t + 1)
                if t >= 2:
                    act.wait_ge(summed, t - 1)
                nc.scalar.activation(square[:, t % 2], store[:, h, d:d + 2], ACT.Square).then_inc(squared, 1)
                if d == 2 and h:
                    root(h - 1)
            root(3)


def patch_values(nc, io, x, store, rstd, const, tag):
    with ExitStack() as ctx:
        sb, ps, sem = allocators(nc, ctx, tag)
        raw = sb("raw", [128, 2, 8, 512])
        w = sb("w", [128, 2, 2, 8, 2, 128], R32)
        bv = sb("bv", [128, 8, 4])
        scale_shift = sb("scale_shift", [128, 8, 2])
        normed = sb("normed", [128, 2, N])
        affine = sb("affine", [128, 2, N])
        v_ps = [ps(f"v_ps{k}", [128, N]) for k in range(4)]
        vec_in, v_done, normed_ready, affine_ready, used = (sem(n) for n in (
            "vec_in", "v_done", "normed_ready", "affine_ready", "used"))
        raw_in, high, low = [sem(f"raw_in{k}") for k in range(2)], sem("high"), sem("low")
        block = ctx.enter_context(nc.Block())
        w_dram = io["Wv"].rearrange("r s c (d n) -> d (s c) r n", d=8)
        STEPS = 16

        @block.sync
        def _(sp):
            for k in range(2):
                sp.dma_start(raw[:, k], w_dram[k]).then_inc(raw_in[k], 16)
            for e in range(2):
                at = slice(64 * e, 64 * e + 64)
                sp.dma_start(bv[at], io["bv"].rearrange("(d a p h) -> a p d h", d=8, a=2, h=4)[e]).then_inc(vec_in, 16)
                for k, name in enumerate(("ln_scale", "ln_bias")):
                    with nc.allow_non_contiguous_dma(reason="16 values"):
                        sp.dma_start(scale_shift[at, :, k], io[name].rearrange("(o d a) -> a o d", o=1, a=2)[e].broadcast_to([64, 8])
                                     ).then_inc(vec_in, 16)
            with sp.Fori(1, 4) as n:
                for k in range(2):
                    sp.wait_ge(low, 4 * n + 2 * k - 2)
                    sp.dma_start(raw[:, k], w_dram[2 * n + k]).then_inc(raw_in[k], 16)

        def slab(t):
            return raw[:, t // 2 % 2].rearrange("p r (e h) -> p r h e", h=4)[:, :, 2 * (t % 2):2 * (t % 2) + 2, :]

        @block.tensor
        def _(pe):
            with pe.Fori(0, 8) as d:
                for g in range(2):
                    pe.wait_ge(low, 2 * d + g + 1)
                    for k in range(2):
                        pe.wait_ge(used, 4 * d + 2 * g + k + 1)
                        for r in range(8):
                            mm = split_product(pe, v_ps[2 * g + k][:], [w[:, g, m, r, k] for m in range(2)],
                                               [x[:, m, r] for m in range(2)], r == 0, r == 7)
                        mm.then_inc(v_done, 1)

        @block.gpsimd
        def _(pool):
            for t in range(4 * 8):
                d, head = t // 4, t % 4
                if t >= 2:
                    pool.wait_ge(affine_ready, t - 1)
                nc.gpsimd.tensor_tensor(normed[:, t % 2], store[:, head, d], rstd[:, head], ALU.mult).then_inc(normed_ready, 1)

        @block.scalar
        def _(act):
            def split(t):
                act.wait_ge(raw_in[t // 2 % 2], 16 * (t // 4 + 1))
                if t >= 2:
                    act.wait_ge(v_done, 2 * t - 2)
                split_high(nc.scalar, w[:, t % 2, 0], slab(t)).then_inc(high, 1)

            split(0)
            split(1)
            act.wait_ge(vec_in, 16 * 6)
            for t in range(32):
                d = t // 4
                act.wait_ge(normed_ready, t + 1)
                if t >= 2:
                    act.wait_ge(used, t - 1 + 4)
                nc.scalar.activation(affine[:, t % 2], normed[:, t % 2], ACT.Identity, scale=scale_shift[:, d, 0:1],
                                     bias=scale_shift[:, d, 1:2]).then_inc(affine_ready, 1)
                if t % 2 and t // 2 + 2 < STEPS:
                    split(t // 2 + 2)

        @block.vector
        def _(dve):
            def split(t):
                dve.wait_ge(high, t + 1)
                split_low(nc.vector, w[:, t % 2, 1], slab(t), w[:, t % 2, 0]).then_inc(low, 1)

            dve.sem_inc(used, 4)
            split(0)
            split(1)
            dve.wait_ge(vec_in, 16 * 6)
            for t in range(32):
                d, head = t // 4, t % 4
                dve.wait_ge(v_done, t + 1)
                dve.wait_ge(affine_ready, t + 1)
                nc.vector.scalar_tensor_tensor(out=store[:, head, d], in0=v_ps[head][:], scalar=bv[:, d, head:head + 1],
                                               in1=affine[:, t % 2], op0=ALU.add, op1=ALU.mult).then_inc(used, 1)
                if t % 2 and t // 2 + 2 < STEPS:
                    split(t // 2 + 2)


def patch_project(nc, io, half, store, scratch, const, tag):
    with ExitStack() as ctx:
        sb, ps, sem = allocators(nc, ctx, tag)
        raw = sb("raw", [128, 2, 8 * 128])
        w = sb("w", [128, 2, 2, 8, 8, C], R32)
        u = sb("u", [128, 2, 2, N], R32)
        xt = sb("xt", [128, 8, N])
        bout = sb("bout", [128, 8])
        acc = [ps(f"acc{r}", [128, N]) for r in range(8)]
        bias_in, xt_in, low, done, acc_done, summed, stored = (sem(n) for n in (
            "bias_in", "xt_in", "low", "done", "acc_done", "summed", "stored"))
        raw_in = [sem(f"raw_in{k}") for k in range(2)]
        high = sem("high")
        block = ctx.enter_context(nc.Block())
        w_dram = io["Wout"].rearrange("a b (h d e) n -> h d e (a b) n", h=4, e=2)
        TILES = [(d, h) for d in range(8) for h in range(4)]

        @block.sync
        def _(sp):
            def load(d, h):
                for e in range(2):
                    sp.dma_start(raw[64 * e:64 * e + 64, h % 2], w_dram[h, d, e]).then_inc(raw_in[h % 2], 16)

            load(0, 0)
            load(0, 1)
            for h in range(2, 4):
                sp.wait_ge(low, h - 1)
                load(0, h)
            sp.dma_start(xt[:], scratch["patches"][half]).then_inc(xt_in, 16)
            with nc.allow_non_contiguous_dma(reason="the bias, once"):
                for s in range(8):
                    sp.dma_start(bout[C * s:C * s + C], io["bout"].rearrange("(c r s) -> s c r", r=8, s=8)[s]).then_inc(bias_in, 16)
            with sp.Fori(1, 8) as d:
                for h in range(4):
                    sp.wait_ge(low, 4 * d + h - 1)
                    load(d, h)
            for r in range(8):
                sp.wait_ge(summed, r + 1)
                sp.dma_start(scratch["patches"][half][:, r], xt[:, r]).then_inc(stored, 16)
            sp.wait_ge(stored, 16 * 8)

        @block.scalar
        def _(act):
            for t, (d, h) in enumerate(TILES):
                k = t % 2
                act.wait_ge(raw_in[k], 32 * (t // 2 + 1))
                if t >= 2:
                    act.wait_ge(done, t - 1)
                split_high(nc.scalar, w[:, k, 0], raw[:, k].rearrange("p (c r s) -> p r s c", r=8, s=8))
                split_high(nc.scalar, u[:, k, 0], store[:, h, d]).then_inc(high, 1)

        @block.vector
        def _(dve):
            for t, (d, h) in enumerate(TILES):
                k = t % 2
                dve.wait_ge(high, t + 1)
                split_low(nc.vector, w[:, k, 1], raw[:, k].rearrange("p (c r s) -> p r s c", r=8, s=8), w[:, k, 0])
                split_low(nc.vector, u[:, k, 1], store[:, h, d], u[:, k, 0]).then_inc(low, 1)
            dve.wait_ge(bias_in, 16 * 8)
            dve.wait_ge(xt_in, 16)
            for r in range(8):
                dve.wait_ge(acc_done, r + 1)
                nc.vector.scalar_tensor_tensor(out=xt[:, r], in0=acc[r][:], scalar=bout[:, r:r + 1], in1=xt[:, r],
                                               op0=ALU.add, op1=ALU.add).then_inc(summed, 1)

        @block.tensor
        def _(pe):
            def tile(t, k, first, last):
                pe.wait_ge(low, t + 1)
                for r in range(8):
                    mm = split_product(pe, acc[r][:], [w[:, k, m, r].rearrange("p s c -> p (s c)") for m in range(2)],
                                       [u[:, k, m] for m in range(2)], first, last)
                    if last:
                        mm.then_inc(acc_done, 1)
                if not last:
                    mm.then_inc(done, 1)

            tile(0, 0, True, False)
            tile(1, 1, False, False)
            with pe.Fori(1, 15) as n:
                for k in range(2):
                    tile(2 * n + k, k, False, False)
            tile(30, 0, False, False)
            tile(31, 1, False, True)


def local_conv(nc, io, xt, padded, image, const, tag):
    with ExitStack() as ctx:
        sb, ps, sem = allocators(nc, ctx, tag)
        ident = sb("ident", [128, 128])
        band = sb("band", [128, 3, 128])
        cross = sb("cross", [96, 128])
        bias = sb("bias", [128, 1])
        edge = sb("edge", [96, B, 16, L])
        res = sb("res", [128, 3, 4, L])
        acc = [ps(f"acc{k}", [128, 4, L]) for k in range(3)]
        turn = [ps(f"turn{k}", [128, 4, 128]) for k in range(3)]
        zeroed, w_in, edge_in, ident_in, bias_in = sem("zeroed"), sem("w_in"), sem("edge_in"), sem("ident_in"), sem("bias_in")
        acc_done, res_ready, turned, moved = sem("acc_done"), sem("res_ready"), sem("turned"), sem("moved")
        block = ctx.enter_context(nc.Block())

        @block.sync
        def _(sp):
            for dy in range(3):
                for side in range(2):
                    rows = padded[16 * 7:128] if side == 0 else padded[0:16]
                    for b in range(B):
                        sp.dma_start(edge[32 * dy + 16 * side:32 * dy + 16 * side + 16, b],
                                     rows[:, b, 2 * side:2 * side + 16, dy:dy + L]).then_inc(edge_in, 16)

        @block.scalar
        def _(act):
            act.wait_ge(zeroed, 1)
            for s in range(8):
                for dx in range(3):
                    at = s + dx - 1
                    if 0 <= at < 8:
                        act.dma_start(band[C * at:C * at + C, :, C * s:C * s + C],
                                      io["filters3"][:, dx].rearrange("y i j -> i y j")).then_inc(w_in, 16)
            for dy in range(3):
                act.dma_start(cross[32 * dy:32 * dy + 16, 0:C], io["filters3"][dy, 0]).then_inc(w_in, 16)
                act.dma_start(cross[32 * dy + 16:32 * dy + 32, 7 * C:8 * C], io["filters3"][dy, 2]).then_inc(w_in, 16)
            act.dma_start(ident[:], const["ident"]).then_inc(ident_in, 16)
            for s in range(8):
                act.dma_start(bias[C * s:C * s + C, :], io["bias3"].rearrange("(c o) -> c o", o=1)).then_inc(bias_in, 16)
            for t in range(16):
                b, w4 = t // 4, t % 4
                act.wait_ge(turned, t + 1)
                nc.scalar.activation(image[:, b, 32 * w4:32 * w4 + 32, :].rearrange("h w c -> h (w c)"),
                                     turn[t % 3][:].rearrange("h a n -> h (a n)"), ACT.Copy).then_inc(moved, 1)

        @block.tensor
        def _(pe):
            pe.wait_ge(w_in, 16 * 28)
            pe.wait_ge(ident_in, 16)

            def turn_tile(t):
                pe.wait_ge(res_ready, t + 1)
                if t >= 3:
                    pe.wait_ge(moved, t - 2)
                for k in range(4):
                    mm = nc.tensor.matmul(turn[t % 3][:, k], res[:, t % 3, k], ident[:], start=True, stop=True)
                mm.then_inc(turned, 1)

            for t in range(16):
                b, w4 = t // 4, t % 4
                if t >= 3:
                    pe.wait_ge(res_ready, t - 2)
                for dy in range(3):
                    nc.tensor.matmul(acc[t % 3][:], band[:, dy], padded[:, b, 4 * w4 + 1:4 * w4 + 5, dy:dy + L],
                                     start=dy == 0, stop=False)
                if t == 0:
                    pe.wait_ge(edge_in, 16 * 6 * B)
                nc.tensor.matmul(acc[t % 3][:], cross[:], edge[:, b, 4 * w4:4 * w4 + 4], start=False, stop=True).then_inc(acc_done, 1)
                if t >= 1:
                    turn_tile(t - 1)
            turn_tile(15)

        @block.vector
        def _(dve):
            dve.memset(band[:], 0.0)
            dve.memset(cross[:], 0.0).then_inc(zeroed, 1)
            dve.wait_ge(bias_in, 16 * 8)
            for t in range(16):
                dve.wait_ge(acc_done, t + 1)
                if t >= 3:
                    dve.wait_ge(turned, t - 2)
                nc.vector.scalar_tensor_tensor(
                    out=res[:, t % 3].rearrange("p w (h r) -> p (w h) r", r=8), in0=acc[t % 3][:].rearrange("p w (h r) -> p (w h) r", r=8),
                    scalar=bias[:, 0:1], in1=xt[:, :, 64 * t:64 * t + 64].rearrange("p r n -> p n r"),
                    op0=ALU.add, op1=ALU.add).then_inc(res_ready, 1)


def build(nc, io, const, out):
    scratch = {
        "filters": nc.dram_tensor("filters_dram", (8, 2, 128, GROUPS, 256), F32, kind="Internal").ap(),
        "spectrum": nc.dram_tensor("spectrum_dram", (C, L, 2, B * ROW), F32, kind="Internal").ap(),
        "products": nc.dram_tensor("products_dram", (L, C, 2, 2 * B * L), F32, kind="Internal").ap(),
        "patches": nc.dram_tensor("patches_dram", (2, 128, 8, N), F32, kind="Internal").ap(),
    }
    build_filters(nc, io, scratch, const)
    with nc.sbuf_tensor("mean1", [128, B], F32) as mean, nc.sbuf_tensor("rstd1", [128, B], F32) as rstd:
        with nc.sbuf_tensor("image0", [128, B, L, C], F32) as image:
            spectrum(nc, image, io["x"], scratch, const, "s0_")
            convolve(nc, 0, scratch, "c0_")
            back_to_image(nc, image, None, scratch, const, "b0_")
            to_patches(nc, image, mean, rstd, scratch, const, "tp_")
        for half in range(2):
            patch_mixer(nc, io, half, mean, rstd, scratch, const)
    with nc.sbuf_tensor("image1", [128, B, L, C], F32) as image:
        with nc.sbuf_tensor("xt", [128, 8, PATCHES], F32) as xt, nc.sbuf_tensor("padded", [128, B, 18, L + 2], F32) as padded:
            normalise_padded(nc, xt, padded, scratch, const, "n2_")
            local_conv(nc, io, xt, padded, image, const, "l_")
        spectrum(nc, image, None, scratch, const, "s3_")
        convolve(nc, 1, scratch, "c3_")
        back_to_image(nc, image, out, scratch, const, "b3_")


def patch_mixer(nc, io, half, mean, rstd, scratch, const):
    with nc.sbuf_tensor(f"xn{half}", [128, 2, 8, N], R32) as x, nc.sbuf_tensor(f"store{half}", [128, 4, 8, N], F32) as store:
        with nc.sbuf_tensor(f"sums{half}", [128, 4, N], F32) as sums:
            patch_correlate(nc, io, half, x, mean, rstd, store, sums, scratch, const, f"q{half}_")
            with nc.sbuf_tensor(f"rstds{half}", [128, 4, N], F32) as rstds:
                patch_norm(nc, store, sums, rstds, const, f"ln{half}_")
                patch_values(nc, io, x, store, rstds, const, f"v{half}_")
        patch_project(nc, io, half, store, scratch, const, f"o{half}_")


INPUTS = {
    "x": "x", "L0_conv_h0": "h00", "L0_conv_numerators": "num0", "L0_conv_denumerator": "den0",
    "L1_conv_Wq": "Wq", "L1_conv_bq": "bq", "L1_conv_Wk": "Wk", "L1_conv_bk": "bk", "L1_conv_Wv": "Wv", "L1_conv_bv": "bv",
    "L1_conv_ln_scale": "ln_scale", "L1_conv_ln_bias": "ln_bias", "L1_conv_Wout": "Wout", "L1_conv_bout": "bout",
    "L2_conv_filters": "filters3", "L2_conv_bias": "bias3",
    "L3_conv_h0": "h01", "L3_conv_numerators": "num1", "L3_conv_denumerator": "den1",
}


def kernel(**inputs):
    import numpy as _np
    import concourse.bacc as _bacc
    from concourse import mybir as _mybir
    from concourse.bass_utils import run_bass_kernel_spmd as _run

    nc = _bacc.Bacc("TRN2", target_bir_lowering=False, num_devices=1)
    arrays, io, const = {}, {}, {}
    for name, short in INPUTS.items():
        a = _np.ascontiguousarray(inputs[name])
        arrays[f"in_{name}"] = a
        io[short] = nc.dram_tensor(f"in_{name}", a.shape, _mybir.dt.from_np(a.dtype), kind="ExternalInput").ap()
    for layer in range(2):
        io[f"num{layer}"] = io[f"num{layer}"][0]
    for name, table in {**dft_tables(), **patch_tables()}.items():
        a = _np.ascontiguousarray(table.astype(_np.float32))
        arrays[f"const_{name}"] = a
        const[name] = nc.dram_tensor(f"const_{name}", a.shape, _mybir.dt.float32, kind="ExternalInput").ap()
    out = nc.dram_tensor("out_dram", (4, 128, 128, 16), _mybir.dt.float32, kind="ExternalOutput").ap()
    build(nc, io, const, out)
    r = _run(nc, [arrays], core_ids=[0])
    return r.results[0]["out_dram"]
```

```python
from contextlib import ExitStack
import numpy as np
import concourse.bass as bass
from concourse import mybir
ALU = mybir.AluOpType
ACT = mybir.ActivationFunctionType
AX = mybir.AxisListType
F32 = mybir.dt.float32

def allocators(nc, ctx, prefix):
    sems = []

    def clear():
        nc.clear_and_free_semaphores(sems)
        nc.all_engine_barrier()

    ctx.callback(clear)

    def sb(name, shape, dt=F32):
        return ctx.enter_context(nc.sbuf_tensor(prefix + name, shape, dt))

    def ps(name, shape):
        return ctx.enter_context(nc.psum_tensor(prefix + name, shape, F32))

    def sem(name):
        sems.append(nc.alloc_semaphore(name=prefix + name))
        return sems[-1]

    return sb, ps, sem

L, FW, B, C = 128, 64, 4, 16


def dft_tables():
    f64 = np.float64
    n = np.arange(L, dtype=f64)
    tau = 2 * np.pi
    p = np.repeat(np.arange(1, 9), 8).astype(f64)
    q = np.tile(np.arange(1, 9), 8).astype(f64)
    edge = [(a, b) for a in range(9) for b in range(9) if a == 0 or b == 0]
    taps = np.zeros((65, FW + 1, 2, L))
    for fw in range(FW + 1):
        ang = tau * (np.outer(p, n) + (q * fw)[:, None]) / L
        taps[:64, fw, 0], taps[:64, fw, 1] = np.cos(ang), -np.sin(ang)
        e = sum(np.exp(-1j * tau * (n * a + fw * b) / L) for a, b in edge)
        taps[64, fw, 0], taps[64, fw, 1] = e.real, e.imag
    ang = tau * np.outer(n, n) / L
    inv_h = np.stack([np.cos(ang), np.sin(ang), -np.sin(ang)], 1) / L
    s = np.arange(FW, dtype=f64)
    fwd = np.zeros((2, L, 2, FW))
    fwd[0, :, 0], fwd[0, :, 1] = np.cos(tau * np.outer(n, s) / L), -np.sin(tau * np.outer(n, s) / L)
    fwd[0, :, 1, 0] = (-1.0) ** n
    odd = tau * np.outer(n, 2 * s + 1) / (2 * L)
    fwd[1, :, 0], fwd[1, :, 1] = np.cos(odd), -np.sin(odd)
    back = np.zeros((2, FW, L))
    back[0], back[1] = 2 * np.cos(tau * np.outer(s, n) / L) / L, -2 * np.sin(tau * np.outer(s, n) / L) / L
    back[0, 0], back[1, 0] = 1.0 / L, (-1.0) ** n / L
    back = back.reshape(L, L)
    respread = np.zeros((L, 2, FW, 2))
    for c in range(2):
        for k in range(FW):
            respread[c * FW + k, 0, k, c] = 1.0
    respread[:, 1] = (back @ fwd[1].reshape(L, 2 * FW)).reshape(L, 2, FW).transpose(0, 2, 1)
    respread = respread.reshape(L, L // 4, 4, 2).transpose(0, 1, 3, 2)
    inv = np.zeros((2, FW, 2, 2, L))
    for par in range(2):
        a = tau * np.outer(2 * s + par, n) / (2 * L)
        co, si = np.cos(a) / L, np.sin(a) / L
        inv[0, :, par, 0], inv[1, :, par, 0] = co, -si
        inv[0, :, par, 1], inv[1, :, par, 1] = -si, -co
    inv[:, 0, 0] = 0.0
    inv[0, 0, 0, 0] = 0.5 / L
    inv[1, 0, 0, 1] = 0.5 * (-1.0) ** n / L
    return {
        "taps": taps.reshape(65, -1), "inv_h": inv_h.reshape(L, -1),
        "fwd_w": fwd.reshape(2, L, L).transpose(1, 0, 2).reshape(L, -1),
        "respread": respread.reshape(L, -1), "inv_w": inv.reshape(L, -1),
    }


def patch_tables():
    f64 = np.float64
    u, v = np.repeat(np.arange(8), 8), np.tile(np.arange(8), 8)
    real = [(a, b) for a in (0, 4) for b in (0, 4)]
    pairs = [(a, b) for a in range(8) for b in range(8) if (a, b) not in real and (a, b) < ((-a) % 8, (-b) % 8)]
    ang = lambda fs: 2 * np.pi * np.array([[(a * x + b * y) / 8 for a, b in fs] for x, y in zip(u, v)], dtype=f64)
    cx, rl = ang(pairs), ang(real)
    re, im = np.cos(cx), -np.sin(cx)
    q = np.concatenate([re, im, re, im, np.cos(rl), np.zeros((64, 4))], 1)
    k = np.concatenate([re, im, im, re, np.cos(rl), np.zeros((64, 4))], 1)
    co, si = 2 * np.cos(cx).T / 64, -2 * np.sin(cx).T / 64
    back = np.concatenate([co, -co, si, si, np.cos(rl).T / 64, np.zeros((4, 64))])
    two = np.zeros((2, 2, 128, 2, 128))
    for n, m in enumerate((q, k)):
        for d in range(2):
            two[n, 0, 64 * d:64 * d + 64, d] = m
    pix, grp = np.arange(128) % 64, np.arange(128) % 16 // 2
    return {
        "patch_q": two[0, 0].reshape(128, 256), "patch_k": two[1, 0].reshape(128, 256), "patch_back": back,
        "over_dims": (pix[:, None] == pix) / 16.0, "average_groups": (grp[:, None] == grp) / 256.0,
        "average": np.full((128, 128), 1 / 256), "ident": np.eye(128),
    }


R32 = mybir.dt.float32r
GROUPS = L // 4


def split_high(eng, out, src):
    return eng.activation(out, src, ACT.Copy)


def split_low(eng, out, src, high):
    return eng.tensor_tensor(out, src, high.bitcast(F32), ALU.subtract)


def split_product(pe, out, w, x, first, last):
    pe.matmul(out, w[0], x[0], start=first, stop=False)
    pe.matmul(out, w[0], x[1], start=False, stop=False)
    return pe.matmul(out, w[1], x[0], start=False, stop=last)


def build_filters(nc, io, scratch, const):
    QUARTERS, PAIRS = 8, 64
    BLOCKS = [list(range(4 * n, 4 * n + 4)) for n in range(15)] + [[60, 61], [62, 63], [FW]]
    NB = len(BLOCKS)
    KB, PIECES = L // 8, 8
    with ExitStack() as ctx:
        sb, ps, sem = allocators(nc, ctx, "f_")
        raw = sb("raw", [128, 8, 64])
        ident = sb("ident", [128, 128])
        taps_ab = sb("taps_ab", [65, QUARTERS, 2, PAIRS])
        table = sb("table", [65, 2, 4, 2, L])
        inv_h = sb("inv_h", [L, 3, L])
        respread_raw = sb("respread_raw", [L, 2 * 128])
        respread = sb("respread", [L, 2, 2 * 128], R32)
        h0s = sb("h0s", [65, 2, C, C])
        h0_taps = sb("h0_taps", [65, QUARTERS, PAIRS])
        den = sb("den", [128, 2, 4, 2, PAIRS])
        sq = sb("sq", [128, 2, 4, 2, PAIRS])
        mag = sb("mag", [128, 2, 4, PAIRS])
        rec = sb("rec", [128, 2, 4, PAIRS])
        straight = sb("straight", [128, 2, 4, 2, PAIRS])
        crossed = sb("crossed", [128, 2, 4, 2, PAIRS])
        ratio = sb("ratio", [128, 2, 4, 2, PAIRS])
        nyq = sb("nyq", [128, 2, PAIRS])
        spec = sb("spec", [L, 2, 2, PAIRS, FW])
        lags = sb("lags", [128, 2, 2, L, C], R32)
        stage = sb("stage", [128, 2, GROUPS, 4, 4, KB])
        ab = [ps(f"ab{k}", [128, 4, 2, 2, PAIRS]) for k in range(2)]
        mid = [ps(f"mid{k}", [128, 4, 128]) for k in range(2)]
        far = [ps(f"far{k}", [128, GROUPS, 2, 8]) for k in range(2)]

        raw_in, consts_in, h0_in = sem("raw_in"), sem("consts_in"), sem("h0_in")
        table_in = [sem(f"table_in{k}") for k in range(2)]
        turned, turned_out, edges_set, taps_ready = sem("turned"), sem("turned_out"), sem("edges_set"), sem("taps_ready")
        respread_split = sem("respread_split")
        ab_ready, den_ready, mag_ready, rec_ready = sem("ab_ready"), sem("den_ready"), sem("mag_ready"), sem("rec_ready")
        prod_ready, num_ready, quot_ready = sem("prod_ready"), sem("num_ready"), sem("quot_ready")
        spec_ready, mid_ready, lags_high, lags_low = sem("spec_ready"), sem("mid_ready"), sem("lags_high"), sem("lags_low")
        far_ready, far_out = sem("far_ready"), [sem(f"far_out{k}") for k in range(2)]
        stored = [sem(f"stored{k}") for k in range(2)]

        block = ctx.enter_context(nc.Block())

        def table_load(eng, blk):
            fws = BLOCKS[blk]
            eng.dma_start(table[:, blk % 2, 0:len(fws)],
                          const["taps"][:, fws[0] * 2 * L:(fws[-1] + 1) * 2 * L]).then_inc(table_in[blk % 2], 16)

        @block.sync
        def _(sp):
            for layer in range(2):
                for ab_ in range(2):
                    src = io[("den", "num")[ab_] + str(layer)].rearrange("(t a) b p q -> t (a b) (p q)", t=2)
                    for t in range(2):
                        sp.dma_start(raw[:, layer * 4 + ab_ * 2 + t, :], src[t]).then_inc(raw_in, 16)
            sp.dma_start(ident[:], const["ident"]).then_inc(raw_in, 16)
            sp.dma_start(inv_h[:], const["inv_h"]).then_inc(consts_in, 16)
            sp.dma_start(respread_raw[:], const["respread"]).then_inc(consts_in, 16)
            for layer in range(2):
                h0 = io[f"h0{layer}"].rearrange("i j a b -> (a b) (i j)")
                sp.dma_start(h0s[:, layer], h0.broadcast_to([65, 256])).then_inc(h0_in, 16)
            table_load(sp, 0)
            table_load(sp, 1)
            for blk in range(2, NB):
                sp.wait_ge(ab_ready, blk - 1)
                table_load(sp, blk)

            def store(q, jp, piece):
                if piece == 0:
                    for k in range(2):
                        sp.wait_ge(far_out[k], q * KB + 9 + 8 * jp)
                at = slice(GROUPS // PIECES * piece, GROUPS // PIECES * (piece + 1))
                sp.dma_start(scratch["filters"][q, jp, :, at], stage[:, jp, at].rearrange("p g m s k -> p g (m s k)")
                             ).then_inc(stored[jp], 16)

            def step(q):
                for blk in range(NB):
                    sp.wait_ge(ab_ready, q * NB + blk - 1)
                    table_load(sp, blk)
                    if 2 <= blk < 10 and not (isinstance(q, int) and q == 1):
                        store(q - 2, 1, blk - 2)
                    if blk >= 10:
                        store(q - 1, 0, blk - 10)

            step(1)
            with sp.Fori(2, QUARTERS) as q:
                step(q)
            for q, jp in ((QUARTERS - 2, 1), (QUARTERS - 1, 0), (QUARTERS - 1, 1)):
                for piece in range(PIECES):
                    store(q, jp, piece)
            for jp in range(2):
                sp.wait_ge(stored[jp], 16 * PIECES * QUARTERS)

        def transform_taps(q, blk):
            n = q * NB + blk
            nc.tensor.wait_ge(table_in[blk % 2], 16 * (q * (NB // 2) + blk // 2 + 1))
            if not (isinstance(q, int) and n < 2):
                nc.tensor.wait_ge(prod_ready, n - 1)
            for k in range(len(BLOCKS[blk])):
                for part in range(2):
                    mm = nc.tensor.matmul(ab[blk % 2][:, k, part], table[:, blk % 2, k, part],
                                          taps_ab[:, q], start=True, stop=True)
            mm.then_inc(ab_ready, 1)

        LAG_GROUPS, SLOT_UNITS = [range(0)] * NB, [range(0)] * NB
        for n in range(4):
            LAG_GROUPS[1 + n], LAG_GROUPS[8 + n] = range(2 * n, 2 * n + 2), range(8 + 2 * n, 10 + 2 * n)
        for n, at in enumerate((0, 5, 10)):
            SLOT_UNITS[5 + n] = range(at, (5, 10, 16)[n])
        for n in range(5):
            SLOT_UNITS[12 + n] = range(16 + 3 * n, 19 + 3 * n if n < 4 else 32)

        def lag_tile(half, g):
            return lags[:, half, g // 4 % 2, :, 4 * (g % 4):4 * (g % 4) + 4].rearrange("p k i -> p i k")

        def to_lags(q, k, g):
            n = q * 16 + g
            if not (isinstance(q, int) and n < 2):
                nc.tensor.wait_ge(lags_low, n - 1)
            for m in range(4):
                pair = 4 * g + m
                re, im = spec[:, k, 0, pair, :], spec[:, k, 1, pair, :]
                lo, hi = mid[g % 2][0:FW, m], mid[g % 2][FW:128, m]
                nc.tensor.matmul(lo, re, inv_h[:, 0], start=True, stop=False)
                nc.tensor.matmul(hi, im, inv_h[:, 0], start=True, stop=False)
                nc.tensor.matmul(lo, im, inv_h[:, 2], start=False, stop=True)
                mm = nc.tensor.matmul(hi, re, inv_h[:, 1], start=False, stop=True)
            mm.then_inc(mid_ready, 1)

        def to_slots(q, u):
            kb = u % KB
            if kb == 0:
                nc.tensor.wait_ge(lags_low, q * 16 + u // 2 + 8)
            nc.tensor.wait_ge(far_out[u % 2], q * KB + u // 2 + 1)
            for j in range(2):
                mm = split_product(nc.tensor, far[u % 2][:, :, j], [lags[:, m, j, 8 * kb:8 * kb + 8, :] for m in range(2)],
                                   [respread[:, m] for m in range(2)], True, True)
            mm.then_inc(far_ready, 1)

        @block.tensor
        def _(pe):
            pe.wait_ge(raw_in, 16 * 9)
            for t in range(8):
                if t >= 2:
                    pe.wait_ge(turned_out, t - 1)
                nc.tensor.transpose(mid[t % 2][0:64, 0, :], raw[:, t, :], ident[:]).then_inc(turned, 1)
            pe.wait_ge(turned_out, 8)
            pe.wait_ge(taps_ready, 2)

            def turn_back(q, k, blk):
                if blk == 1:
                    pe.wait_ge(spec_ready, q + 1)
                for g in LAG_GROUPS[blk]:
                    to_lags(q, k, g)
                for u in SLOT_UNITS[blk]:
                    to_slots(q, u)

            def step(q, k):
                for blk in range(NB):
                    transform_taps(q + 1, blk)
                    turn_back(q, k, blk)

            for blk in range(NB):
                transform_taps(0, blk)
            pe.wait_ge(consts_in, 32)
            pe.wait_ge(respread_split, 2)
            step(0, 0)
            with pe.Fori(1, QUARTERS // 2) as p:
                step(2 * p - 1, 1)
                step(2 * p, 0)
            for blk in range(NB):
                turn_back(QUARTERS - 1, 1, blk)

        @block.scalar
        def _(act):
            def split_den(q, blk):
                n, f, s = q * NB + blk, len(BLOCKS[blk]), blk % 2
                act.wait_ge(ab_ready, n + 1)
                if not (isinstance(q, int) and n < 2):
                    act.wait_ge(prod_ready, n - 1)
                    act.wait_ge(mag_ready, n - 1)
                nc.scalar.activation(den[:, s, 0:f], ab[s][:, 0:f, :, 0], ACT.Copy)
                nc.scalar.activation(sq[:, s, 0:f], ab[s][:, 0:f, :, 0], ACT.Square).then_inc(den_ready, 1)

            def lags_out(q, g):
                if g % 8 == 0 and not (isinstance(q, int) and q == 0 and g == 0):
                    act.wait_ge(far_ready, q * 2 * KB + 2 * g)
                act.wait_ge(mid_ready, q * 16 + g + 1)
                split_high(nc.scalar, lag_tile(0, g), mid[g % 2][:]).then_inc(lags_high, 1)

            def slots_out(q, u):
                jp, kb = u // KB, u % KB
                act.wait_ge(far_ready, q * 2 * KB + u + 1)
                if kb == 0 and not (isinstance(q, int) and q == 0):
                    act.wait_ge(stored[jp], 16 * PIECES * q)
                nc.scalar.activation(stage[:, jp, :, :, :, kb], far[u % 2][:].rearrange("p g j (c s) -> p g (j c) s", c=2),
                                     ACT.Copy).then_inc(far_out[u % 2], 1)
            for k in range(2):
                act.sem_inc(far_out[k], 1)
            def step(q):
                for blk in range(NB):
                    split_den(q + 1, blk)
                    for g in LAG_GROUPS[blk]:
                        lags_out(q, g)
                    for u in SLOT_UNITS[blk]:
                        slots_out(q, u)

            act.wait_ge(consts_in, 32)
            split_high(nc.scalar, respread[:, 0], respread_raw[:]).then_inc(respread_split, 1)
            for blk in range(NB):
                split_den(0, blk)
            step(0)
            with act.Fori(1, QUARTERS - 1) as q:
                step(q)
            for blk in range(NB):
                for g in LAG_GROUPS[blk]:
                    lags_out(QUARTERS - 1, g)
                for u in SLOT_UNITS[blk]:
                    slots_out(QUARTERS - 1, u)

        @block.vector
        def _(dve):
            for t in range(8):
                dve.wait_ge(turned, t + 1)
                layer, ab_, half = t // 4, t // 2 % 2, t % 2
                for jq in range(4):
                    op = nc.vector.tensor_copy(
                        taps_ab[0:64, 4 * layer + jq, ab_].rearrange("r (j i) -> r i j", i=C)[:, 8 * half:8 * half + 8, :],
                        mid[t % 2][0:64, 0, :].rearrange("r (i q j) -> r q i j", q=4, j=4)[:, jq])
                op.then_inc(turned_out, 1)
            dve.memset(taps_ab[64:65, :, 1, :], 0.0)
            dve.memset(taps_ab[64:65, :, 0, :], 1.0).then_inc(edges_set, 1)
            dve.wait_ge(h0_in, 32)
            dve.wait_ge(turned_out, 8)
            dve.wait_ge(edges_set, 1)
            for layer in range(2):
                at = slice(4 * layer, 4 * layer + 4)
                nc.vector.tensor_tensor(h0_taps[:, at].rearrange("p q (j i) -> p q j i", i=C),
                                        taps_ab[:, at, 0].rearrange("p q (j i) -> p q j i", i=C),
                                        h0s[:, layer].rearrange("p i (q j) -> p q j i", j=4), ALU.mult).then_inc(edges_set, 1)
            dve.wait_ge(edges_set, 3)
            for layer in range(2):
                at = slice(4 * layer, 4 * layer + 4)
                nc.vector.tensor_tensor(taps_ab[:, at, 1], taps_ab[:, at, 1], h0_taps[:, at], ALU.add).then_inc(taps_ready, 1)
            dve.wait_ge(respread_split, 1)
            split_low(nc.vector, respread[:, 1], respread_raw[:], respread[:, 0]).then_inc(respread_split, 1)

            def quotient(q, blk):
                n, f, s = q * NB + blk, len(BLOCKS[blk]), blk % 2
                dve.wait_ge(den_ready, n + 1)
                if not (isinstance(q, int) and n < 2):
                    dve.wait_ge(quot_ready, n - 1)
                nc.vector.tensor_tensor(straight[:, s, 0:f], ab[s][:, 0:f, :, 1], den[:, s, 0:f], ALU.mult)
                nc.vector.tensor_tensor(crossed[:, s, 0:f, 0], ab[s][:, 0:f, 1, 1], den[:, s, 0:f, 0], ALU.mult)
                nc.vector.tensor_tensor(crossed[:, s, 0:f, 1], ab[s][:, 0:f, 0, 1], den[:, s, 0:f, 1],
                                        ALU.mult).then_inc(prod_ready, 1)
                dve.wait_ge(mag_ready, n + 1)
                nc.vector.reciprocal(rec[:, s, 0:f], mag[:, s, 0:f]).then_inc(rec_ready, 1)

            def lags_rest(q, g):
                dve.wait_ge(lags_high, q * 16 + g + 1)
                split_low(nc.vector, lag_tile(1, g), mid[g % 2][:], lag_tile(0, g)).then_inc(lags_low, 1)

            def step(q):
                for blk in range(NB):
                    quotient(q + 1, blk)
                    for g in LAG_GROUPS[blk]:
                        lags_rest(q, g)

            for blk in range(NB):
                quotient(0, blk)
            step(0)
            with dve.Fori(1, QUARTERS - 1) as q:
                step(q)
            for g in range(16):
                lags_rest(QUARTERS - 1, g)

        @block.gpsimd
        def _(pool):
            def magnitude(q, blk):
                n, f, s = q * NB + blk, len(BLOCKS[blk]), blk % 2
                pool.wait_ge(den_ready, n + 1)
                if not (isinstance(q, int) and n < 2):
                    pool.wait_ge(rec_ready, n - 1)
                nc.gpsimd.tensor_tensor(mag[:, s, 0:f], sq[:, s, 0:f, 0], sq[:, s, 0:f, 1], ALU.add).then_inc(mag_ready, 1)

            def combine(q, k):
                magnitude(q, 0)
                for blk in range(NB):
                    n, f, s = q * NB + blk, len(BLOCKS[blk]), blk % 2
                    pool.wait_ge(prod_ready, n + 1)
                    if not (isinstance(q, int) and n < 2):
                        pool.wait_ge(quot_ready, n - 1)
                    nc.gpsimd.tensor_tensor(ratio[:, s, 0:f, 0], straight[:, s, 0:f, 0], straight[:, s, 0:f, 1], ALU.add)
                    nc.gpsimd.tensor_tensor(ratio[:, s, 0:f, 1], crossed[:, s, 0:f, 0], crossed[:, s, 0:f, 1],
                                            ALU.subtract).then_inc(num_ready, 1)
                    if blk + 1 < NB:
                        magnitude(q, blk + 1)
                    pool.wait_ge(num_ready, n + 1)
                    pool.wait_ge(rec_ready, n + 1)
                    if blk == 0 and not (isinstance(q, int) and q < 2):
                        pool.wait_ge(mid_ready, 16 * (q - 1))
                    for part in range(2):
                        out = nyq[:, part:part + 1] if blk == NB - 1 else \
                            spec[:, k, part, :, BLOCKS[blk][0]:BLOCKS[blk][-1] + 1].rearrange("p n f -> p f n")
                        op = nc.gpsimd.tensor_tensor(out, ratio[:, s, 0:f, part], rec[:, s, 0:f], ALU.mult)
                    op.then_inc(quot_ready, 1)
                pool.wait_ge(quot_ready, (q + 1) * NB)
                nc.gpsimd.tensor_tensor(spec[:, k, 0, :, 0], spec[:, k, 0, :, 0], nyq[:, 1], ALU.subtract)
                nc.gpsimd.tensor_tensor(spec[:, k, 1, :, 0], spec[:, k, 1, :, 0], nyq[:, 0], ALU.add).then_inc(spec_ready, 1)

            combine(0, 0)
            combine(1, 1)
            with pool.Fori(1, QUARTERS // 2) as p:
                combine(2 * p, 0)
                combine(2 * p + 1, 1)


ROW = L + 8


def spectrum(nc, image, source, scratch, const, tag):
    with ExitStack() as ctx:
        sb, ps, sem = allocators(nc, ctx, tag)
        ident = sb("ident", [128, 128])
        average = sb("average", [128, 128])
        fwd_w = sb("fwd_w", [L, 2, 128])
        eps = sb("eps", [128, 1])
        stats = sb("stats", [128, 32, 6])
        dev = sb("dev", [128, 32, 2])
        spread = sb("spread", [128, 32, 2])
        mean = sb("mean", [128, 32])
        var = sb("var", [128, 32])
        std = sb("std", [128, 32])
        rstd = sb("rstd", [128, 32])
        cols = sb("cols", [L, C, B, L])
        rows = sb("rows", [128, 4, B, ROW])
        turn = [ps(f"turn{k}", [128, 4, L]) for k in range(4)]
        freq = [ps(f"freq{k}", [128, B, L]) for k in range(2)]
        tot = ps("tot", [128, 64])

        image_in = [sem(f"image_in{b}") for b in range(B)]
        consts_in, stats_ready, zeroed = sem("consts_in"), sem("stats_ready"), sem("zeroed")
        sum_ready, mean_ready, dev_ready, sq_ready = sem("sum_ready"), sem("mean_ready"), sem("dev_ready"), sem("sq_ready")
        spread_ready, var_ready, std_ready, rstd_ready = sem("spread_ready"), sem("var_ready"), sem("std_ready"), sem("rstd_ready")
        turn_ready, cols_ready, freq_ready, rows_ready = sem("turn_ready"), sem("cols_ready"), sem("freq_ready"), sem("rows_ready")
        stored = [sem(f"stored{k}") for k in range(4)]
        block = ctx.enter_context(nc.Block())

        @block.sync
        def _(sp):
            if source is not None:
                for b in range(B):
                    sp.dma_start(image[:, b], source[b]).then_inc(image_in[b], 16)
            sp.dma_start(ident[:], const["ident"]).then_inc(consts_in, 16)
            sp.dma_start(average[:], const["average"]).then_inc(consts_in, 16)
            sp.dma_start(fwd_w[:], const["fwd_w"]).then_inc(consts_in, 16)
            for u in range(2 * C):
                i, par = u // 2, u % 2
                sp.wait_ge(rows_ready, u + 1)
                for part in range(2):
                    sp.dma_start(scratch["spectrum"][i, par * FW:(par + 1) * FW, part],
                                 rows[part * FW:(part + 1) * FW, u % 4].rearrange("p b h -> p (b h)")).then_inc(stored[u % 4], 16)
            for k in range(4):
                sp.wait_ge(stored[k], 16 * 2 * (2 * C // 4))

        @block.vector
        def _(dve):
            dve.memset(eps[:], 1e-5)
            dve.memset(rows[:, :, :, 0:8], 0.0).then_inc(zeroed, 1)
            for n in range(32):
                b, g = n // 8, n % 8
                if source is not None and g == 0:
                    dve.wait_ge(image_in[b], 16)
                op = nc.vector.bn_stats(stats[:, n], image[:, b, :, 2 * g:2 * g + 2])
            op.then_inc(stats_ready, 1)
            sample = stats[:].rearrange("p n (s k) -> p n s k", k=3)
            dve.wait_ge(sum_ready, 1)
            nc.vector.tensor_reduce(mean[:], tot[:].rearrange("p (n s) -> p n s", s=2), AX.X, ALU.add).then_inc(mean_ready, 1)
            dve.wait_ge(mean_ready, 1)
            nc.vector.tensor_tensor(dev[:], sample[:, :, :, 1], mean[:].unsqueeze(2).broadcast_to([128, 32, 2]),
                                    ALU.subtract).then_inc(dev_ready, 1)
            dve.wait_ge(dev_ready, 1)
            nc.vector.tensor_tensor(dev[:], dev[:], dev[:], ALU.mult).then_inc(sq_ready, 1)
            dve.wait_ge(sq_ready, 1)
            nc.vector.scalar_tensor_tensor(out=spread[:], in0=sample[:, :, :, 2], scalar=1.0 / 128, in1=dev[:],
                                           op0=ALU.mult, op1=ALU.add).then_inc(spread_ready, 1)
            dve.wait_ge(sum_ready, 2)
            nc.vector.tensor_reduce(var[:], tot[:].rearrange("p (n s) -> p n s", s=2), AX.X, ALU.add).then_inc(var_ready, 1)
            dve.wait_ge(std_ready, 1)
            nc.vector.reciprocal(rstd[:], std[:]).then_inc(rstd_ready, 1)
            dve.wait_ge(rstd_ready, 1)
            for i in range(C):
                dve.wait_ge(turn_ready, i + 1)
                for b in range(B):
                    n = 8 * b + i // 2
                    op = nc.vector.tensor_scalar(cols[:, i, b], turn[i % 4][:, b], mean[:, n:n + 1], rstd[:, n:n + 1],
                                                 ALU.subtract, ALU.mult)
                op.then_inc(cols_ready, 1)

        @block.scalar
        def _(act):
            act.wait_ge(var_ready, 1)
            act.wait_ge(zeroed, 1)
            nc.scalar.activation(std[:], var[:], ACT.Sqrt, bias=eps[:, 0:1]).then_inc(std_ready, 1)
            for u in range(2 * C):
                act.wait_ge(freq_ready, u + 1)
                if u >= 4:
                    act.wait_ge(stored[u % 4], 32 * (u // 4))
                nc.scalar.activation(rows[:, u % 4, :, 8:ROW], freq[u % 2][:], ACT.Copy).then_inc(rows_ready, 1)

        @block.tensor
        def _(pe):
            def turn_channel(i):
                if i >= 4:
                    pe.wait_ge(cols_ready, i - 3)
                for b in range(B):
                    mm = nc.tensor.transpose(turn[i % 4][:, b], image[:, b, :, i], ident[:])
                mm.then_inc(turn_ready, 1)

            pe.wait_ge(consts_in, 48)
            if source is not None:
                for b in range(B):
                    pe.wait_ge(image_in[b], 16)
            for i in range(4):
                turn_channel(i)
            pe.wait_ge(stats_ready, 1)
            nc.tensor.matmul(tot[:].rearrange("p (n s) -> p n s", s=2), average[:],
                             stats[:].rearrange("p n (s k) -> p n s k", k=3)[:, :, :, 1], start=True, stop=True).then_inc(sum_ready, 1)
            pe.wait_ge(mean_ready, 1)
            pe.wait_ge(spread_ready, 1)
            nc.tensor.matmul(tot[:], average[:], spread[:].rearrange("p n s -> p (n s)"), start=True, stop=True).then_inc(sum_ready, 1)

            for i in range(C):
                pe.wait_ge(cols_ready, i + 1)
                for par in range(2):
                    u = 2 * i + par
                    if u >= 2:
                        pe.wait_ge(rows_ready, u - 1)
                    nc.tensor.matmul(freq[par][:], fwd_w[:, par], cols[:, i], start=True, stop=True).then_inc(freq_ready, 1)
                if i + 4 < C:
                    turn_channel(i + 4)


def convolve(nc, layer, scratch, tag):
    KB, RING = L // 8, 2
    with ExitStack() as ctx:
        sb, ps, sem = allocators(nc, ctx, tag)
        filt = sb("filt", [128, RING, 32, 4, KB])
        shifted = sb("shifted", [128, RING, 4, 2, B, L])
        out = sb("out", [128, RING, B, 2, L])
        acc = [[ps(f"acc{k}{cx}", [128, B, L]) for cx in range(2)] for k in range(RING)]
        filt_in = [sem(f"filt_in{k}") for k in range(RING)]
        rows_in = [sem(f"rows_in{k}") for k in range(RING)]
        group_done, acc_out = sem("group_done"), [[sem(f"acc_out{k}{cx}") for cx in range(2)] for k in range(RING)]
        stored = [sem(f"stored{k}") for k in range(RING)]
        block = ctx.enter_context(nc.Block())

        def load(eng, g, k):
            for jq in range(4):
                eng.dma_start(filt[:, k, 8 * jq:8 * jq + 8].rearrange("p (j m) s k -> p j (m s k)", j=2),
                              scratch["filters"][4 * layer + jq, :, :, g].rearrange("j p n -> p j n")).then_inc(filt_in[k], 16)
            for lag in range(8):
                eng.dma_start(shifted[C * lag:C * (lag + 1), k].rearrange("p s c b h -> p (s c b) h"),
                              scratch["spectrum"][:, bass.ds(4 * g, 4)].rearrange("i s c (b h) -> i (s c b) h", b=B)
                              [:, :, 8 - lag:8 - lag + L]).then_inc(rows_in[k], 16)

        @block.sync
        def _(sp):
            for k in range(RING):
                load(sp, k, k)
            with sp.Fori(1, GROUPS // RING) as n:
                for k in range(RING):
                    sp.wait_ge(group_done, RING * (n - 1) + k + 1)
                    load(sp, RING * n + k, k)

        @block.tensor
        def _(pe):
            with pe.Fori(0, GROUPS // RING) as n:
                for k in range(RING):
                    pe.wait_ge(filt_in[k], 16 * 4 * (n + 1))
                    pe.wait_ge(rows_in[k], 16 * 8 * (n + 1))
                    for cx in range(2):
                        pe.wait_ge(acc_out[k][cx], n + 1)
                        for kb in range(KB):
                            for s in range(4):
                                mm = nc.tensor.matmul(
                                    acc[k][cx][32 * s:32 * s + 32, :, 8 * kb:L],
                                    filt[:, k, :, s, kb],
                                    shifted[:, k, s, cx, :, 0:L - 8 * kb], start=kb == 0, stop=kb == KB - 1)
                    mm.then_inc(group_done, 1)

        def evacuate(eng, copy, cx, store):
            for k in range(RING):
                eng.sem_inc(acc_out[k][cx], 1)
            with eng.Fori(0, GROUPS // RING) as n:
                for k in range(RING):
                    eng.wait_ge(group_done, RING * n + k + 1)
                    eng.wait_ge(stored[k], 16 * (n + 1))
                    copy(out[:, k, :, cx], acc[k][cx][:]).then_inc(acc_out[k][cx], 1)
                    store(n, k)

        @block.vector
        def _(dve):
            evacuate(dve, nc.vector.tensor_copy, 0, lambda n, k: None)

        @block.scalar
        def _(act):
            def store(n, k):
                for cx in range(2):
                    act.wait_ge(acc_out[k][cx], n + 2)
                act.dma_start(scratch["products"][bass.ds(4 * (RING * n + k), 4)].rearrange("s j c n -> (s j c) n"),
                              out[:, k].rearrange("p b x h -> p (b x h)")).then_inc(stored[k], 16)

            for k in range(RING):
                act.sem_inc(stored[k], 16)
            evacuate(act, nc.scalar.copy, 1, store)
            for k in range(RING):
                act.wait_ge(stored[k], 16 * (GROUPS // RING + 1))


def back_to_image(nc, image, out_dram, scratch, const, tag):
    RING = 4
    CHUNKS = [(b, half) for b in range(B) for half in range(2)]
    UNITS = [(b, quarter) for b in range(B) for quarter in range(4)]
    with ExitStack() as ctx:
        sb, ps, sem = allocators(nc, ctx, tag)
        inv_w = sb("inv_w", [128, 2, 2, L])
        prod = sb("prod", [128, RING, 2, 8, 2, L])
        img = [ps(f"img{k}", [128, 4, L]) for k in range(4)]
        consts_in, done, added, out_stored = sem("consts_in"), sem("done"), sem("added"), sem("out_stored")
        prod_in = [sem(f"prod_in{k}") for k in range(RING)]
        block = ctx.enter_context(nc.Block())

        @block.sync
        def _(sp):
            sp.dma_start(inv_w[:], const["inv_w"]).then_inc(consts_in, 16)
            for n, (b, half) in enumerate(CHUNKS):
                if n >= RING:
                    sp.wait_ge(done, 2 * (n - RING) + 2)
                for par in range(2):
                    for c in range(2):
                        sp.dma_start(prod[FW * c:FW * (c + 1), n % RING, par],
                                     scratch["products"][FW * par:FW * (par + 1), 8 * half:8 * half + 8, c]
                                     [:, :, 2 * L * b:2 * L * (b + 1)].rearrange("s j (x h) -> s j x h", x=2)).then_inc(prod_in[n % RING], 16)

        @block.tensor
        def _(pe):
            pe.wait_ge(consts_in, 16)
            for u, (b, quarter) in enumerate(UNITS):
                n = u // 2
                if u % 2 == 0:
                    pe.wait_ge(prod_in[n % RING], 16 * 4 * (n // RING + 1))
                if u >= 4:
                    pe.wait_ge(added, u - 3)
                for j in range(4):
                    for t in range(4):
                        par, cx = t // 2, t % 2
                        mm = nc.tensor.matmul(img[u % 4][:, j], prod[:, n % RING, par, 4 * (quarter % 2) + j, cx],
                                              inv_w[:, par, cx], start=t == 0, stop=t == 3)
                mm.then_inc(done, 1)

        @block.vector
        def _(dve):
            for u, (b, quarter) in enumerate(UNITS):
                dve.wait_ge(done, u + 1)
                at = image[:, b, :, 4 * quarter:4 * quarter + 4]
                nc.vector.tensor_tensor(at, at, img[u % 4][:].rearrange("p j w -> p w j"), ALU.add).then_inc(added, 1)

        @block.scalar
        def _(act):
            if out_dram is not None:
                for b in range(B):
                    act.wait_ge(added, 4 * b + 4)
                    act.dma_start(out_dram[b], image[:, b]).then_inc(out_stored, 16)
                act.wait_ge(out_stored, 16 * B)


PATCHES = 1024
N = 512


def slabs(w):
    return w.rearrange("r s c (d n) -> d (s c) r n", d=8)


def moments_tensors(sb, ps):
    return (sb("average", [128, 128]), sb("eps", [128, 1]), sb("stats", [128, B, 8, 6]), sb("dev", [128, B, 16]),
            sb("spread", [128, B, 16]), sb("var", [128, B]), sb("std", [128, B]), ps("tot", [128, B, 16]))


def to_patches(nc, io, image, mean, rstd, raw, scratch, const, tag):
    with ExitStack() as ctx:
        sb, ps, sem = allocators(nc, ctx, tag)
        ident = sb("ident", [128, 128])
        xt = sb("xt", [128, 8, PATCHES])
        average, eps, stats, dev, spread, var, std, tot = moments_tensors(sb, ps)
        turn = [ps(f"turn{k}", [128, 4, L]) for k in range(4)]
        ident_in, average_in, turned, moved, stored = (sem(n) for n in ("ident_in", "average_in", "turned", "moved", "stored"))
        next_in = sem("next_in")
        stats_ready, step, sum_ready, std_ready = sem("stats_ready"), sem("step"), sem("sum_ready"), sem("std_ready")
        sample = stats[:].rearrange("p b r (s k) -> p b (r s) k", k=3)
        block = ctx.enter_context(nc.Block())

        @block.sync
        def _(sp):
            sp.dma_start(ident[:], const["ident"]).then_inc(ident_in, 16)
            sp.dma_start(average[:], const["average_groups"]).then_inc(average_in, 16)
            sp.dma_start(raw[:, 0], slabs(io["Wq"])[0]).then_inc(next_in, 16)
            for half in range(2):
                sp.wait_ge(moved, 8 * half + 8)
                sp.dma_start(scratch["patches"][half], xt[:, :, N * half:N * half + N]).then_inc(stored, 16)
            sp.wait_ge(stored, 32)
            sp.wait_ge(next_in, 16)

        @block.tensor
        def _(pe):
            pe.wait_ge(ident_in, 16)
            for t in range(16):
                if t >= 4:
                    pe.wait_ge(moved, t - 3)
                for k in range(4):
                    b, ww = (4 * t + k) // 16, (4 * t + k) % 16
                    mm = nc.tensor.transpose(turn[t % 4][:, k], image[:, b, 8 * ww:8 * ww + 8, :].rearrange("h s c -> h (s c)"),
                                             ident[:])
                mm.then_inc(turned, 1)
            pe.wait_ge(average_in, 16)
            pe.wait_ge(stats_ready, 8 * B)
            nc.tensor.matmul(tot[:], average[:], sample[:, :, :, 1], start=True, stop=True).then_inc(sum_ready, 1)
            pe.wait_ge(step, 5)
            nc.tensor.matmul(tot[:], average[:], spread[:], start=True, stop=True).then_inc(sum_ready, 1)

        @block.scalar
        def _(act):
            for t in range(16):
                act.wait_ge(turned, t + 1)
                nc.scalar.activation(xt[:, :, 64 * t:64 * t + 64], turn[t % 4][:].rearrange("p k (h r) -> p r (k h)", r=8),
                                     ACT.Copy).then_inc(moved, 1)
            act.wait_ge(step, 6)
            nc.scalar.activation(std[:], var[:], ACT.Sqrt, bias=eps[:, 0:1]).then_inc(std_ready, 1)

        @block.vector
        def _(dve):
            dve.memset(eps[:], 1e-5).then_inc(step, 1)
            for b in range(B):
                dve.wait_ge(moved, 4 * b + 4)
                for r in range(8):
                    nc.vector.bn_stats(stats[:, b, r], xt[:, r, 256 * b:256 * b + 256]).then_inc(stats_ready, 1)
            dve.wait_ge(sum_ready, 1)
            nc.vector.tensor_reduce(mean[:], tot[:], AX.X, ALU.add).then_inc(step, 1)
            dve.wait_ge(step, 2)
            nc.vector.tensor_tensor(dev[:], sample[:, :, :, 1], mean[:].unsqueeze(2).broadcast_to([128, B, 16]),
                                    ALU.subtract).then_inc(step, 1)
            dve.wait_ge(step, 3)
            nc.vector.tensor_tensor(dev[:], dev[:], dev[:], ALU.mult).then_inc(step, 1)
            dve.wait_ge(step, 4)
            nc.vector.scalar_tensor_tensor(out=spread[:], in0=sample[:, :, :, 2], scalar=1.0 / 128, in1=dev[:],
                                           op0=ALU.mult, op1=ALU.add).then_inc(step, 1)
            dve.wait_ge(sum_ready, 2)
            nc.vector.tensor_reduce(var[:], tot[:], AX.X, ALU.add).then_inc(step, 1)
            dve.wait_ge(std_ready, 1)
            nc.vector.reciprocal(rstd[:], std[:]).then_inc(step, 1)
            dve.wait_ge(step, 7)


def patch_correlate(nc, io, half, x, mean, rstd, raw, store, sums, scratch, const, tag):
    with ExitStack() as ctx:
        sb, ps, sem = allocators(nc, ctx, tag)
        raw = [raw[:, n] for n in range(2)]
        w = [sb(f"w_{n}", [128, 2, 8, 2, 128], R32) for n in "qk"]
        bias = [sb(f"bias_{n}", [128, 8, 4]) for n in "qk"]
        to_freq = [sb(f"to_freq_{n}", [128, 2, 2, 128], R32) for n in "qk"]
        gather = sb("gather", [128, 64])
        whole = sb("whole", [128, N])
        src = [sb(f"src_{n}", [128, 2, 2, N], R32) for n in "qk"]
        qf = sb("qf", [128, 2, 2, N])
        pf = sb("pf", [128, 2, 2, N])
        acc_q, acc_k = [ps(f"acc_q{k}", [128, N]) for k in range(2)], ps("acc_k", [128, N])
        acc = [acc_q, [acc_k, acc_k]]
        freq = [[ps(f"freq_{n}{d}", [128, N]) for d in range(2)] for n in "qk"]
        o_ps = ps("o_ps", [128, N])
        consts_in, bias_in, x_in, scaled, x_high, x_low = (sem(n) for n in (
            "consts_in", "bias_in", "x_in", "scaled", "x_high", "x_low"))
        raw_in, high, low, done, out = ([sem(f"{n}_{m}") for m in "qk"] for n in ("raw_in", "high", "low", "done", "out"))
        qf_done, qf_out, kf_done, pf_ready = sem("qf_done"), sem("qf_out"), sem("kf_done"), sem("pf_ready")
        transforms_in = sem("transforms_in")
        consts_high, consts_low, src_high, src_low = sem("consts_high"), sem("consts_low"), sem("src_high"), sem("src_low")
        o_done, o_out, sums_zero, summed = sem("o_done"), sem("o_out"), sem("sums_zero"), sem("summed")
        block = ctx.enter_context(nc.Block())
        w_dram = [slabs(io["Wq"]), slabs(io["Wk"])]
        xs = raw[1]
        to_freq_raw = [qf[:, 0, n, 0:256] for n in range(2)]
        STEPS = 16

        @block.sync
        def _(sp):
            for n, name in enumerate(("patch_q", "patch_k")):
                sp.dma_start(to_freq_raw[n], const[name]).then_inc(transforms_in, 16)
            if half == 0:
                sp.dma_start(xs, scratch["patches"][half]).then_inc(x_in, 16)
            for n, name in enumerate(("bq", "bk")):
                for e in range(2):
                    sp.dma_start(bias[n][64 * e:64 * e + 64], io[name].rearrange("(d a p h) -> a p d h", d=8, a=2, h=4)[e]
                                 ).then_inc(bias_in, 16)
            sp.dma_start(gather[:], const["patch_back"]).then_inc(consts_in, 16)
            sp.wait_ge(x_low, 2)
            sp.dma_start(raw[1], w_dram[1][0]).then_inc(raw_in[1], 16)
            with sp.Fori(1, 8) as d:
                for n in range(2):
                    sp.wait_ge(low[n], 2 * d)
                    sp.dma_start(raw[n], w_dram[n][d]).then_inc(raw_in[n], 16)

        def slab(n, g):
            return raw[n].rearrange("p r (e h) -> p r h e", h=4)[:, :, 2 * g:2 * g + 2, :]

        @block.tensor
        def _(pe):
            def project(n, t, k):
                if n or not (isinstance(t, int) and t == 0):
                    pe.wait_ge(out[n], 2 * t + (k if n else k - 1))
                if k == 0:
                    pe.wait_ge(low[n], t + 1)
                for r in range(8):
                    mm = split_product(pe, acc[n][k][:], [w[n][:, m, r, k] for m in range(2)], [x[:, m, r] for m in range(2)],
                                       r == 0, r == 7)
                mm.then_inc(done[n], 1)

            def transform(n, t, k):
                pe.wait_ge(src_low, 4 * t + 2 * n + k + 1)
                pe.wait_ge(pf_ready if n else qf_out, 2 * t + k)
                for d in range(2):
                    mm = split_product(pe, freq[n][d][:], [to_freq[n][:, m, d] for m in range(2)],
                                       [src[n][:, k, m] for m in range(2)], True, True)
                mm.then_inc(kf_done if n else qf_done, 1)

            def back(t, k):
                pe.wait_ge(pf_ready, 2 * t + k + 1)
                pe.wait_ge(o_out, 2 * t + k)
                for d in range(2):
                    mm = pe.matmul(o_ps[64 * d:64 * d + 64], gather[:], pf[:, k, d], start=True, stop=True)
                mm.then_inc(o_done, 1)

            def step(t, first):
                project(0, t, 0)
                if not first:
                    transform(1, t - 1, 1)
                project(0, t, 1)
                if not first:
                    back(t - 1, 0)
                transform(0, t, 0)
                project(1, t, 0)
                transform(0, t, 1)
                if not first:
                    back(t - 1, 1)
                project(1, t, 1)
                transform(1, t, 0)

            pe.wait_ge(consts_in, 16)
            pe.wait_ge(consts_low, 2)
            pe.wait_ge(x_low, 2)
            step(0, True)
            step(1, False)
            with pe.Fori(1, 8) as d:
                step(2 * d, False)
                step(2 * d + 1, False)
            transform(1, STEPS - 1, 1)
            back(STEPS - 1, 0)
            back(STEPS - 1, 1)

        @block.scalar
        def _(act):
            def split(n, t, g):
                if n or t >= 2:
                    act.wait_ge(raw_in[n], 16 * (t // 2 + n))
                if t:
                    act.wait_ge(done[n], 2 * t)
                split_high(nc.scalar, w[n][:, 0], slab(n, g)).then_inc(high[n], 1)

            def evacuate(n, t, k):
                act.wait_ge(done[n], 2 * t + k + 1)
                if t:
                    if n:
                        act.wait_ge(kf_done, 2 * t + k - 1)
                    else:
                        act.wait_ge(qf_done, 2 * t + k - 1)
                at = 2 * (t % 2) + k
                nc.scalar.activation(src[n][:, k, 0], acc[n][k][:], ACT.Identity, bias=bias[n][:, t // 2, at:at + 1]
                                     ).then_inc(src_high, 1)
                act.wait_ge(src_low, 4 * t + 2 * n + k)
                nc.scalar.activation(whole[:], acc[n][k][:], ACT.Identity, bias=bias[n][:, t // 2, at:at + 1]).then_inc(out[n], 1)

            def spectrum_out(t, k):
                act.wait_ge(qf_done, 2 * t + k + 1)
                if t:
                    act.wait_ge(pf_ready, 2 * t + k - 1)
                for d in range(2):
                    op = nc.scalar.activation(qf[:, k, d], freq[0][d][:], ACT.Copy)
                op.then_inc(qf_out, 1)

            split(0, 0, 0)
            act.wait_ge(transforms_in, 32)
            for n in range(2):
                split_high(nc.scalar, to_freq[n][:, 0].rearrange("p d f -> p (d f)"), to_freq_raw[n]).then_inc(consts_high, 1)
            for b in range(2):
                act.wait_ge(scaled, b + 1)
                split_high(nc.scalar, x[:, 0, :, 256 * b:256 * b + 256], xs[:, :, 256 * b:256 * b + 256]).then_inc(x_high, 1)
            act.wait_ge(bias_in, 64)
            split(1, 0, 0)
            act.wait_ge(consts_low, 2)
            for t in range(STEPS):
                evacuate(0, t, 0)
                evacuate(0, t, 1)
                spectrum_out(t, 0)
                if t + 1 < STEPS:
                    split(0, t + 1, (t + 1) % 2)
                evacuate(1, t, 0)
                spectrum_out(t, 1)
                evacuate(1, t, 1)
                if t + 1 < STEPS:
                    split(1, t + 1, (t + 1) % 2)

        @block.vector
        def _(dve):
            def split(n, t, g):
                dve.wait_ge(high[n], t + 1)
                split_low(nc.vector, w[n][:, 1], slab(n, g), w[n][:, 0]).then_inc(low[n], 1)

            def product(t, k):
                dve.wait_ge(kf_done, 2 * t + k + 1)
                dve.wait_ge(qf_out, 2 * t + k + 1)
                for d in range(2):
                    op = nc.vector.tensor_tensor(pf[:, k, d], freq[1][d][:], qf[:, k, d], ALU.mult)
                op.then_inc(pf_ready, 1)

            def pixels_out(t, k, d, g):
                dve.wait_ge(o_done, 2 * t + k + 1)
                flat = store[:].rearrange("p h d n -> p (h d n)")
                at = dve.snap(d * N + (2 * g + k) * 8 * N)
                nc.vector.tensor_copy(flat[:, bass.ds(at, N)], o_ps[:]).then_inc(o_out, 1)

            def step(t, d, g, first, last):
                if not first:
                    product(t - 1, 1)
                    pixels_out(t - 1, 0, d - 1 if g == 0 else d, 1 - g)
                    pixels_out(t - 1, 1, d - 1 if g == 0 else d, 1 - g)
                if not last:
                    split(0, t + 1, 1 - g)
                product(t, 0)
                if not last:
                    split(1, t + 1, 1 - g)

            dve.memset(sums[:], 0.0).then_inc(sums_zero, 1)
            if half == 0:
                dve.wait_ge(x_in, 16)
            for b in range(2):
                at = slice(256 * b, 256 * b + 256)
                n = 2 * half + b
                nc.vector.tensor_scalar(xs[:, :, at], xs[:, :, at], mean[:, n:n + 1], rstd[:, n:n + 1],
                                        ALU.subtract, ALU.mult).then_inc(scaled, 1)
            for n in range(2):
                dve.wait_ge(consts_high, n + 1)
                split_low(nc.vector, to_freq[n][:, 1].rearrange("p d f -> p (d f)"), to_freq_raw[n],
                          to_freq[n][:, 0].rearrange("p d f -> p (d f)")).then_inc(consts_low, 1)
            for b in range(2):
                at = slice(256 * b, 256 * b + 256)
                dve.wait_ge(x_high, b + 1)
                split_low(nc.vector, x[:, 1, :, at], xs[:, :, at], x[:, 0, :, at]).then_inc(x_low, 1)
            split(1, 0, 0)
            step(0, 0, 0, True, False)
            step(1, 0, 1, False, False)
            with dve.Fori(1, 7) as d:
                step(2 * d, d, 0, False, False)
                step(2 * d + 1, d, 1, False, False)
            step(14, 7, 0, False, False)
            step(15, 7, 1, False, True)
            product(15, 1)
            pixels_out(15, 0, 7, 1)
            pixels_out(15, 1, 7, 1)

        @block.gpsimd
        def _(pool):
            def rest(t, n, k):
                pool.wait_ge(src_high, 4 * t + 2 * n + k + 1)
                pool.wait_ge(out[n], 2 * t + k + 1)
                split_low(nc.gpsimd, src[n][:, k, 1], whole[:], src[n][:, k, 0]).then_inc(src_low, 1)

            def add(t, d, head):
                pool.wait_ge(o_out, 2 * t + head % 2 + 1)
                pool.wait_ge(summed, 2 * t + head % 2 + 1)
                flat = store[:].rearrange("p h d n -> p (h d n)")
                at = pool.snap(d * N + head * 8 * N)
                nc.gpsimd.tensor_tensor(sums[:, head], sums[:, head], flat[:, bass.ds(at, N)], ALU.add).then_inc(summed, 1)

            def step(t, d, g, first):
                rest(t, 0, 0)
                rest(t, 0, 1)
                if not first:
                    for k in range(2):
                        add(t - 1, d if g else d - 1, 2 * (1 - g) + k)
                rest(t, 1, 0)
                rest(t, 1, 1)

            pool.wait_ge(high[0], 1)
            split_low(nc.gpsimd, w[0][:, 1], slab(0, 0), w[0][:, 0]).then_inc(low[0], 1)
            pool.wait_ge(sums_zero, 1)
            pool.sem_inc(summed, 1)
            step(0, 0, 0, True)
            step(1, 0, 1, False)
            with pool.Fori(1, 8) as d:
                step(2 * d, d, 0, False)
                step(2 * d + 1, d, 1, False)
            for k in range(2):
                add(STEPS - 1, 7, 2 + k)


def patch_norm(nc, io, store, sums, rstd, raw, const, tag):
    with ExitStack() as ctx:
        sb, ps, sem = allocators(nc, ctx, tag)
        over_dims = sb("over_dims", [128, 128])
        eps = sb("eps", [128, 1])
        square = sb("square", [128, 2, 2, N])
        std = sb("std", [128, 3, N])
        mean_ps = [ps(f"mean_ps{h}", [128, N]) for h in range(4)]
        var_ps = [ps(f"var_ps{h}", [128, N]) for h in range(4)]
        const_in, eps_set, mean_ready, centred = sem("const_in"), sem("eps_set"), sem("mean_ready"), sem("centred")
        squared, summed, std_ready, done = sem("squared"), sem("summed"), sem("std_ready"), sem("done")
        next_in = sem("next_in")
        block = ctx.enter_context(nc.Block())
        TILES = [(h, d) for h in range(4) for d in range(0, 8, 2)]

        @block.sync
        def _(sp):
            sp.dma_start(over_dims[:], const["over_dims"]).then_inc(const_in, 16)
            for k in range(2):
                sp.dma_start(raw[:, k], slabs(io["Wv"])[k]).then_inc(next_in, 16)
            sp.wait_ge(next_in, 32)

        @block.tensor
        def _(pe):
            pe.wait_ge(const_in, 16)
            for h in range(4):
                pe.matmul(mean_ps[h][:], over_dims[:], sums[:, h], start=True, stop=True).then_inc(mean_ready, 1)
            for t, (h, d) in enumerate(TILES):
                pe.wait_ge(squared, t + 1)
                for e in range(2):
                    mm = pe.matmul(var_ps[h][:], over_dims[:], square[:, t % 2, e], start=d + e == 0, stop=d + e == 7)
                mm.then_inc(summed, 1)

        @block.vector
        def _(dve):
            dve.memset(eps[:], 1e-6).then_inc(eps_set, 1)

            def inverse(h):
                dve.wait_ge(std_ready, h + 1)
                nc.vector.reciprocal(rstd[:, h], std[:, h]).then_inc(done, 1)

            for t, (h, d) in enumerate(TILES):
                dve.wait_ge(mean_ready, h + 1)
                nc.vector.tensor_tensor(store[:, h, d:d + 2], store[:, h, d:d + 2],
                                        mean_ps[h][:].unsqueeze(1).broadcast_to([128, 2, N]), ALU.subtract).then_inc(centred, 1)
                if d == 4 and h:
                    inverse(h - 1)

        @block.scalar
        def _(act):
            act.wait_ge(eps_set, 1)

            def root(h):
                act.wait_ge(summed, 4 * h + 4)
                nc.scalar.activation(std[:, h] if h < 3 else rstd[:, h], var_ps[h][:], ACT.Sqrt, bias=eps[:, 0:1]
                                     ).then_inc(std_ready, 1)

            for t, (h, d) in enumerate(TILES):
                act.wait_ge(centred, t + 1)
                if t >= 2:
                    act.wait_ge(summed, t - 1)
                nc.scalar.activation(square[:, t % 2], store[:, h, d:d + 2], ACT.Square).then_inc(squared, 1)
                if d == 2 and h:
                    root(h - 1)
            root(3)


def patch_values(nc, io, x, store, rstd, raw, const, tag):
    with ExitStack() as ctx:
        sb, ps, sem = allocators(nc, ctx, tag)
        w = sb("w", [128, 2, 2, 8, 2, 128], R32)
        bv = sb("bv", [128, 8, 4])
        scale_shift = sb("scale_shift", [128, 8, 2])
        normed = sb("normed", [128, 2, N])
        affine = sb("affine", [128, 2, N])
        v_ps = [ps(f"v_ps{k}", [128, N]) for k in range(4)]
        vec_in, v_done, normed_ready, affine_ready, used = (sem(n) for n in (
            "vec_in", "v_done", "normed_ready", "affine_ready", "used"))
        raw_in, high, low = [sem(f"raw_in{k}") for k in range(2)], sem("high"), sem("low")
        inverted = sem("inverted")
        block = ctx.enter_context(nc.Block())
        w_dram = slabs(io["Wv"])
        STEPS = 16

        @block.sync
        def _(sp):
            for e in range(2):
                at = slice(64 * e, 64 * e + 64)
                sp.dma_start(bv[at], io["bv"].rearrange("(d a p h) -> a p d h", d=8, a=2, h=4)[e]).then_inc(vec_in, 16)
                for k, name in enumerate(("ln_scale", "ln_bias")):
                    with nc.allow_non_contiguous_dma(reason="16 values"):
                        sp.dma_start(scale_shift[at, :, k], io[name].rearrange("(o d a) -> a o d", o=1, a=2)[e].broadcast_to([64, 8])
                                     ).then_inc(vec_in, 16)
            with sp.Fori(1, 4) as n:
                for k in range(2):
                    sp.wait_ge(low, 4 * n + 2 * k - 2)
                    sp.dma_start(raw[:, k], w_dram[2 * n + k]).then_inc(raw_in[k], 16)

        def slab(t):
            return raw[:, t // 2 % 2].rearrange("p r (e h) -> p r h e", h=4)[:, :, 2 * (t % 2):2 * (t % 2) + 2, :]

        @block.tensor
        def _(pe):
            with pe.Fori(0, 8) as d:
                for g in range(2):
                    pe.wait_ge(low, 2 * d + g + 1)
                    for k in range(2):
                        pe.wait_ge(used, 4 * d + 2 * g + k + 1)
                        for r in range(8):
                            mm = split_product(pe, v_ps[2 * g + k][:], [w[:, g, m, r, k] for m in range(2)],
                                               [x[:, m, r] for m in range(2)], r == 0, r == 7)
                        mm.then_inc(v_done, 1)

        @block.gpsimd
        def _(pool):
            for t in range(4 * 8):
                d, head = t // 4, t % 4
                if t >= 2:
                    pool.wait_ge(affine_ready, t - 1)
                if t == 3:
                    pool.wait_ge(inverted, 1)
                nc.gpsimd.tensor_tensor(normed[:, t % 2], store[:, head, d], rstd[:, head], ALU.mult).then_inc(normed_ready, 1)

        @block.scalar
        def _(act):
            def split(t):
                if t >= 4:
                    act.wait_ge(raw_in[t // 2 % 2], 16 * (t // 4))
                if t >= 2:
                    act.wait_ge(v_done, 2 * t - 2)
                split_high(nc.scalar, w[:, t % 2, 0], slab(t)).then_inc(high, 1)

            split(0)
            split(1)
            act.wait_ge(vec_in, 16 * 6)
            for t in range(32):
                d = t // 4
                act.wait_ge(normed_ready, t + 1)
                if t >= 2:
                    act.wait_ge(used, t - 1 + 4)
                nc.scalar.activation(affine[:, t % 2], normed[:, t % 2], ACT.Identity, scale=scale_shift[:, d, 0:1],
                                     bias=scale_shift[:, d, 1:2]).then_inc(affine_ready, 1)
                if t % 2 and t // 2 + 2 < STEPS:
                    split(t // 2 + 2)

        @block.vector
        def _(dve):
            def split(t):
                dve.wait_ge(high, t + 1)
                split_low(nc.vector, w[:, t % 2, 1], slab(t), w[:, t % 2, 0]).then_inc(low, 1)

            dve.sem_inc(used, 4)
            split(0)
            split(1)
            nc.vector.reciprocal(rstd[:, 3], rstd[:, 3]).then_inc(inverted, 1)
            dve.wait_ge(vec_in, 16 * 6)
            for t in range(32):
                d, head = t // 4, t % 4
                dve.wait_ge(v_done, t + 1)
                dve.wait_ge(affine_ready, t + 1)
                nc.vector.scalar_tensor_tensor(out=store[:, head, d], in0=v_ps[head][:], scalar=bv[:, d, head:head + 1],
                                               in1=affine[:, t % 2], op0=ALU.add, op1=ALU.mult).then_inc(used, 1)
                if t % 2 and t // 2 + 2 < STEPS:
                    split(t // 2 + 2)


def patch_project(nc, io, half, store, next_raw, scratch, const, tag):
    with ExitStack() as ctx:
        sb, ps, sem = allocators(nc, ctx, tag)
        raw = sb("raw", [128, 2, 8 * 128])
        w = sb("w", [128, 2, 2, 8, 8, C], R32)
        u = sb("u", [128, 2, 2, N], R32)
        xt = sb("xt", [128, 8, N])
        bout = sb("bout", [128, 8])
        acc = [ps(f"acc{r}", [128, N]) for r in range(8)]
        bias_in, xt_in, low, done, acc_done, summed, stored = (sem(n) for n in (
            "bias_in", "xt_in", "low", "done", "acc_done", "summed", "stored"))
        raw_in = [sem(f"raw_in{k}") for k in range(2)]
        high, next_in = sem("high"), sem("next_in")
        block = ctx.enter_context(nc.Block())
        w_dram = io["Wout"].rearrange("a b (h d e) n -> h d e (a b) n", h=4, e=2)
        TILES = [(d, h) for d in range(8) for h in range(4)]

        @block.sync
        def _(sp):
            def load(d, h):
                for e in range(2):
                    sp.dma_start(raw[64 * e:64 * e + 64, h % 2], w_dram[h, d, e]).then_inc(raw_in[h % 2], 16)

            def load_next(row):
                if half == 0:
                    sp.dma_start(next_raw[:, 0, row], slabs(io["Wq"])[0][:, row]).then_inc(next_in, 16)
                    sp.dma_start(next_raw[:, 1, row], scratch["patches"][1][:, row]).then_inc(next_in, 16)

            load(0, 0)
            load(0, 1)
            for h in range(2, 4):
                sp.wait_ge(low, h - 1)
                load(0, h)
            sp.dma_start(xt[:], scratch["patches"][half]).then_inc(xt_in, 16)
            load_next(0)
            with nc.allow_non_contiguous_dma(reason="the bias, once"):
                for s in range(8):
                    sp.dma_start(bout[C * s:C * s + C], io["bout"].rearrange("(c r s) -> s c r", r=8, s=8)[s]).then_inc(bias_in, 16)
            with sp.Fori(1, 8) as d:
                for h in range(4):
                    sp.wait_ge(low, 4 * d + h - 1)
                    load(d, h)
                load_next(d)
            for r in range(8):
                sp.wait_ge(summed, r + 1)
                sp.dma_start(scratch["patches"][half][:, r], xt[:, r]).then_inc(stored, 16)
            sp.wait_ge(stored, 16 * 8)
            if half == 0:
                sp.wait_ge(next_in, 16 * 2 * 8)

        @block.scalar
        def _(act):
            for t, (d, h) in enumerate(TILES):
                k = t % 2
                act.wait_ge(raw_in[k], 32 * (t // 2 + 1))
                if t >= 2:
                    act.wait_ge(done, t - 1)
                split_high(nc.scalar, w[:, k, 0], raw[:, k].rearrange("p (c r s) -> p r s c", r=8, s=8))
                split_high(nc.scalar, u[:, k, 0], store[:, h, d]).then_inc(high, 1)

        @block.vector
        def _(dve):
            for t, (d, h) in enumerate(TILES):
                k = t % 2
                dve.wait_ge(high, t + 1)
                split_low(nc.vector, w[:, k, 1], raw[:, k].rearrange("p (c r s) -> p r s c", r=8, s=8), w[:, k, 0])
                split_low(nc.vector, u[:, k, 1], store[:, h, d], u[:, k, 0]).then_inc(low, 1)
            dve.wait_ge(bias_in, 16 * 8)
            dve.wait_ge(xt_in, 16)
            for r in range(8):
                dve.wait_ge(acc_done, r + 1)
                nc.vector.scalar_tensor_tensor(out=xt[:, r], in0=acc[r][:], scalar=bout[:, r:r + 1], in1=xt[:, r],
                                               op0=ALU.add, op1=ALU.add).then_inc(summed, 1)

        @block.tensor
        def _(pe):
            def tile(t, k, first, last):
                pe.wait_ge(low, t + 1)
                for r in range(8):
                    mm = split_product(pe, acc[r][:], [w[:, k, m, r].rearrange("p s c -> p (s c)") for m in range(2)],
                                       [u[:, k, m] for m in range(2)], first, last)
                    if last:
                        mm.then_inc(acc_done, 1)
                if not last:
                    mm.then_inc(done, 1)

            tile(0, 0, True, False)
            tile(1, 1, False, False)
            with pe.Fori(1, 15) as n:
                for k in range(2):
                    tile(2 * n + k, k, False, False)
            tile(30, 0, False, False)
            tile(31, 1, False, True)


def local_conv(nc, io, image, scratch, const, tag):
    with ExitStack() as ctx:
        sb, ps, sem = allocators(nc, ctx, tag)
        xt = sb("xt", [128, 8, PATCHES])
        padded = sb("padded", [128, B, 18, L + 2])
        average, eps, stats, dev, spread, var, std, tot = moments_tensors(sb, ps)
        mean, rstd = sb("mean", [128, B]), sb("rstd", [128, B])
        ident = sb("ident", [128, 128])
        band = sb("band", [128, 3, 128])
        cross = sb("cross", [96, 128])
        bias = sb("bias", [128, 1])
        edge = sb("edge", [96, B, 16, L])
        res = sb("res", [128, 3, 4, L])
        acc = [ps(f"acc{k}", [128, 4, L]) for k in range(3)]
        turn = [ps(f"turn{k}", [128, 4, 128]) for k in range(3)]
        zeroed, w_in, ident_in, bias_in = sem("zeroed"), sem("w_in"), sem("ident_in"), sem("bias_in")
        edge_in = [sem(f"edge_in{b}") for b in range(B)]
        acc_done, res_ready, turned, moved = sem("acc_done"), sem("res_ready"), sem("turned"), sem("moved")
        xt_in = [sem(f"xt_in{b}") for b in range(B)]
        average_in, stats_ready, step, sum_ready = sem("average_in"), sem("stats_ready"), sem("step"), sem("sum_ready")
        std_ready, normed, border = sem("std_ready"), sem("normed"), sem("border")
        sample = stats[:].rearrange("p b r (s k) -> p b (r s) k", k=3)
        block = ctx.enter_context(nc.Block())

        @block.sync
        def _(sp):
            for b in range(B):
                sp.dma_start(xt[:, :, 256 * b:256 * b + 256], scratch["patches"][b // 2][:, :, 256 * (b % 2):256 * (b % 2) + 256]
                             ).then_inc(xt_in[b], 16)
            sp.dma_start(average[:], const["average_groups"]).then_inc(average_in, 16)
            sp.wait_ge(border, 2)
            for b in range(B):
                sp.wait_ge(normed, b + 1)
                for dy in range(3):
                    for side in range(2):
                        rows = padded[16 * 7:128] if side == 0 else padded[0:16]
                        sp.dma_start(edge[32 * dy + 16 * side:32 * dy + 16 * side + 16, b],
                                     rows[:, b, 2 * side:2 * side + 16, dy:dy + L]).then_inc(edge_in[b], 16)

        @block.gpsimd
        def _(pool):
            pool.memset(band[:], 0.0)
            pool.memset(cross[:], 0.0).then_inc(zeroed, 1)
            pool.memset(padded[:, :, 0:18:17, :], 0.0).then_inc(border, 1)
            pool.wait_ge(border, 1)
            pool.memset(padded[:, :, :, 0:L + 2:L + 1], 0.0).then_inc(border, 1)

        @block.scalar
        def _(act):
            act.wait_ge(zeroed, 1)
            for s in range(8):
                for dx in range(3):
                    at = s + dx - 1
                    if 0 <= at < 8:
                        act.dma_start(band[C * at:C * at + C, :, C * s:C * s + C],
                                      io["filters3"][:, dx].rearrange("y i j -> i y j")).then_inc(w_in, 16)
            for dy in range(3):
                act.dma_start(cross[32 * dy:32 * dy + 16, 0:C], io["filters3"][dy, 0]).then_inc(w_in, 16)
                act.dma_start(cross[32 * dy + 16:32 * dy + 32, 7 * C:8 * C], io["filters3"][dy, 2]).then_inc(w_in, 16)
            act.dma_start(ident[:], const["ident"]).then_inc(ident_in, 16)
            for s in range(8):
                act.dma_start(bias[C * s:C * s + C, :], io["bias3"].rearrange("(c o) -> c o", o=1)).then_inc(bias_in, 16)
            act.wait_ge(step, 6)
            nc.scalar.activation(std[:], var[:], ACT.Sqrt, bias=eps[:, 0:1]).then_inc(std_ready, 1)
            for t in range(16):
                b, w4 = t // 4, t % 4
                act.wait_ge(turned, t + 1)
                nc.scalar.activation(image[:, b, 32 * w4:32 * w4 + 32, :].rearrange("h w c -> h (w c)"),
                                     turn[t % 3][:].rearrange("h a n -> h (a n)"), ACT.Copy).then_inc(moved, 1)

        @block.tensor
        def _(pe):
            pe.wait_ge(average_in, 16)
            pe.wait_ge(stats_ready, 8 * B)
            nc.tensor.matmul(tot[:], average[:], sample[:, :, :, 1], start=True, stop=True).then_inc(sum_ready, 1)
            pe.wait_ge(step, 5)
            nc.tensor.matmul(tot[:], average[:], spread[:], start=True, stop=True).then_inc(sum_ready, 1)
            pe.wait_ge(border, 2)
            pe.wait_ge(w_in, 16 * 28)
            pe.wait_ge(ident_in, 16)

            def turn_tile(t):
                pe.wait_ge(res_ready, t + 1)
                if t >= 3:
                    pe.wait_ge(moved, t - 2)
                for k in range(4):
                    mm = nc.tensor.transpose(turn[t % 3][:, k], res[:, t % 3, k], ident[:])
                mm.then_inc(turned, 1)

            for t in range(16):
                b, w4 = t // 4, t % 4
                if t >= 3:
                    pe.wait_ge(res_ready, t - 2)
                pe.wait_ge(normed, b + 1)
                for dy in range(3):
                    nc.tensor.matmul(acc[t % 3][:], band[:, dy], padded[:, b, 4 * w4 + 1:4 * w4 + 5, dy:dy + L],
                                     start=dy == 0, stop=False)
                if w4 == 0:
                    pe.wait_ge(edge_in[b], 16 * 6)
                nc.tensor.matmul(acc[t % 3][:], cross[:], edge[:, b, 4 * w4:4 * w4 + 4], start=False, stop=True).then_inc(acc_done, 1)
                if t >= 1:
                    turn_tile(t - 1)
            turn_tile(15)

        @block.vector
        def _(dve):
            dve.memset(eps[:], 1e-5).then_inc(step, 1)
            for b in range(B):
                dve.wait_ge(xt_in[b], 16)
                for r in range(8):
                    nc.vector.bn_stats(stats[:, b, r], xt[:, r, 256 * b:256 * b + 256]).then_inc(stats_ready, 1)
            dve.wait_ge(sum_ready, 1)
            nc.vector.tensor_reduce(mean[:], tot[:], AX.X, ALU.add).then_inc(step, 1)
            dve.wait_ge(step, 2)
            nc.vector.tensor_tensor(dev[:], sample[:, :, :, 1], mean[:].unsqueeze(2).broadcast_to([128, B, 16]),
                                    ALU.subtract).then_inc(step, 1)
            dve.wait_ge(step, 3)
            nc.vector.tensor_tensor(dev[:], dev[:], dev[:], ALU.mult).then_inc(step, 1)
            dve.wait_ge(step, 4)
            nc.vector.scalar_tensor_tensor(out=spread[:], in0=sample[:, :, :, 2], scalar=1.0 / 128, in1=dev[:],
                                           op0=ALU.mult, op1=ALU.add).then_inc(step, 1)
            dve.wait_ge(sum_ready, 2)
            nc.vector.tensor_reduce(var[:], tot[:], AX.X, ALU.add).then_inc(step, 1)
            dve.wait_ge(std_ready, 1)
            nc.vector.reciprocal(rstd[:], std[:]).then_inc(step, 1)
            dve.wait_ge(step, 7)
            for b in range(B):
                nc.vector.tensor_scalar(padded[:, b, 1:17, 1:L + 1].rearrange("p w (h r) -> p r w h", r=8),
                                        xt[:, :, 256 * b:256 * b + 256].rearrange("p r (w h) -> p r w h", h=16),
                                        mean[:, b:b + 1], rstd[:, b:b + 1], ALU.subtract, ALU.mult).then_inc(normed, 1)
            dve.wait_ge(bias_in, 16 * 8)
            for t in range(16):
                dve.wait_ge(acc_done, t + 1)
                if t >= 3:
                    dve.wait_ge(turned, t - 2)
                nc.vector.scalar_tensor_tensor(
                    out=res[:, t % 3].rearrange("p w (h r) -> p (w h) r", r=8), in0=acc[t % 3][:].rearrange("p w (h r) -> p (w h) r", r=8),
                    scalar=bias[:, 0:1], in1=xt[:, :, 64 * t:64 * t + 64].rearrange("p r n -> p n r"),
                    op0=ALU.add, op1=ALU.add).then_inc(res_ready, 1)


def build(nc, io, const, out):
    scratch = {
        "filters": nc.dram_tensor("filters_dram", (8, 2, 128, GROUPS, 256), F32, kind="Internal").ap(),
        "spectrum": nc.dram_tensor("spectrum_dram", (C, L, 2, B * ROW), F32, kind="Internal").ap(),
        "products": nc.dram_tensor("products_dram", (L, C, 2, 2 * B * L), F32, kind="Internal").ap(),
        "patches": nc.dram_tensor("patches_dram", (2, 128, 8, N), F32, kind="Internal").ap(),
    }
    build_filters(nc, io, scratch, const)
    with nc.sbuf_tensor("mean1", [128, B], F32) as mean, nc.sbuf_tensor("rstd1", [128, B], F32) as rstd:
        with nc.sbuf_tensor("raw_weights", [128, 2, 8, 512], F32) as raw:
            with nc.sbuf_tensor("image0", [128, B, L, C], F32) as image:
                spectrum(nc, image, io["x"], scratch, const, "s0_")
                convolve(nc, 0, scratch, "c0_")
                back_to_image(nc, image, None, scratch, const, "b0_")
                to_patches(nc, io, image, mean, rstd, raw, scratch, const, "tp_")
            for half in range(2):
                patch_mixer(nc, io, half, mean, rstd, raw, scratch, const)
    with nc.sbuf_tensor("image1", [128, B, L, C], F32) as image:
        local_conv(nc, io, image, scratch, const, "l_")
        spectrum(nc, image, None, scratch, const, "s3_")
        convolve(nc, 1, scratch, "c3_")
        back_to_image(nc, image, out, scratch, const, "b3_")


def patch_mixer(nc, io, half, mean, rstd, raw, scratch, const):
    with nc.sbuf_tensor(f"xn{half}", [128, 2, 8, N], R32) as x, nc.sbuf_tensor(f"store{half}", [128, 4, 8, N], F32) as store:
        with nc.sbuf_tensor(f"sums{half}", [128, 4, N], F32) as sums:
            patch_correlate(nc, io, half, x, mean, rstd, raw, store, sums, scratch, const, f"q{half}_")
            with nc.sbuf_tensor(f"rstds{half}", [128, 4, N], F32) as rstds:
                patch_norm(nc, io, store, sums, rstds, raw, const, f"ln{half}_")
                patch_values(nc, io, x, store, rstds, raw, const, f"v{half}_")
        patch_project(nc, io, half, store, raw, scratch, const, f"o{half}_")


INPUTS = {
    "x": "x", "L0_conv_h0": "h00", "L0_conv_numerators": "num0", "L0_conv_denumerator": "den0",
    "L1_conv_Wq": "Wq", "L1_conv_bq": "bq", "L1_conv_Wk": "Wk", "L1_conv_bk": "bk", "L1_conv_Wv": "Wv", "L1_conv_bv": "bv",
    "L1_conv_ln_scale": "ln_scale", "L1_conv_ln_bias": "ln_bias", "L1_conv_Wout": "Wout", "L1_conv_bout": "bout",
    "L2_conv_filters": "filters3", "L2_conv_bias": "bias3",
    "L3_conv_h0": "h01", "L3_conv_numerators": "num1", "L3_conv_denumerator": "den1",
}


def kernel(**inputs):
    import numpy as _np
    import concourse.bacc as _bacc
    from concourse import mybir as _mybir
    from concourse.bass_utils import run_bass_kernel_spmd as _run

    nc = _bacc.Bacc("TRN2", target_bir_lowering=False, num_devices=1)
    arrays, io, const = {}, {}, {}
    for name, short in INPUTS.items():
        a = _np.ascontiguousarray(inputs[name])
        arrays[f"in_{name}"] = a
        io[short] = nc.dram_tensor(f"in_{name}", a.shape, _mybir.dt.from_np(a.dtype), kind="ExternalInput").ap()
    for layer in range(2):
        io[f"num{layer}"] = io[f"num{layer}"][0]
    for name, table in {**dft_tables(), **patch_tables()}.items():
        a = _np.ascontiguousarray(table.astype(_np.float32))
        arrays[f"const_{name}"] = a
        const[name] = nc.dram_tensor(f"const_{name}", a.shape, _mybir.dt.float32, kind="ExternalInput").ap()
    out = nc.dram_tensor("out_dram", (4, 128, 128, 16), _mybir.dt.float32, kind="ExternalOutput").ap()
    build(nc, io, const, out)
    r = _run(nc, [arrays], core_ids=[0])
    return r.results[0]["out_dram"]
```
